# Optimizing a Trainium2 kernel written in Bass

```python
import numpy as np
import jax
import jax.numpy as jnp

def _softmax(x, axis=-1):
    return jax.nn.softmax(x, axis=axis)

def _gelu(x):
    return jax.nn.gelu(x, approximate=True)

def _silu(x):
    return jax.nn.silu(x)

def _sigmoid(x):
    return jax.nn.sigmoid(x)

def _layernorm(x, axis=-1, eps=1e-05):
    m = jnp.mean(x, axis=axis, keepdims=True)
    v = jnp.var(x, axis=axis, keepdims=True)
    return (x - m) / jnp.sqrt(v + eps)

def _scatter_add(tgt, idx, src, axis=0):
    return tgt.at[idx].add(src)

def _segment_sum(src, seg, n):
    return jax.ops.segment_sum(src, seg, n)
kernel_name = 'mk_gnn_resnorm_d4_gnn_r8_f6170e'

def setup_inputs(seed: int=0):
    np.random.seed(seed)
    _w = jnp.asarray

    def _rec_inputs():
        import jax
        import jax.numpy as jnp
        _gk = jax.random.key(seed)
        x = -0.000202 + 1 * jax.random.normal(jax.random.fold_in(_gk, 1), (12500, 64), jnp.float32)
        _s = jax.random.randint(jax.random.fold_in(_gk, 2), (100000,), 0, 12500, jnp.int32)
        _d = jax.random.randint(jax.random.fold_in(_gk, 3), (100000,), 0, 12500, jnp.int32)
        _loop = jnp.arange(12500, dtype=jnp.int32)
        src = jnp.concatenate([_s, _d, _loop])
        dst = jnp.concatenate([_d, _s, _loop])
        _o = jnp.argsort(dst, stable=True)
        src = src[_o]
        dst = dst[_o]
        edge_attr_32 = 0.000196303 + 1.00016 * jax.random.normal(jax.random.fold_in(_gk, 11), (212500, 32), jnp.float32)
        return (x, src, dst, edge_attr_32)
    x, src, dst, edge_attr_32 = _rec_inputs()

    def _L0_gnn_setup():
        import jax, jax.numpy as jnp
        import numpy as np
        N = 12500
        E = 200000
        DIM = 64
        HEADS = 4
        CH = DIM // HEADS
        NEG_SLOPE = 0.2
        LN_EPS = 1e-05
        key = jax.random.key(seed)
        ks = jax.random.split(key, 6)
        x = jax.random.normal(ks[0], (N, DIM), dtype=jnp.float32)
        edge_index = jax.random.randint(ks[1], (2, E), 0, N, dtype=jnp.int64)
        scale = 1.0 / np.sqrt(DIM)
        W = jax.random.normal(ks[2], (DIM, HEADS * CH), dtype=jnp.float32) * scale
        att_src = jax.random.normal(ks[3], (HEADS, CH), dtype=jnp.float32) * scale
        att_dst = jax.random.normal(ks[4], (HEADS, CH), dtype=jnp.float32) * scale
        bias = jnp.zeros((HEADS * CH,), dtype=jnp.float32)
        gamma = jnp.ones((DIM,), dtype=jnp.float32)
        beta = jnp.zeros((DIM,), dtype=jnp.float32)
        return dict(x=x, edge_index=edge_index, W=W, att_src=att_src, att_dst=att_dst, bias=bias, gamma=gamma, beta=beta)
    _L0_gnn_all = _L0_gnn_setup()
    _L0_gnn_in = {k: v for k, v in _L0_gnn_all.items() if k in ('W', 'att_src', 'att_dst', 'bias', 'gamma', 'beta')}
    del _L0_gnn_all

    def _L1_gnn_setup():
        import jax, jax.numpy as jnp
        import numpy as np
        N_NODES = 12500

        def _gcn_norm(edge_index, num_nodes):
            loop = jnp.arange(num_nodes, dtype=edge_index.dtype)
            src = jnp.concatenate([edge_index[0], loop])
            dst = jnp.concatenate([edge_index[1], loop])
            deg = jax.ops.segment_sum(jnp.ones_like(src, dtype=jnp.float32), dst, num_segments=num_nodes)
            dinv = jnp.where(deg > 0, jax.lax.rsqrt(deg), 0.0)
            norm = dinv[src] * dinv[dst]
            return (src, dst, norm)
        key = jax.random.key(seed)
        ks = jax.random.split(key, 7)
        d = 64
        E = 125000
        x = jax.random.normal(ks[0], (N_NODES, d), dtype=jnp.float32)
        edge_index = jax.random.randint(ks[1], (2, E), 0, N_NODES, dtype=jnp.int64)
        s = 1.0 / np.sqrt(d)
        Ws = jax.random.normal(ks[2], (3, d, d), dtype=jnp.float32) * s
        bs = jax.random.normal(ks[3], (3, d), dtype=jnp.float32) * 0.02
        W_out = jax.random.normal(ks[4], (d, d), dtype=jnp.float32) * s
        b_out = jax.random.normal(ks[5], (d,), dtype=jnp.float32) * 0.02
        return {'x': x, 'edge_index': edge_index, 'Ws': Ws, 'bs': bs, 'W_out': W_out, 'b_out': b_out}
    _L1_gnn_all = _L1_gnn_setup()
    _L1_gnn_in = {k: v for k, v in _L1_gnn_all.items() if k in ('Ws', 'bs', 'W_out', 'b_out')}
    del _L1_gnn_all

    def _L2_gnn_setup():
        import jax, jax.numpy as jnp
        import numpy as np
        N, D, E, ED, L = (12500, 64, 100000, 32, 5)
        LN_EPS = 1e-05

        def _leaky(x):
            return jax.nn.leaky_relu(x, negative_slope=0.1)
        key = jax.random.key(seed)
        ks = jax.random.split(key, 16)
        s = 0.05
        return {'x': jax.random.normal(ks[0], (N, D), dtype=jnp.float32), 'edge_index': jax.random.randint(ks[1], (2, E), 0, N, dtype=jnp.int64), 'edge_attr': jax.random.normal(ks[2], (E, ED), dtype=jnp.float32), 'W1': jax.random.normal(ks[3], (L, D, 2 * D), dtype=jnp.float32) * s, 'b1': jnp.zeros((L, 2 * D), dtype=jnp.float32), 'W2': jax.random.normal(ks[4], (L, 2 * D, D), dtype=jnp.float32) * s, 'b2': jnp.zeros((L, D), dtype=jnp.float32), 'We1': jax.random.normal(ks[5], (L, ED, D), dtype=jnp.float32) * s, 'be1': jnp.zeros((L, D), dtype=jnp.float32), 'We2': jax.random.normal(ks[6], (L, D, D), dtype=jnp.float32) * s, 'be2': jnp.zeros((L, D), dtype=jnp.float32), 'res_w': jnp.ones((L,), dtype=jnp.float32), 'dot_scale': jnp.ones((L,), dtype=jnp.float32), 'ln_g': jnp.ones((L, D), dtype=jnp.float32), 'ln_b': jnp.zeros((L, D), dtype=jnp.float32)}
    _L2_gnn_all = _L2_gnn_setup()
    _L2_gnn_in = {k: v for k, v in _L2_gnn_all.items() if k in ('W1', 'b1', 'W2', 'b2', 'We1', 'be1', 'We2', 'be2', 'res_w', 'dot_scale', 'ln_g', 'ln_b')}
    del _L2_gnn_all

    def _L3_gnn_setup():
        import jax, jax.numpy as jnp
        import numpy as np
        N_NODES = 12500
        N_EDGES = 150000
        D_IN = 64
        D_OUT = 64
        BN_EPS = 1e-05
        key = jax.random.key(seed)
        k1, k2, k3, k4 = jax.random.split(key, 4)
        x = jax.random.normal(k1, (N_NODES, D_IN), dtype=jnp.float32)
        edge_index = jax.random.randint(k2, (2, N_EDGES), 0, N_NODES, dtype=jnp.int64)
        W = jax.random.normal(k3, (D_IN, D_OUT), dtype=jnp.float32) / np.sqrt(D_IN)
        gamma = jnp.ones((D_OUT,), dtype=jnp.float32)
        beta = jnp.zeros((D_OUT,), dtype=jnp.float32)
        return {'x': x, 'edge_index': edge_index, 'W': W, 'gamma': gamma, 'beta': beta}
    _L3_gnn_all = _L3_gnn_setup()
    _L3_gnn_in = {k: v for k, v in _L3_gnn_all.items() if k in ('W', 'gamma', 'beta')}
    del _L3_gnn_all
    return {'x': x, 'src': src, 'dst': dst, 'edge_attr_32': edge_attr_32, 'L0_gnn_W': _L0_gnn_in['W'], 'L0_gnn_att_src': _L0_gnn_in['att_src'], 'L0_gnn_att_dst': _L0_gnn_in['att_dst'], 'L0_gnn_bias': _L0_gnn_in['bias'], 'L0_gnn_gamma': _L0_gnn_in['gamma'], 'L0_gnn_beta': _L0_gnn_in['beta'], 'L1_gnn_Ws': _L1_gnn_in['Ws'], 'L1_gnn_bs': _L1_gnn_in['bs'], 'L1_gnn_W_out': _L1_gnn_in['W_out'], 'L1_gnn_b_out': _L1_gnn_in['b_out'], 'L2_gnn_W1': _L2_gnn_in['W1'], 'L2_gnn_b1': _L2_gnn_in['b1'], 'L2_gnn_W2': _L2_gnn_in['W2'], 'L2_gnn_b2': _L2_gnn_in['b2'], 'L2_gnn_We1': _L2_gnn_in['We1'], 'L2_gnn_be1': _L2_gnn_in['be1'], 'L2_gnn_We2': _L2_gnn_in['We2'], 'L2_gnn_be2': _L2_gnn_in['be2'], 'L2_gnn_res_w': _L2_gnn_in['res_w'], 'L2_gnn_dot_scale': _L2_gnn_in['dot_scale'], 'L2_gnn_ln_g': _L2_gnn_in['ln_g'], 'L2_gnn_ln_b': _L2_gnn_in['ln_b'], 'L3_gnn_W': _L3_gnn_in['W'], 'L3_gnn_gamma': _L3_gnn_in['gamma'], 'L3_gnn_beta': _L3_gnn_in['beta']}

def reference(x, src, dst, edge_attr_32, L0_gnn_W, L0_gnn_att_src, L0_gnn_att_dst, L0_gnn_bias, L0_gnn_gamma, L0_gnn_beta, L1_gnn_Ws, L1_gnn_bs, L1_gnn_W_out, L1_gnn_b_out, L2_gnn_W1, L2_gnn_b1, L2_gnn_W2, L2_gnn_b2, L2_gnn_We1, L2_gnn_be1, L2_gnn_We2, L2_gnn_be2, L2_gnn_res_w, L2_gnn_dot_scale, L2_gnn_ln_g, L2_gnn_ln_b, L3_gnn_W, L3_gnn_gamma, L3_gnn_beta):
    import jax
    import jax.numpy as jnp

    def _L0_gnn_ref(x, edge_index, W, att_src, att_dst, bias, gamma, beta):
        import jax, jax.numpy as jnp
        import numpy as np
        N = 12500
        E = 200000
        DIM = 64
        HEADS = 4
        CH = DIM // HEADS
        NEG_SLOPE = 0.2
        LN_EPS = 1e-05
        n = x.shape[0]
        loops = jnp.arange(n, dtype=edge_index.dtype)
        src = jnp.concatenate([edge_index[0], loops])
        dst = jnp.concatenate([edge_index[1], loops])
        h = (x @ W).reshape(n, HEADS, CH)
        a_src = jnp.einsum('nhc,hc->nh', h, att_src)
        a_dst = jnp.einsum('nhc,hc->nh', h, att_dst)
        e = a_src[src] + a_dst[dst]
        e = jax.nn.leaky_relu(e, NEG_SLOPE)
        m = jax.ops.segment_max(e, dst, num_segments=n)
        e = jnp.exp(e - m[dst])
        s = jax.ops.segment_sum(e, dst, num_segments=n)
        alpha = e / (s[dst] + 1e-16)
        msg = h[src] * alpha[:, :, None]
        out = jax.ops.segment_sum(msg, dst, num_segments=n)
        out = out.reshape(n, HEADS * CH) + bias
        y = x + out
        mu = jnp.mean(y, axis=-1, keepdims=True)
        var = jnp.var(y, axis=-1, keepdims=True)
        return (y - mu) / jnp.sqrt(var + LN_EPS) * gamma + beta

    def _L1_gnn_ref(x, edge_index, Ws, bs, W_out, b_out):
        import jax, jax.numpy as jnp
        import numpy as np
        N_NODES = 12500

        def _gcn_norm(edge_index, num_nodes):
            loop = jnp.arange(num_nodes, dtype=edge_index.dtype)
            src = jnp.concatenate([edge_index[0], loop])
            dst = jnp.concatenate([edge_index[1], loop])
            deg = jax.ops.segment_sum(jnp.ones_like(src, dtype=jnp.float32), dst, num_segments=num_nodes)
            dinv = jnp.where(deg > 0, jax.lax.rsqrt(deg), 0.0)
            norm = dinv[src] * dinv[dst]
            return (src, dst, norm)
        num_nodes = x.shape[0]
        src, dst, norm = _gcn_norm(edge_index, num_nodes)
        for i in range(Ws.shape[0]):
            h = x @ Ws[i]
            msg = norm[:, None] * h[src]
            x = jax.ops.segment_sum(msg, dst, num_segments=num_nodes) + bs[i]
            x = jax.nn.relu(x)
        return x @ W_out + b_out

    def _L2_gnn_ref(x, edge_index, edge_attr, W1, b1, W2, b2, We1, be1, We2, be2, res_w, dot_scale, ln_g, ln_b):
        import jax, jax.numpy as jnp
        import numpy as np
        N, D, E, ED, L = (12500, 64, 100000, 32, 5)
        LN_EPS = 1e-05

        def _leaky(x):
            return jax.nn.leaky_relu(x, negative_slope=0.1)
        src, dst = (edge_index[0], edge_index[1])
        n = x.shape[0]
        for l in range(W1.shape[0]):
            h = _leaky(x @ W1[l] + b1[l]) @ W2[l] + b2[l]
            e = _leaky(edge_attr @ We1[l] + be1[l]) @ We2[l] + be2[l]
            msg = h[src] * e * dot_scale[l]
            agg = jax.ops.segment_sum(msg, dst, num_segments=n)
            out = x + agg * res_w[l]
            mu = jnp.mean(out, axis=-1, keepdims=True)
            var = jnp.mean(jnp.square(out - mu), axis=-1, keepdims=True)
            x = (out - mu) * jax.lax.rsqrt(var + LN_EPS) * ln_g[l] + ln_b[l]
        return x

    def _L3_gnn_ref(x, edge_index, W, gamma, beta):
        import jax, jax.numpy as jnp
        import numpy as np
        N_NODES = 12500
        N_EDGES = 150000
        D_IN = 64
        D_OUT = 64
        BN_EPS = 1e-05
        src, dst = (edge_index[0], edge_index[1])
        n = x.shape[0]
        agg = jax.ops.segment_sum(x[src], dst, num_segments=n)
        cnt = jax.ops.segment_sum(jnp.ones((src.shape[0],), x.dtype), dst, num_segments=n)
        mean_agg = agg / jnp.maximum(cnt, 1.0)[:, None]
        h = jax.nn.elu(mean_agg @ W)
        mu = jnp.mean(h, axis=0)
        var = jnp.var(h, axis=0)
        out = (h - mu) * jax.lax.rsqrt(var + BN_EPS) * gamma + beta
        return out
    edge_index = jnp.stack([src, dst])
    x = _layernorm(x + _L0_gnn_ref(x, edge_index, L0_gnn_W, L0_gnn_att_src, L0_gnn_att_dst, L0_gnn_bias, L0_gnn_gamma, L0_gnn_beta), axis=-1)
    x = _layernorm(x + _L1_gnn_ref(x, edge_index, L1_gnn_Ws, L1_gnn_bs, L1_gnn_W_out, L1_gnn_b_out), axis=-1)
    x = _layernorm(x + _L2_gnn_ref(x, edge_index, edge_attr_32, L2_gnn_W1, L2_gnn_b1, L2_gnn_W2, L2_gnn_b2, L2_gnn_We1, L2_gnn_be1, L2_gnn_We2, L2_gnn_be2, L2_gnn_res_w, L2_gnn_dot_scale, L2_gnn_ln_g, L2_gnn_ln_b), axis=-1)
    x = _layernorm(x + _L3_gnn_ref(x, edge_index, L3_gnn_W, L3_gnn_gamma, L3_gnn_beta), axis=-1)
    return x

_drawn_inputs = setup_inputs


def setup_inputs(seed=0):
    import zlib

    import numpy as np

    out = dict(_drawn_inputs(seed))
    spreads = {'L0_gnn_bias': (0.0, 0.1),
     'L0_gnn_gamma': (1.0, 0.2),
     'L0_gnn_beta': (0.0, 0.1),
     'L2_gnn_b1': (0.0, 0.1),
     'L2_gnn_b2': (0.0, 0.1),
     'L2_gnn_be1': (0.0, 0.1),
     'L2_gnn_be2': (0.0, 0.1),
     'L2_gnn_res_w': (1.0, 0.2),
     'L2_gnn_dot_scale': (1.0, 0.2),
     'L2_gnn_ln_g': (1.0, 0.2),
     'L2_gnn_ln_b': (0.0, 0.1),
     'L3_gnn_gamma': (1.0, 0.2),
     'L3_gnn_beta': (0.0, 0.1)}
    factors = {'L1_gnn_bs': 7.248, 'L1_gnn_b_out': 3.575}
    for name, (base, spread) in spreads.items():
        noise = np.random.default_rng([zlib.crc32(name.encode()), seed]).standard_normal(out[name].shape)
        drawn = base * np.exp(spread * noise) if base else spread * noise
        out[name] = jnp.asarray(drawn.astype(out[name].dtype))
    for name, factor in factors.items():
        out[name] = (out[name] * factor).astype(out[name].dtype)
    return out
```

```python
import concourse.bass as bass
from concourse import mybir
from contextlib import ExitStack

F32 = mybir.dt.float32
BF16 = mybir.dt.bfloat16
I32 = mybir.dt.int32
ALU = mybir.AluOpType
ACT = mybir.ActivationFunctionType
AX = mybir.AxisListType

P = 128
G = 8
U = 4
C = 4
FAR = 2.0 ** 100


class Layout:

    def __init__(self, nodes, edges, dim, heads, edge_dim):
        self.nodes, self.edges, self.dim, self.heads, self.edge_dim = nodes, edges, dim, heads, edge_dim
        self.groups = -(-edges // (P * G * U)) * U
        self.tiles = self.groups * G
        self.blocks_used = -(-nodes // P)
        self.blocks = -(-(self.blocks_used + 1) // (2 * C)) * 2 * C
        self.chunks = self.blocks // C
        self.group_rows = -(-self.groups // P)
        while self.groups % self.group_rows:
            self.group_rows += 1


class Params:

    def __init__(self, *columns):
        self.at, self.width = {}, 0
        for name, width in columns:
            self.at[name] = (self.width, self.width + width)
            self.width += width

    def __call__(self, tensor, name):
        a, b = self.at[name]
        return tensor[:, a:b]


def param_columns(dim):
    return {
        "l0": Params(("W", 2 * dim), ("att_src", dim), ("att_dst", dim), ("bias", dim), ("gamma", dim),
                     ("beta", dim)),
        "l1": Params(("W", 2 * dim), ("b", dim)),
        "l2": Params(("W1", 4 * dim), ("b1", 1), ("W2", dim), ("b2", dim), ("We1", 8 * dim),
                     ("be1", 1), ("We2", dim), ("be2", dim), ("res_w", 1), ("dot_scale", 1),
                     ("ln_g", dim), ("ln_b", dim)),
        "l3": Params(("W", 2 * dim), ("gamma", dim), ("beta", dim)),
    }


class Steps:

    def __init__(self, semaphore):
        self.semaphore, self.count = semaphore, 0

    def add(self, instruction):
        instruction.then_inc(self.semaphore, 1)
        self.count += 1


def build(nc, L, src_idx, dst_idx, dst_tiles, dst_groups, x_in, attr, l0_params, l1_params, l2_params,
          l3_params, l1_layers, l2_layers, out):
    D, H, DH = L.dim, L.heads, L.dim // L.heads
    B, NG, NT = L.blocks, L.groups, L.tiles
    ITER = NG // U
    COLS = param_columns(D)
    ROW0 = D + H
    ACCW = D + H + 1
    ctx = ExitStack()
    with ctx:
        def sb(name, shape, dt):
            return ctx.enter_context(nc.sbuf_tensor(name, shape, dt))

        def ps(name, shape, dt):
            return ctx.enter_context(nc.psum_tensor(name, shape, dt))

        semaphores = []

        def sem(name):
            s = ctx.enter_context(nc.semaphore(name))
            semaphores.append(s)
            return s

        def scratch(name, shape, dt):
            return nc.dram_tensor(name, shape, dt, kind="Internal").ap()

        table0 = scratch("attention_table", (B * P, ROW0), F32)
        table_dst = scratch("attention_dst_table", (B * P, 2 * H), F32)
        table = scratch("feature_table", (B * P, D), F32)
        spill = scratch("gathered_rows", (NG, P, G * ROW0), F32)
        group_min = scratch("group_min", (NG, 1), I32)
        group_max = scratch("group_max", (NG, 1), I32)

        ident = sb("ident", [P, P], F32)
        iota1 = sb("iota1", [P, P], F32)
        iota_p = sb("iota_p", [P, 1], F32)
        ones = sb("ones", [P, P], F32)
        far_ident = sb("far_ident", [P, H, P], BF16)
        block_of = sb("block_of", [P, NT], F32)
        place_of = sb("place_of", [P, NT], F32)
        key = sb("key", [P, NT], F32)
        base_place = sb("base_place", [P, NG], F32)
        near_block = sb("near_block", [1, NG], F32)
        low = sb("low", [P, NG], F32)
        high = sb("high", [P, NG], F32)
        low_far = sb("low_far", [P, NG], F32)
        high_far = sb("high_far", [P, NG], F32)
        pass_block = sb("pass_block", [1, NG], I32)
        scattered = sb("scattered", [P, 1], F32)
        gathered_near = sb("gathered_near", [P, 1], F32)
        window = sb("window", [P, 1], F32)
        windows = sb("windows", [1, 1], I32)
        valid = sb("valid", [P, B], F32)
        count = sb("count", [P, B], F32)
        dinv = sb("dinv", [P, B], F32)
        stat = sb("stat", [P, 3, B], F32)
        x_outer = sb("x_outer", [P, B, D], F32)
        x_inner = sb("x_inner", [P, B, D], F32)
        acc = sb("acc", [P, B, ACCW], F32)
        stage = sb("stage", [P, B, ROW0], F32)
        tmp = sb("tmp", [P, B, D], F32)
        head_max = sb("head_max", [P, B, H], F32)
        dst_rows = sb("dst_rows", [P, B, 2 * H], F32)
        self_weight = sb("self_weight", [P, B, H], F32)

        idx_buf = sb("idx_buf", [P, U, G], I32)
        rows_buf = sb("rows_buf", [P, U, G, ROW0], F32)
        onehot = sb("onehot", [P, 2, G, P], F32)
        not_hot = onehot[:, 0, :, :].rearrange("p g e -> p (g e)").bitcast(BF16).rearrange("p (s g e) -> p s g e", s=2, g=G)
        attr_buf = sb("attr_buf", [P, U, G // 4, P], F32)
        hidden = sb("hidden", [P, 2, 4 * P], F32)
        message = sb("message", [P, 2, G, ACCW], F32)
        red = sb("red", [P, G, H], F32)
        red1 = sb("red1", [P, H], F32)
        dst_buf = sb("dst_buf", [P, U, G, 2 * H], F32)
        logit = sb("logit", [P, 3, G, H], F32)
        params = sb("params", [P, COLS["l2"].width], F32)
        params1 = params[:, 0:COLS["l1"].width]
        params0 = params[:, 0:COLS["l0"].width]
        params3 = params[:, 0:COLS["l3"].width]
        over_nodes = params[:, COLS["l3"].width:COLS["l3"].width + 4 * D].rearrange("p (n d) -> p n d", n=4)
        rows_flat = rows_buf[:, :, :, :].rearrange("p u g w -> p (u g w)")
        node_x = rows_flat[:, 0:2 * C * D].rearrange("p (s b d) -> p s b d", s=2, d=D)
        node_t = rows_flat[:, 2 * C * D:4 * C * D].rearrange("p (s j n) -> p s j n", s=2, n=P)

        dst_i = tmp[:, :, :].rearrange("p b d -> p (b d)")[:, 0:NT].bitcast(I32)
        dst_part = x_inner[:, :, :].rearrange("p b d -> p (b d)")[:, 0:NT].bitcast(I32)
        GR, GP = L.group_rows, NG // L.group_rows
        stage_flat = stage[:, :, :].rearrange("p b d -> p (b d)")
        acc_flat = acc[:, :, :].rearrange("p b d -> p (b d)")
        groups_i = stage_flat[0:GP, 0:GR * G * P].bitcast(I32).rearrange("p (r e) -> p r e", r=GR)
        groups_f = acc_flat[0:GP, 0:GR * G * P].rearrange("p (r e) -> p r e", r=GR)
        span = sb("span", [P, 4, max(GR, 2)], F32)
        span_i = sb("span_i", [P, 2, GR], I32)
        x_inner_flat = x_inner[:, :, :].rearrange("p b d -> p (b d)")
        base_i = x_inner_flat[:, NT:NT + 3 * NG].bitcast(I32).rearrange("p (n g) -> p n g", n=3)
        span_row = x_inner_flat[:, NT + 3 * NG:NT + 6 * NG].rearrange("p (n g) -> p n g", n=3)

        banks = ps("banks", [P, 8, 512], F32)
        bank = [banks[:, n, :] for n in range(8)]

        s_load = sem("s_load")
        s_load2 = sem("s_load2")
        s_store = sem("s_store")
        s_pool = sem("s_pool")
        s_dve = sem("s_dve")
        s_ready = sem("s_ready")
        s_var = sem("s_var")
        s_std = sem("s_std")
        s_pe = sem("s_pe")
        s_chunk_x = sem("s_chunk_x")
        s_chunk_t = sem("s_chunk_t")
        s_chunk_tc = sem("s_chunk_tc")
        s_chunk_m = sem("s_chunk_m")
        s_chunk_o = sem("s_chunk_o")
        s_chunk_h = sem("s_chunk_h")
        s_chunk_b = sem("s_chunk_b")
        s_chunk_l = sem("s_chunk_l")
        s_turn = sem("s_turn")
        s_idx = [sem(f"s_idx{u}") for u in range(U)]
        s_rows = [sem(f"s_rows{u}") for u in range(U)]
        s_attr = [sem(f"s_attr{u}") for u in range(U)]
        s_spill = [sem(f"s_spill{u}") for u in range(U)]
        s_hot = sem("s_hot")
        s_sum = sem("s_sum")
        s_acc = sem("s_acc")
        s_hid = sem("s_hid")
        s_act_hid = sem("s_act_hid")
        s_edge = sem("s_edge")
        s_msg = sem("s_msg")
        s_bc = sem("s_bc")
        s_red = sem("s_red")
        s_group = sem("s_group")
        s_logit = sem("s_logit")
        s_exp = sem("s_exp")
        numbers = [s.num for s in semaphores]
        assert numbers == list(range(numbers[0], numbers[0] + len(numbers)))

        def stage_end():
            used = range(numbers[0], numbers[-1] + 1)
            nc.gpsimd.dma_reset(used)
            nc.gpsimd.sem_clear(used)
            nc.all_engine_barrier()

        def whole(t, width=D):
            return t[:, :, 0:width]

        def over_blocks(vector, width=D, blocks=B):
            return vector.unsqueeze(1).broadcast_to([P, blocks, width])

        def over_row(per_node, width=D, blocks=B):
            return per_node.unsqueeze(2).broadcast_to([P, blocks, width])

        def rows_of(t):
            return t.rearrange("(b p) d -> p b d", p=P)

        with nc.Block() as block:
            @block.sync
            def _(sp):
                sp.dma_start(dst_i, dst_tiles).then_inc(s_load, 16)
                sp.dma_start(groups_i, dst_groups.rearrange("(p r) e -> p r e", r=GR)).then_inc(s_idx[0], 16)
                sp.dma_start(params0, l0_params).then_inc(s_idx[1], 16)
                sp.dma_start(x_outer[:, :, :], x_in.rearrange("(b p) d -> p b d", p=P)).then_inc(s_idx[1], 16)
                sp.wait_ge(s_hot, 1)
                sp.dma_start(group_min.rearrange("(p r) o -> p (r o)", r=GR), span_i[0:GP, 0, :]).then_inc(s_store, 16)
                sp.dma_start(group_max.rearrange("(p r) o -> p (r o)", r=GR), span_i[0:GP, 1, :]).then_inc(s_store, 16)
                sp.wait_ge(s_store, 32)
                for n, t in enumerate((group_min, group_max)):
                    sp.dma_start(base_i[:, n, :], t.rearrange("g o -> o g").broadcast_to([P, NG])).then_inc(s_attr[0], 16)
                sp.wait_ge(s_idx[1], 32)

            @block.gpsimd
            def _(pool):
                pool.iota(iota1[:, :], pattern=[[1, P]], base=1, channel_multiplier=0,
                          allow_small_or_imprecise_dtypes=True).then_inc(s_pool, 1)
                pool.iota(iota_p[:, :], pattern=[[0, 1]], base=0, channel_multiplier=1,
                          allow_small_or_imprecise_dtypes=True).then_inc(s_pool, 1)
                pool.memset(ident[:, :], 0.0).then_inc(s_pool, 1)
                pool.memset(ones[:, :], 1.0).then_inc(s_pool, 1)
                pool.memset(far_ident[:, :, :], 0.0).then_inc(s_pool, 1)
                pool.memset(valid[:, :], 1.0).then_inc(s_pool, 1)
                pool.wait_ge(s_pool, 6)
                pool.affine_select(out=ident[:, :], in_=ident[:, :], compare_op=ALU.not_equal, fill=1.0,
                                   base=0, pattern=[[-1, P]], channel_multiplier=1).then_inc(s_pool, 1)
                pool.affine_select(out=far_ident[:, :, :], in_=far_ident[:, :, :], compare_op=ALU.not_equal,
                                   fill=-FAR, base=0, pattern=[[0, H], [-1, P]],
                                   channel_multiplier=1).then_inc(s_pool, 1)
                pool.affine_select(out=valid[:, :], in_=valid[:, :], compare_op=ALU.is_ge, fill=0.0,
                                   base=L.nodes - 1, pattern=[[-P, B]], channel_multiplier=-1).then_inc(s_pool, 1)
                pool.wait_ge(s_dve, 4)
                pool.affine_select(out=place_of[:, :], in_=place_of[:, :], compare_op=ALU.is_ge, fill=0.0,
                                   base=L.edges - 1, pattern=[[-P, NT]], channel_multiplier=-1).then_inc(s_pool, 1)

            @block.vector
            def _(dve):
                d = Steps(s_dve)

                def then(instruction):
                    d.add(instruction)
                    dve.wait_ge(s_dve, d.count)

                dve.wait_ge(s_load, 16)
                then(dve.tensor_scalar(dst_part, dst_i, 127, None, ALU.bitwise_and))
                then(dve.tensor_scalar(place_of[:, :], dst_part, 1.0, None, ALU.add))
                then(dve.tensor_scalar(dst_part, dst_i, 7, None, ALU.logical_shift_right))
                then(dve.tensor_copy(block_of[:, :], dst_part))
                dve.wait_ge(s_idx[0], 16)
                then(dve.tensor_copy(groups_f, groups_i))
                then(dve.tensor_reduce(out=span[0:GP, 0, 0:GR], in_=groups_f, op=ALU.min, axis=AX.X))
                then(dve.tensor_reduce(out=span[0:GP, 1, 0:GR], in_=groups_f, op=ALU.max, axis=AX.X))
                then(dve.tensor_copy(span_i[0:GP, :, :], span[0:GP, 0:2, 0:GR]))
                dve.wait_ge(s_dve, d.count)
                dve.sem_inc(s_hot, 1)
                dve.wait_ge(s_attr[0], 32)
                then(dve.tensor_scalar(base_i[:, 2, :], base_i[:, 0, :], 127, None, ALU.bitwise_and))
                then(dve.tensor_copy(base_place[:, :], base_i[:, 2, :]))
                then(dve.tensor_scalar(base_i[:, 2, :], base_i[:, 0, :], 7, None, ALU.logical_shift_right))
                then(dve.tensor_copy(near_block[:, :], base_i[0:1, 2, :]))
                then(dve.tensor_copy(span_row[:, 0:2, :], base_i[:, 0:2, :]))
                then(dve.tensor_tensor(span_row[:, 2, :], span_row[:, 1, :], span_row[:, 0, :], ALU.subtract))
                then(dve.tensor_reduce(out=span[:, 2, 0:1], in_=span_row[:, 2, :], op=ALU.max, axis=AX.X))
                then(dve.tensor_scalar(scattered[:, :], span[:, 2, 0:1], float(P), None, ALU.is_ge))
                then(dve.tensor_scalar(gathered_near[:, :], scattered[:, :], -1.0, 1.0, ALU.mult, ALU.add))
                then(dve.tensor_scalar(span[:, 3, 0:1], scattered[:, :], float(L.blocks_used - 1), 1.0, ALU.mult, ALU.add))
                then(dve.tensor_copy(windows[:, :], span[0:1, 3, 0:1]))
                then(dve.tensor_scalar(near_block[:, :], near_block[:, :], gathered_near[0:1, :], None, ALU.mult))
                dve.wait_ge(s_pool, 2)
                then(dve.tensor_scalar(low[:, :], base_place[:, :], iota_p[:, :], scattered[:, :], ALU.is_le, ALU.max))
                then(dve.tensor_scalar(high[:, :], low[:, :], -1.0, 1.0, ALU.mult, ALU.add))
                then(dve.tensor_scalar(low_far[:, :], high[:, :], -FAR, None, ALU.mult))
                then(dve.tensor_scalar(high_far[:, :], low[:, :], -FAR, None, ALU.mult))
                dve.wait_ge(s_pool, 10)
        stage_end()
        pass_windows = nc.values_load(windows[0:1, 0:1], min_val=1, max_val=L.blocks_used,
                                      skip_runtime_bounds_check_because="it is 1 or the number of blocks")

        def each_group(engine, body):
            with engine.Fori(0, ITER - 1) as i:
                for u in range(U):
                    body(i * U + u, i, u, False)
            for u in range(U):
                body((ITER - 1) * U + u, ITER - 1, u, u == U - 1)

        def of_group(t, g):
            return t[bass.ds(g, 1), :, :].rearrange("o p e -> (o p) e")

        def index_loads(sp, indices, after_rows=None, beside=None):
            for u in range(U):
                sp.dma_start(idx_buf[:, u, :], of_group(indices, u)).then_inc(s_idx[u], 16)

            def body(g, i, u, last):
                if beside:
                    beside(g, i, u)
                sp.wait_ge(s_rows[u], (i + 1) * (16 * G))
                if after_rows:
                    after_rows(g, i, u)
                if not (isinstance(i, int) and i == ITER - 1):
                    sp.dma_start(idx_buf[:, u, :], of_group(indices, g + U)).then_inc(s_idx[u], 16)

            each_group(sp, body)

        def gather(pool, source, slot_rows, wait_free):
            with pool.Fori(0, ITER) as i:
                for u in range(U):
                    pool.wait_ge(s_idx[u], (i + 1) * 16)
                    wait_free(pool, i * U + u, i, u)
                    pool.sem_inc(s_turn, 1)
                    for t in range(G):
                        pool.indirect_dma_start(
                            out=slot_rows(u, t), out_offset=None, in_=source,
                            in_offset=bass.IndirectOffsetOnAxis(ap=idx_buf[:, u, t:t + 1], axis=0),
                        ).then_inc(s_rows[u], 16)

        def open_windows(dve):
            d = Steps(s_dve)
            d.add(dve.tensor_scalar(key[:, :], block_of[:, :], window[:, :], gathered_near[:, :], ALU.is_equal, ALU.max))
            d.add(dve.tensor_tensor(span[0:1, 0, 0:1], window[0:1, :], scattered[0:1, :], ALU.mult))
            dve.wait_ge(s_dve, d.count)
            d.add(dve.tensor_tensor(key[:, :], key[:, :], place_of[:, :], ALU.mult))
            d.add(dve.tensor_scalar(pass_block[0:1, :], near_block[0:1, :], span[0:1, 0, 0:1], None, ALU.add))
            d.add(dve.tensor_scalar(window[:, :], window[:, :], 1.0, None, ALU.add))
            dve.wait_ge(s_dve, d.count)

        def make_onehot(dve, g, to, op=ALU.is_equal):
            dve.tensor_tensor(
                to, iota1[:, :].unsqueeze(1).broadcast_to([P, G, P]),
                key[:, bass.ds(g * G, G)].unsqueeze(2).broadcast_to([P, G, P]), op).then_inc(s_hot, 1)

        def block_of_group(dve, g):
            return dve.value_load(pass_block[0:1, bass.ds(g, 1)], min_val=0, max_val=L.blocks_used - 1)

        def add_sums(dve, g, slot, width):
            b = block_of_group(dve, g)
            dve.wait_ge(s_sum, g + (U + 1))
            for n, side in enumerate((low, high)):
                dve.wait_ge(s_acc, g * 2 + (4 + n))
                to = acc[:, bass.ds(b + n, 1), 0:width].rearrange("p o w -> p (o w)")
                dve.scalar_tensor_tensor(
                    out=to, in0=bank[6 + slot][:, 0:width], scalar=side[:, bass.ds(g, 1)], in1=to,
                    op0=ALU.mult, op1=ALU.add).then_inc(s_acc, 1)

        def sum_group(pe, g, slot, rows, width):
            pe.wait_ge(s_hot, g + 1)
            pe.wait_ge(s_acc, g * 2 + 2)
            for t in range(G):
                ins = pe.matmul(bank[6 + slot][:, 0:width], onehot[:, slot, t, :], rows(t),
                                start=(t == 0), stop=(t == G - 1))
            ins.then_inc(s_sum, 1)

        def run_windows(emit):
            with nc.Fori(0, pass_windows):
                with nc.Block() as block:
                    emit(block)
                stage_end()

        def sum_pass(block):
            @block.sync
            def _(sp):
                index_loads(sp, src_idx)

            @block.gpsimd
            def _(pool):
                gather(pool, table, lambda u, t: rows_buf[:, u, t, 0:D],
                       lambda e, g, i, u: e.wait_ge(s_sum, g + 1))

            @block.vector
            def _(dve):
                dve.sem_inc(s_acc, 4)
                open_windows(dve)

                def body(g, i, u, last):
                    make_onehot(dve, g, onehot[:, u % 2, :, :])
                    add_sums(dve, g, u % 2, D)

                each_group(dve, body)
                dve.wait_ge(s_acc, 4 + 2 * NG)

            @block.tensor
            def _(pe):
                pe.sem_inc(s_sum, U)

                def body(g, i, u, last):
                    pe.wait_ge(s_rows[u], (i + 1) * (16 * G))
                    sum_group(pe, g, u % 2, lambda t: rows_buf[:, u, t, 0:D], D)

                each_group(pe, body)

        def edge_mlp_pass(block):
            w1, b1 = COLS["l2"](params, "We1"), COLS["l2"](params, "be1")
            w2, b2 = COLS["l2"](params, "We2"), COLS["l2"](params, "be2")

            @block.sync
            def _(sp):
                def attributes(g, i, u):
                    sp.wait_ge(s_hid, g * 2 + 2)
                    sp.dma_start(attr_buf[:, u, :, :].rearrange("p a e -> p (a e)"), of_group(attr, g)).then_inc(s_attr[u], 16)

                index_loads(sp, src_idx, beside=attributes)

            @block.gpsimd
            def _(pool):
                gather(pool, table, lambda u, t: rows_buf[:, u, t, 0:D],
                       lambda e, g, i, u: e.wait_ge(s_msg, g + 1))

            @block.scalar
            def _(act):
                act.sem_inc(s_act_hid, 2)

                def body(g, i, u, last):
                    for half in range(2):
                        act.wait_ge(s_hid, g * 2 + (2 * U + half + 1))
                        act.wait_ge(s_edge, g * 2 + (half + 1))
                        act.activation(hidden[:, half, :], bank[half], ACT.Relu, bias=b1).then_inc(s_act_hid, 1)

                each_group(act, body)

            @block.vector
            def _(dve):
                dve.sem_inc(s_acc, 4)
                dve.sem_inc(s_msg, U)
                open_windows(dve)

                def body(g, i, u, last):
                    slot = u % 2
                    make_onehot(dve, g, onehot[:, slot, :, :])
                    dve.wait_ge(s_rows[u], (i + 1) * (16 * G))
                    dve.wait_ge(s_edge, g * 2 + 4)
                    dve.tensor_tensor(
                        message[:, slot, :, 0:D], bank[4 + slot].rearrange("p (t d) -> p t d", d=D),
                        rows_buf[:, u, :, 0:D], ALU.mult).then_inc(s_msg, 1)
                    add_sums(dve, g, slot, D)

                each_group(dve, body)
                dve.wait_ge(s_acc, 4 + 2 * NG)

            @block.tensor
            def _(pe):
                pe.sem_inc(s_sum, U)
                pe.sem_inc(s_hid, 2 * U)
                pe.sem_inc(s_edge, 2)

                def edge_features(g, i, u):
                    slot = u % 2
                    pe.wait_ge(s_attr[u], (i + 1) * 16)
                    for half in range(2):
                        pe.wait_ge(s_act_hid, g * 2 + (half + 1))
                        for j in range(4):
                            ins = pe.matmul(bank[half][:, j * P:(j + 1) * P], w1[:, j * P:(j + 1) * P],
                                            attr_buf[:, u, half, :], start=True, stop=True)
                        ins.then_inc(s_hid, 1)
                    pe.wait_ge(s_msg, g + (U - 1))
                    for half in range(2):
                        pe.wait_ge(s_act_hid, g * 2 + (half + 3))
                        for j in range(4):
                            to = bank[4 + slot][:, (4 * half + j) * D:(4 * half + j + 1) * D]
                            pe.matmul(to, ones[0:1, :], b2[0:1, :], start=True, stop=False)
                            ins = pe.matmul(to, hidden[:, half, j * P:(j + 1) * P], w2, start=False, stop=True)
                        ins.then_inc(s_edge, 1)

                edge_features(0, 0, 0)

                def body(g, i, u, last):
                    if not last:
                        edge_features(g + 1, i + (u + 1) // U, (u + 1) % U)
                    pe.wait_ge(s_msg, g + (U + 1))
                    sum_group(pe, g, u % 2, lambda t: message[:, u % 2, t, 0:D], D)

                each_group(pe, body)

        def max_pass(block):
            @block.sync
            def _(sp):
                def keep(g, i, u):
                    sp.dma_start(of_group(spill, g), rows_buf[:, u, :, :].rearrange("p t w -> p (t w)")).then_inc(s_spill[u], 16)
                    sp.wait_ge(s_spill[u], (i + 1) * 16)

                index_loads(sp, src_idx, after_rows=keep)

            @block.gpsimd
            def _(pool):
                gather(pool, table0, lambda u, t: rows_buf[:, u, t, :],
                       lambda e, g, i, u: e.wait_ge(s_bc, g * 4 + 4))

            @block.vector
            def _(dve):
                dve.sem_inc(s_acc, 4)
                dve.sem_inc(s_red, 2)
                open_windows(dve)

                def body(g, i, u, last):
                    make_onehot(dve, g, not_hot[:, u % 2, :, :], ALU.not_equal)
                    for k in range(4):
                        dve.wait_ge(s_bc, g * 4 + (4 * U + k + 1))
                        dve.tensor_reduce(
                            out=red[:, 2 * k:2 * k + 2, :],
                            in_=banks[:, 2 * (k % 2):2 * (k % 2) + 2, :].rearrange("p b (h e) -> p b h e", h=H),
                            op=ALU.max, axis=AX.X).then_inc(s_red, 1)
                    dve.wait_ge(s_red, g * 4 + 6)
                    dve.wait_ge(s_acc, g * 2 + 4)
                    dve.tensor_reduce(out=red1[:, :], in_=red[:, :, :].rearrange("p g h -> p h g"),
                                      op=ALU.max, axis=AX.X).then_inc(s_group, 1)
                    b = block_of_group(dve, g)
                    dve.wait_ge(s_group, g + 1)
                    for n, side in enumerate((low_far, high_far)):
                        dve.wait_ge(s_acc, g * 2 + (4 + n))
                        to = head_max[:, bass.ds(b + n, 1), :].rearrange("p o w -> p (o w)")
                        dve.scalar_tensor_tensor(
                            out=to, in0=red1[:, :], scalar=side[:, bass.ds(g, 1)], in1=to,
                            op0=ALU.add, op1=ALU.max).then_inc(s_acc, 1)

                each_group(dve, body)
                dve.wait_ge(s_acc, 4 + 2 * NG)

            @block.tensor
            def _(pe):
                pe.sem_inc(s_bc, 4 * U)

                def body(g, i, u, last):
                    pe.wait_ge(s_rows[u], (i + 1) * (16 * G))
                    pe.wait_ge(s_hot, g + 1)
                    for k in range(4):
                        pe.wait_ge(s_red, g * 4 + (k + 1))
                        for t in (2 * k, 2 * k + 1):
                            to = bank[t % 4]
                            pe.matmul(to, not_hot[:, u % 2, t, :], far_ident[:, :, :].rearrange("p h e -> p (h e)"),
                                      start=True, stop=False)
                            for h in range(H):
                                ins = pe.matmul(to[:, h * P:(h + 1) * P],
                                                rows_buf[:, u, t, D + h:D + h + 1].broadcast_to([P, P]),
                                                ident[:, :], start=False, stop=(h == H - 1))
                        ins.then_inc(s_bc, 1)

                each_group(pe, body)

        def attention_pass(block):
            @block.sync
            def _(sp):
                def kept(g, i, u):
                    sp.wait_ge(s_msg, g + 1)
                    sp.dma_start(rows_buf[:, u, :, :].rearrange("p t w -> p (t w)"), of_group(spill, g)).then_inc(s_attr[u], 16)

                index_loads(sp, dst_idx, beside=kept)

            @block.gpsimd
            def _(pool):
                gather(pool, table_dst, lambda u, t: dst_buf[:, u, t, :],
                       lambda e, g, i, u: e.wait_ge(s_msg, g + 1))

            @block.scalar
            def _(act):
                def body(g, i, u, last):
                    act.wait_ge(s_logit, g * 3 + 3)
                    act.wait_ge(s_sum, g + (U - 1))
                    act.activation(message[:, u % 2, :, D:D + H], logit[:, 2, :, :], ACT.Exp).then_inc(s_exp, 1)

                each_group(act, body)

            @block.vector
            def _(dve):
                dve.sem_inc(s_acc, 4)
                dve.sem_inc(s_msg, U)
                open_windows(dve)

                def body(g, i, u, last):
                    slot = u % 2
                    make_onehot(dve, g, onehot[:, slot, :, :])
                    dve.wait_ge(s_attr[u], (i + 1) * 16)
                    dve.wait_ge(s_rows[u], (i + 1) * (16 * G))
                    dve.tensor_tensor(logit[:, 0, :, :], rows_buf[:, u, :, D:D + H], dst_buf[:, u, :, 0:H], ALU.add).then_inc(s_logit, 1)
                    dve.wait_ge(s_logit, g * 3 + 1)
                    dve.scalar_tensor_tensor(out=logit[:, 1, :, :], in0=logit[:, 0, :, :], scalar=0.2,
                                             in1=logit[:, 0, :, :], op0=ALU.mult, op1=ALU.max).then_inc(s_logit, 1)
                    dve.wait_ge(s_logit, g * 3 + 2)
                    dve.tensor_tensor(logit[:, 2, :, :], logit[:, 1, :, :], dst_buf[:, u, :, H:2 * H], ALU.subtract).then_inc(s_logit, 1)
                    dve.wait_ge(s_exp, g + 1)
                    dve.tensor_tensor(
                        message[:, slot, :, 0:D].rearrange("p t (h c) -> p t h c", h=H),
                        rows_buf[:, u, :, 0:D].rearrange("p t (h c) -> p t h c", h=H),
                        message[:, slot, :, D:D + H].unsqueeze(3).broadcast_to([P, G, H, DH]),
                        ALU.mult).then_inc(s_msg, 1)
                    add_sums(dve, g, slot, ACCW)

                each_group(dve, body)
                dve.wait_ge(s_acc, 4 + 2 * NG)

            @block.tensor
            def _(pe):
                pe.sem_inc(s_sum, U)

                def body(g, i, u, last):
                    pe.wait_ge(s_msg, g + (U + 1))
                    sum_group(pe, g, u % 2, lambda t: message[:, u % 2, t, :], ACCW)

                each_group(pe, body)

        def each_chunk_pair(engine, body):
            with engine.Fori(0, L.chunks // 2) as i:
                body(i)

        def bring_chunks(block, x):
            @block.gpsimd
            def _(pool):
                def body(i):
                    for slot in range(2):
                        c = i * 2 + slot
                        pool.wait_ge(s_chunk_t, c + 1)
                        pool.sem_inc(s_turn, 1)
                        pool.tensor_copy(node_x[:, slot, :, :], x[:, bass.ds(c * C, C), :]).then_inc(s_chunk_x, 1)

                each_chunk_pair(pool, body)

        def transpose_chunk(pe, c, slot):
            pe.wait_ge(s_chunk_x, c + 1)
            pe.wait_ge(s_chunk_tc, c + 1)
            for j in range(C // 2):
                ins = pe.transpose(bank[slot][:, j * P:(j + 1) * P],
                                   node_x[:, slot, 2 * j:2 * j + 2, :].rearrange("p b d -> p (b d)"), ident[:, :])
            ins.then_inc(s_chunk_t, 1)

        def copy_transposed(act, c, slot, s_used):
            act.wait_ge(s_chunk_t, c + 3)
            act.wait_ge(s_used, c + 1)
            act.activation(node_t[:, slot, :, :].rearrange("p j n -> p (j n)"), bank[slot][:, 0:C // 2 * P],
                           ACT.Copy).then_inc(s_chunk_tc, 1)

        def project(block, x, w):
            bring_chunks(block, x)

            @block.tensor
            def _(pe):
                pe.sem_inc(s_chunk_t, 2)
                pe.sem_inc(s_chunk_m, 2)
                pe.wait_ge(s_load, 16)

                def body(i):
                    for slot in range(2):
                        transpose_chunk(pe, i * 2 + slot, slot)
                    for slot in range(2):
                        c = i * 2 + slot
                        pe.wait_ge(s_chunk_tc, c + 3)
                        pe.wait_ge(s_chunk_o, c + 1)
                        for j in range(C // 2):
                            ins = pe.matmul(bank[4 + slot][:, j * 2 * D:(j + 1) * 2 * D], node_t[:, slot, j, :],
                                            w, start=True, stop=True)
                        ins.then_inc(s_chunk_m, 1)

                each_chunk_pair(pe, body)

        def project_copies(act):
            act.sem_inc(s_chunk_tc, 2)

            def body(i):
                for slot in range(2):
                    copy_transposed(act, i * 2 + slot, slot, s_chunk_m)

            each_chunk_pair(act, body)

        def take_products(dve, to, op):
            dve.sem_inc(s_chunk_o, 2)

            def body(i):
                for slot in range(2):
                    c = i * 2 + slot
                    dve.wait_ge(s_chunk_m, c + 3)
                    op(to[:, bass.ds(c * C, C), 0:D], bank[4 + slot][:, 0:C * D].rearrange("p (b d) -> p b d", d=D),
                       bass.ds(c * C, C)).then_inc(s_chunk_o, 1)

            each_chunk_pair(dve, body)
            dve.wait_ge(s_chunk_o, 2 + L.chunks)

        def layer_norm(dve, then, n, x, to, gamma=None, beta=None):
            then(dve.tensor_reduce(out=stat[:, 0, :], in_=x, op=ALU.add, axis=AX.X))
            then(dve.tensor_scalar(stat[:, 0, :], stat[:, 0, :], 1.0 / D, None, ALU.mult))
            then(dve.tensor_tensor(tmp[:, :, :], x, over_row(stat[:, 0, :]), ALU.subtract))
            then(dve.tensor_tensor(whole(stage), tmp[:, :, :], tmp[:, :, :], ALU.mult))
            then(dve.tensor_reduce(out=stat[:, 1, :], in_=whole(stage), op=ALU.add, axis=AX.X))
            dve.tensor_scalar(stat[:, 1, :], stat[:, 1, :], 1.0 / D, 1e-5, ALU.mult, ALU.add).then_inc(s_var, 1)
            dve.wait_ge(s_std, n + 1)
            then(dve.reciprocal(stat[:, 2, :], stat[:, 2, :]))
            then(dve.tensor_tensor(to, tmp[:, :, :], over_row(stat[:, 2, :]), ALU.mult))
            if gamma is not None:
                then(dve.tensor_tensor(to, to, over_blocks(gamma), ALU.mult))
                then(dve.tensor_tensor(to, to, over_blocks(beta), ALU.add))

        def layer_norm_root(act, n):
            act.wait_ge(s_var, n + 1)
            act.activation(stat[:, 2, :], stat[:, 1, :], ACT.Sqrt).then_inc(s_std, 1)

        def chain(dve):
            d = Steps(s_dve)

            def then(instruction):
                d.add(instruction)
                dve.wait_ge(s_dve, d.count)

            return then

        def store_table(sp, to, source):
            sp.wait_ge(s_ready, 1)
            sp.dma_start(rows_of(to), source).then_inc(s_store, 16)
            sp.wait_ge(s_store, 16)

        with nc.Block() as block:
            w0 = COLS["l0"](params0, "W")
            project(block, x_outer, w0)

            @block.sync
            def _(sp):
                sp.dma_start(params0, l0_params).then_inc(s_load, 16)
                store_table(sp, table0, stage[:, :, :])

            @block.scalar
            def _(act):
                project_copies(act)

            @block.vector
            def _(dve):
                then = chain(dve)
                take_products(dve, stage, lambda o, i, b: dve.tensor_copy(o, i))
                for name, to in (("att_dst", dst_rows[:, :, 0:H]), ("att_src", stage[:, :, D:D + H])):
                    then(dve.tensor_tensor(tmp[:, :, :], whole(stage), over_blocks(COLS["l0"](params0, name)), ALU.mult))
                    then(dve.tensor_reduce(out=to, in_=tmp[:, :, :].rearrange("p b (h c) -> p b h c", h=H),
                                           op=ALU.add, axis=AX.X))
                dve.sem_inc(s_ready, 1)
                then(dve.tensor_copy(head_max[:, :, :], stage[:, :, D:D + H]))
                then(dve.memset(window[:, :], 0.0))
        stage_end()

        run_windows(max_pass)

        with nc.Block() as block:
            @block.sync
            def _(sp):
                store_table(sp, table_dst, dst_rows[:, :, :])

            @block.scalar
            def _(act):
                act.wait_ge(s_var, 1)
                act.activation(self_weight[:, :, :], self_weight[:, :, :], ACT.Exp).then_inc(s_std, 1)
                act.wait_ge(s_std, 1)

            @block.vector
            def _(dve):
                then = chain(dve)
                for source, to in ((head_max[:, :, :], dst_rows[:, :, H:2 * H]),
                                   (stage[:, :, D:D + H], self_weight[:, :, :])):
                    then(dve.tensor_tensor(to, source, dst_rows[:, :, 0:H], ALU.add))
                    then(dve.scalar_tensor_tensor(out=to, in0=to, scalar=0.2, in1=to, op0=ALU.mult, op1=ALU.max))
                dve.sem_inc(s_ready, 1)
                dve.tensor_tensor(self_weight[:, :, :], self_weight[:, :, :], dst_rows[:, :, H:2 * H], ALU.subtract).then_inc(s_var, 1)
                then(dve.memset(acc[:, :, :], 0.0))
                then(dve.memset(message[:, :, :, D + H:ACCW], 1.0))
                then(dve.memset(window[:, :], 0.0))
        stage_end()

        run_windows(attention_pass)

        with nc.Block() as block:
            @block.scalar
            def _(act):
                act.wait_ge(s_var, 1)
                act.activation(dinv[:, :], dinv[:, :], ACT.Sqrt).then_inc(s_std, 1)
                layer_norm_root(act, 1)
                layer_norm_root(act, 2)

            @block.vector
            def _(dve):
                then = chain(dve)
                then(dve.tensor_copy(count[:, :], acc[:, :, D + H]))
                dve.tensor_scalar(dinv[:, :], count[:, :], 1.0, None, ALU.add).then_inc(s_var, 1)
                by_head = lambda t: t.rearrange("p b (h c) -> p (b h) c", h=H)
                weight = self_weight[:, :, :].rearrange("p b h -> p (b h)").unsqueeze(2).broadcast_to([P, B * H, DH])
                for h in range(H):
                    cols = slice(h * DH, (h + 1) * DH)
                    then(dve.tensor_tensor(tmp[:, :, cols], stage[:, :, cols], over_row(self_weight[:, :, h], DH), ALU.mult))
                then(dve.tensor_tensor(whole(acc), whole(acc), tmp[:, :, :], ALU.add))
                then(dve.tensor_tensor(self_weight[:, :, :], self_weight[:, :, :], acc[:, :, D:D + H], ALU.add))
                then(dve.tensor_scalar(self_weight[:, :, :], self_weight[:, :, :], 1e-16, None, ALU.add))
                then(dve.reciprocal(self_weight[:, :, :], self_weight[:, :, :]))
                for h in range(H):
                    cols = slice(h * DH, (h + 1) * DH)
                    then(dve.tensor_tensor(tmp[:, :, cols], acc[:, :, cols], over_row(self_weight[:, :, h], DH), ALU.mult))
                then(dve.tensor_tensor(x_inner[:, :, :], tmp[:, :, :], over_blocks(COLS["l0"](params0, "bias")), ALU.add))
                then(dve.tensor_tensor(x_inner[:, :, :], x_inner[:, :, :], x_outer[:, :, :], ALU.add))
                layer_norm(dve, then, 1, x_inner[:, :, :], x_inner[:, :, :],
                           COLS["l0"](params0, "gamma"), COLS["l0"](params0, "beta"))
                then(dve.tensor_tensor(x_inner[:, :, :], x_inner[:, :, :], x_outer[:, :, :], ALU.add))
                layer_norm(dve, then, 2, x_inner[:, :, :], x_outer[:, :, :])
                then(dve.reciprocal(dinv[:, :], dinv[:, :]))
                then(dve.tensor_copy(x_inner[:, :, :], x_outer[:, :, :]))
        stage_end()

        with nc.Fori(0, l1_layers) as layer:
            with nc.Block() as block:
                project(block, x_inner, COLS["l1"](params, "W"))

                @block.sync
                def _(sp):
                    sp.dma_start(params1, of_group(l1_params, layer)).then_inc(s_load, 16)
                    store_table(sp, table, whole(stage))

                @block.scalar
                def _(act):
                    project_copies(act)

                @block.vector
                def _(dve):
                    then = chain(dve)
                    take_products(dve, stage, lambda o, i, b: dve.tensor_tensor(
                        o, i, over_row(dinv[:, b], D, C), ALU.mult))
                    dve.sem_inc(s_ready, 1)
                    then(dve.memset(acc[:, :, :], 0.0))
                    then(dve.memset(window[:, :], 0.0))
            stage_end()

            run_windows(sum_pass)

            with nc.Block() as block:
                @block.vector
                def _(dve):
                    then = chain(dve)
                    then(dve.tensor_tensor(whole(acc), whole(acc), whole(stage), ALU.add))
                    then(dve.tensor_tensor(whole(acc), whole(acc), over_row(dinv[:, :]), ALU.mult))
                    then(dve.tensor_tensor(whole(acc), whole(acc), over_blocks(COLS["l1"](params, "b")), ALU.add))
                    then(dve.tensor_scalar(x_inner[:, :, :], whole(acc), 0.0, None, ALU.max))
            stage_end()

        with nc.Block() as block:
            project(block, x_inner, COLS["l1"](params, "W"))

            @block.sync
            def _(sp):
                sp.dma_start(params1, of_group(l1_params, l1_layers)).then_inc(s_load, 16)

            @block.scalar
            def _(act):
                project_copies(act)
                layer_norm_root(act, 0)

            @block.vector
            def _(dve):
                then = chain(dve)
                dve.wait_ge(s_load, 16)
                take_products(dve, acc, lambda o, i, b: dve.tensor_tensor(
                    o, i, over_blocks(COLS["l1"](params, "b"), D, C), ALU.add))
                then(dve.tensor_tensor(whole(acc), whole(acc), x_outer[:, :, :], ALU.add))
                layer_norm(dve, then, 0, whole(acc), x_outer[:, :, :])
                then(dve.tensor_copy(x_inner[:, :, :], x_outer[:, :, :]))
        stage_end()

        p2 = lambda name: COLS["l2"](params, name)
        with nc.Fori(0, l2_layers) as layer:
            with nc.Block() as block:
                @block.sync
                def _(sp):
                    sp.dma_start(params[:, :], of_group(l2_params, layer)).then_inc(s_load, 16)
                    store_table(sp, table, whole(stage))

                @block.scalar
                def _(act):
                    act.sem_inc(s_chunk_tc, 2)
                    act.sem_inc(s_chunk_b, 2)
                    act.wait_ge(s_load, 16)

                    def body(i):
                        for slot in range(2):
                            copy_transposed(act, i * 2 + slot, slot, s_chunk_h)
                        for slot in range(2):
                            c = i * 2 + slot
                            act.wait_ge(s_chunk_h, c + 3)
                            act.wait_ge(s_chunk_m, c + 1)
                            act.activation(hidden[:, slot, :], bank[2 + slot], ACT.Identity, bias=p2("b1")).then_inc(s_chunk_b, 1)

                    each_chunk_pair(act, body)

                bring_chunks(block, x_inner)

                @block.tensor
                def _(pe):
                    pe.sem_inc(s_chunk_t, 2)
                    pe.wait_ge(s_load, 16)
                    pe.sem_inc(s_chunk_h, 2)
                    pe.sem_inc(s_chunk_m, 2)

                    def body(i):
                        for slot in range(2):
                            transpose_chunk(pe, i * 2 + slot, slot)
                        for slot in range(2):
                            c = i * 2 + slot
                            pe.wait_ge(s_chunk_tc, c + 3)
                            pe.wait_ge(s_chunk_b, c + 1)
                            for n in range(C):
                                ins = pe.matmul(bank[2 + slot][:, n * P:(n + 1) * P], p2("W1")[:, n % 2 * P:(n % 2 + 1) * P],
                                                node_t[:, slot, n // 2, :], start=True, stop=True)
                            ins.then_inc(s_chunk_h, 1)
                        for slot in range(2):
                            c = i * 2 + slot
                            pe.wait_ge(s_chunk_l, c + 1)
                            pe.wait_ge(s_chunk_o, c + 1)
                            for n in range(C):
                                ins = pe.matmul(bank[6 + slot][:, n * D:(n + 1) * D],
                                                hidden[:, slot, n * P:(n + 1) * P], p2("W2"), start=True, stop=True)
                            ins.then_inc(s_chunk_m, 1)

                    each_chunk_pair(pe, body)

                @block.vector
                def _(dve):
                    then = chain(dve)
                    dve.sem_inc(s_chunk_o, 2)
                    dve.wait_ge(s_load, 16)

                    def body(i):
                        for slot in range(2):
                            c = i * 2 + slot
                            dve.wait_ge(s_chunk_b, c + 3)
                            dve.scalar_tensor_tensor(
                                out=hidden[:, slot, :], in0=hidden[:, slot, :], scalar=0.1,
                                in1=hidden[:, slot, :], op0=ALU.mult, op1=ALU.max).then_inc(s_chunk_l, 1)
                        for slot in range(2):
                            c = i * 2 + slot
                            dve.wait_ge(s_chunk_m, c + 3)
                            dve.tensor_tensor(
                                stage[:, bass.ds(c * C, C), 0:D], bank[6 + slot][:, 0:C * D].rearrange("p (b d) -> p b d", d=D),
                                over_blocks(p2("b2"), D, C), ALU.add).then_inc(s_chunk_o, 1)

                    each_chunk_pair(dve, body)
                    dve.wait_ge(s_chunk_o, 2 + L.chunks)
                    dve.sem_inc(s_ready, 1)
                    minus = p2("We1").rearrange("p (j s d) -> p j s d", j=4, s=2)[:, :, 1, :]
                    then(dve.tensor_scalar(minus, minus, -1.0, None, ALU.mult))
                    then(dve.tensor_scalar(p2("be1")[D:2 * D, :], p2("be1")[D:2 * D, :], -1.0, None, ALU.mult))
                    then(dve.tensor_scalar(p2("We2")[D:2 * D, :], p2("We2")[D:2 * D, :], -0.1, None, ALU.mult))
                    then(dve.memset(acc[:, :, :], 0.0))
                    then(dve.memset(window[:, :], 0.0))
            stage_end()

            run_windows(edge_mlp_pass)

            with nc.Block() as block:
                @block.scalar
                def _(act):
                    layer_norm_root(act, 0)

                @block.vector
                def _(dve):
                    then = chain(dve)
                    then(dve.tensor_scalar(whole(acc), whole(acc), p2("dot_scale"), p2("res_w"), ALU.mult, ALU.mult))
                    then(dve.tensor_tensor(x_inner[:, :, :], x_inner[:, :, :], whole(acc), ALU.add))
                    layer_norm(dve, then, 0, x_inner[:, :, :], x_inner[:, :, :], p2("ln_g"), p2("ln_b"))
            stage_end()

        with nc.Block() as block:
            @block.sync
            def _(sp):
                store_table(sp, table, x_outer[:, :, :])

            @block.scalar
            def _(act):
                layer_norm_root(act, 0)

            @block.vector
            def _(dve):
                then = chain(dve)
                then(dve.tensor_tensor(x_inner[:, :, :], x_inner[:, :, :], x_outer[:, :, :], ALU.add))
                layer_norm(dve, then, 0, x_inner[:, :, :], x_outer[:, :, :])
                dve.sem_inc(s_ready, 1)
                then(dve.memset(acc[:, :, :], 0.0))
                then(dve.memset(window[:, :], 0.0))
                then(dve.tensor_scalar(count[:, :], count[:, :], 1.0, None, ALU.max))
                then(dve.reciprocal(count[:, :], count[:, :]))
        stage_end()

        run_windows(sum_pass)

        with nc.Block() as block:
            @block.vector
            def _(dve):
                then = chain(dve)
                then(dve.tensor_tensor(x_inner[:, :, :], whole(acc), over_row(count[:, :]), ALU.mult))
        stage_end()

        with nc.Block() as block:
            p3 = lambda name: COLS["l3"](params3, name)
            w3 = p3("W")

            project(block, x_inner, w3)

            @block.sync
            def _(sp):
                sp.dma_start(params3, l3_params).then_inc(s_load, 16)

            @block.scalar
            def _(act):
                project_copies(act)
                act.wait_ge(s_var, 1)
                act.activation(tmp[:, :, :], tmp[:, :, :], ACT.Exp).then_inc(s_std, 1)

            @block.vector
            def _(dve):
                then = chain(dve)
                take_products(dve, acc, lambda o, i, b: dve.tensor_copy(o, i))
                dve.tensor_scalar(tmp[:, :, :], whole(acc), 0.0, None, ALU.min).then_inc(s_var, 1)
                then(dve.tensor_scalar(whole(acc), whole(acc), 0.0, -1.0, ALU.max, ALU.add))
                dve.wait_ge(s_std, 1)
                then(dve.tensor_tensor(whole(acc), whole(acc), tmp[:, :, :], ALU.add))
                then(dve.tensor_tensor(whole(acc), whole(acc), over_row(valid[:, :]), ALU.mult))
                then(dve.tensor_reduce(out=over_nodes[:, 0, :], in_=whole(acc).rearrange("p b d -> p d b"), op=ALU.add, axis=AX.X))
        stage_end()

        with nc.Block() as block:
            @block.tensor
            def _(pe):
                pe.matmul(bank[0][:, 0:D], ones[:, :], over_nodes[:, 0, :], start=True, stop=True).then_inc(s_pe, 1)
                pe.wait_ge(s_ready, 1)
                pe.matmul(bank[0][:, D:2 * D], ones[:, :], over_nodes[:, 2, :], start=True, stop=True).then_inc(s_pe, 1)

            @block.scalar
            def _(act):
                act.wait_ge(s_var, 1)
                act.activation(over_nodes[:, 3, :], over_nodes[:, 3, :], ACT.Sqrt).then_inc(s_std, 1)
                layer_norm_root(act, 1)

            @block.vector
            def _(dve):
                then = chain(dve)
                mean, squares, scale = (over_nodes[:, n, :] for n in (1, 2, 3))
                dve.wait_ge(s_pe, 1)
                then(dve.tensor_scalar(mean, bank[0][:, 0:D], 1.0 / L.nodes, None, ALU.mult))
                then(dve.tensor_tensor(whole(acc), whole(acc), over_blocks(mean), ALU.subtract))
                then(dve.tensor_tensor(tmp[:, :, :], whole(acc), whole(acc), ALU.mult))
                then(dve.tensor_tensor(tmp[:, :, :], tmp[:, :, :], over_row(valid[:, :]), ALU.mult))
                then(dve.tensor_reduce(out=squares, in_=tmp[:, :, :].rearrange("p b d -> p d b"), op=ALU.add, axis=AX.X))
                dve.sem_inc(s_ready, 1)
                dve.wait_ge(s_pe, 2)
                dve.tensor_scalar(scale, bank[0][:, D:2 * D], 1.0 / L.nodes, 1e-5, ALU.mult, ALU.add).then_inc(s_var, 1)
                dve.wait_ge(s_std, 1)
                then(dve.reciprocal(scale, scale))
                then(dve.tensor_tensor(scale, scale, p3("gamma"), ALU.mult))
                then(dve.tensor_tensor(whole(acc), whole(acc), over_blocks(scale), ALU.mult))
                then(dve.tensor_tensor(whole(acc), whole(acc), over_blocks(p3("beta")), ALU.add))
                then(dve.tensor_tensor(whole(acc), whole(acc), x_outer[:, :, :], ALU.add))
                layer_norm(dve, then, 1, whole(acc), x_outer[:, :, :])
                dve.sem_inc(s_turn, 1)

            @block.sync
            def _(sp):
                sp.wait_ge(s_turn, 1)
                full = L.nodes // P
                stores = 0
                if full:
                    sp.dma_start(rows_of(out[0:full * P, :]), x_outer[:, 0:full, :]).then_inc(s_store, 16)
                    stores += 1
                if L.nodes % P:
                    sp.dma_start(out[full * P:L.nodes, :], x_outer[0:L.nodes % P, full, :]).then_inc(s_store, 16)
                    stores += 1
                sp.wait_ge(s_store, 16 * stores)
    return nc


def kernel(x, src, dst, edge_attr_32, **w):
    import numpy as np
    import concourse.bacc as bacc
    from concourse.bass_utils import run_bass_kernel_spmd

    x, attr = np.asarray(x), np.asarray(edge_attr_32)
    nodes, dim = x.shape
    edges, edge_dim = attr.shape
    w = {k: np.asarray(v) for k, v in w.items()}
    heads = w["L0_gnn_att_src"].shape[0]
    L = Layout(nodes, edges, dim, heads, edge_dim)
    cols = param_columns(dim)

    def padded(a, n):
        return np.concatenate([a, np.broadcast_to(a[-1:], (n - a.shape[0],) + a.shape[1:])])

    def rows(v):
        return np.broadcast_to(np.reshape(v, (1, -1)), (P, np.size(v)))

    def stacked(m):
        return np.tile(m, (P // m.shape[0], 1))

    def diagonal(m, times):
        out = np.zeros((times, m.shape[0], times, m.shape[1]), m.dtype)
        for n in range(times):
            out[n, :, n, :] = m
        return out.reshape(times * m.shape[0], times * m.shape[1])

    def packed(layer, **named):
        return np.ascontiguousarray(np.concatenate([named[n] for n in cols[layer].at], axis=1))

    src_p = padded(np.asarray(src).astype(np.int32), L.tiles * P)
    dst_p = padded(np.asarray(dst).astype(np.int32), L.tiles * P)

    def by_group(idx):
        return np.ascontiguousarray(idx.reshape(L.groups, G, P).transpose(0, 2, 1))

    attr_p = np.zeros((L.tiles * P, edge_dim), attr.dtype)
    attr_p[:edges] = attr
    attr_p = attr_p.reshape(L.groups, G // 4, 4, P, edge_dim).transpose(0, 2, 4, 1, 3)
    x_p = np.zeros((L.blocks * P, dim), x.dtype)
    x_p[:nodes] = x
    l1_w = list(w["L1_gnn_Ws"]) + [w["L1_gnn_W_out"]]
    l1_b = list(w["L1_gnn_bs"]) + [w["L1_gnn_b_out"]]
    l2 = {k[7:]: v for k, v in w.items() if k.startswith("L2_gnn_")}
    arrays = {
        "src_idx": by_group(src_p),
        "dst_idx": by_group(dst_p),
        "dst_tiles": np.ascontiguousarray(dst_p.reshape(L.tiles, P).T),
        "dst_groups": dst_p.reshape(L.groups, G * P),
        "x": x_p,
        "attr": np.ascontiguousarray(attr_p).reshape(L.groups, P, G // 4 * P),
        "l0_params": packed("l0", W=diagonal(w["L0_gnn_W"], 2), att_src=rows(w["L0_gnn_att_src"]),
                            att_dst=rows(w["L0_gnn_att_dst"]), bias=rows(w["L0_gnn_bias"]),
                            gamma=rows(w["L0_gnn_gamma"]), beta=rows(w["L0_gnn_beta"])),
        "l1_params": np.stack([packed("l1", W=diagonal(a, 2), b=rows(b)) for a, b in zip(l1_w, l1_b)]),
        "l2_params": np.stack([
            packed("l2", W1=diagonal(l2["W1"][n], 2), b1=l2["b1"][n][:, None], W2=l2["W2"][n], b2=rows(l2["b2"][n]),
                   We1=diagonal(np.tile(l2["We1"][n], (1, 2)), 4), be1=stacked(l2["be1"][n][:, None]),
                   We2=stacked(l2["We2"][n]), be2=rows(l2["be2"][n]), res_w=rows(l2["res_w"][n]),
                   dot_scale=rows(l2["dot_scale"][n]), ln_g=rows(l2["ln_g"][n]), ln_b=rows(l2["ln_b"][n]))
            for n in range(l2["W1"].shape[0])]),
        "l3_params": packed("l3", W=diagonal(w["L3_gnn_W"], 2), gamma=rows(w["L3_gnn_gamma"]), beta=rows(w["L3_gnn_beta"])),
    }
    nc = bacc.Bacc("TRN2", target_bir_lowering=False, num_devices=1)
    t = {k: nc.dram_tensor(k, a.shape, mybir.dt.from_np(a.dtype), kind="ExternalInput").ap() for k, a in arrays.items()}
    out = nc.dram_tensor("out", (nodes, dim), F32, kind="ExternalOutput").ap()
    build(nc, L, t["src_idx"], t["dst_idx"], t["dst_tiles"], t["dst_groups"], t["x"], t["attr"], t["l0_params"],
          t["l1_params"], t["l2_params"], t["l3_params"], len(w["L1_gnn_Ws"]), len(l2["W1"]), out)
    r = run_bass_kernel_spmd(nc, [arrays], core_ids=[0])
    return r.results[0]["out"]
```

```python
import concourse.bass as bass
from concourse import mybir
from contextlib import ExitStack

F32 = mybir.dt.float32
BF16 = mybir.dt.bfloat16
I32 = mybir.dt.int32
ALU = mybir.AluOpType
ACT = mybir.ActivationFunctionType
AX = mybir.AxisListType

P = 128
G = 8
U = 4
C = 4
FAR = 2.0 ** 100


class Layout:

    def __init__(self, nodes, edges, dim, heads, edge_dim):
        self.nodes, self.edges, self.dim, self.heads, self.edge_dim = nodes, edges, dim, heads, edge_dim
        self.groups = -(-edges // (P * G * U)) * U
        self.tiles = self.groups * G
        self.blocks_used = -(-nodes // P)
        self.blocks = -(-(self.blocks_used + 1) // (2 * C)) * 2 * C
        self.chunks = self.blocks // C
        self.group_rows = -(-self.groups // P)
        while self.groups % self.group_rows:
            self.group_rows += 1


class Params:

    def __init__(self, *columns):
        self.at, self.width = {}, 0
        for name, width in columns:
            self.at[name] = (self.width, self.width + width)
            self.width += width

    def __call__(self, tensor, name):
        a, b = self.at[name]
        return tensor[:, a:b]


def param_columns(dim):
    return {
        "l0": Params(("W", 2 * dim), ("att_src", dim), ("att_dst", dim), ("bias", dim), ("gamma", dim),
                     ("beta", dim)),
        "l1": Params(("W", 2 * dim), ("b", dim)),
        "l2": Params(("W1", 4 * dim), ("b1", 1), ("W2", dim), ("b2", dim), ("We1", 4 * dim),
                     ("be1", 1), ("We2", 2 * dim), ("be2", dim), ("res_w", 1), ("dot_scale", 1),
                     ("ln_g", dim), ("ln_b", dim)),
        "l3": Params(("W", 2 * dim), ("gamma", dim), ("beta", dim)),
    }


class Steps:

    def __init__(self, semaphore):
        self.semaphore, self.count = semaphore, 0

    def add(self, instruction):
        instruction.then_inc(self.semaphore, 1)
        self.count += 1


def build(nc, L, src_idx, dst_tiles, dst_groups, x_in, attr, l0_params, l1_params, l2_params,
          l3_params, l1_layers, l2_layers, out):
    D, H, DH = L.dim, L.heads, L.dim // L.heads
    B, NG, NT = L.blocks, L.groups, L.tiles
    ITER = NG // U
    COLS = param_columns(D)
    ROW0 = D + H
    ACCW = D + H + 1
    ctx = ExitStack()
    with ctx:
        def sb(name, shape, dt):
            return ctx.enter_context(nc.sbuf_tensor(name, shape, dt))

        def ps(name, shape, dt):
            return ctx.enter_context(nc.psum_tensor(name, shape, dt))

        semaphores = []

        def sem(name):
            s = ctx.enter_context(nc.semaphore(name))
            semaphores.append(s)
            return s

        def scratch(name, shape, dt):
            return nc.dram_tensor(name, shape, dt, kind="Internal").ap()

        table0 = scratch("attention_table", (B * P, ROW0), F32)
        table = scratch("feature_table", (B * P, D), F32)
        spill = scratch("gathered_rows", (NG, P, G * ROW0), F32)
        group_min = scratch("group_min", (NG, 1), I32)
        group_max = scratch("group_max", (NG, 1), I32)

        ident = sb("ident", [P, P], F32)
        ident_bf = sb("ident_bf", [P, P], BF16)
        iota1 = sb("iota1", [P, P], F32)
        iota_p = sb("iota_p", [P, 1], F32)
        ones = sb("ones", [P, P], F32)
        far_ident = sb("far_ident", [P, H, P], BF16)
        assert B <= 256
        block_of = sb("block_of", [P, NT], BF16)
        place_of = sb("place_of", [P, NT], BF16)
        key = sb("key", [P, NT], F32)
        base_place = sb("base_place", [P, NG], F32)
        near_block = sb("near_block", [1, NG], F32)
        low = sb("low", [P, NG], F32)
        high = sb("high", [P, NG], F32)
        low_far = sb("low_far", [P, NG], F32)
        high_far = sb("high_far", [P, NG], F32)
        pass_block = sb("pass_block", [1, NG], I32)
        scattered = sb("scattered", [P, 1], F32)
        gathered_near = sb("gathered_near", [P, 1], F32)
        window = sb("window", [P, 1], F32)
        windows = sb("windows", [1, 1], I32)
        valid = sb("valid", [P, B], F32)
        count = sb("count", [P, B], F32)
        dinv = sb("dinv", [P, B], F32)
        stat = sb("stat", [P, 3, B], F32)
        x_outer = sb("x_outer", [P, B, D], F32)
        x_inner = sb("x_inner", [P, B, D], F32)
        acc = sb("acc", [P, B, ACCW], F32)
        stage = sb("stage", [P, B, ROW0], F32)
        tmp_flat = sb("tmp", [P, max(B * D, 5 * G * P)], F32)
        tmp = tmp_flat[:, 0:B * D].rearrange("p (b d) -> p b d", d=D)
        onehots = tmp_flat[:, 0:4 * G * P].rearrange("p (s t e) -> p s t e", s=4, t=G)
        onehots_t = tmp_flat[:, 4 * G * P:5 * G * P].bitcast(BF16).rearrange("p (s t e) -> p s t e", s=2, t=G)
        dst_parts = x_inner[:, :, 0:3 * H].bitcast(BF16).rearrange("p b (h n) -> p b h n", n=3)
        head_max = sb("head_max", [P, B, H], F32)
        dst_rows = sb("dst_rows", [P, B, 2 * H], F32)
        self_weight = sb("self_weight", [P, B, H], F32)

        idx_buf = sb("idx_buf", [P, U, G], I32)
        rows_buf = sb("rows_buf", [P, U, G, ROW0], F32)
        onehot = sb("onehot", [P, 2, G, P], F32)
        not_hot = onehot[:, 0, :, :].rearrange("p g e -> p (g e)").bitcast(BF16).rearrange("p (s g e) -> p s g e", s=2, g=G)
        attr_buf = sb("attr_buf", [P, U, G // 4, P], F32)
        hidden = sb("hidden", [P, 2, 4 * P], F32)
        message = sb("message", [P, 2, G, ACCW], F32)
        edge_feat = sb("edge_feat", [P, G, D], F32)
        parts = sb("parts", [P, 2, 3, G * H], BF16)
        rest = sb("rest", [P, 2, G, H], F32)
        parts_t = sb("parts_t", [3 * G * H, 2, P], BF16)
        pick = sb("pick", [3 * G * H, G * H], BF16)
        red = sb("red", [P, G, H], F32)
        red1 = sb("red1", [P, H], F32)
        logit = sb("logit", [P, 4, G, H], F32)
        dst_value = sb("dst_value", [P, G, 2 * H], F32)
        window_dst = sb("window_dst", [P, 2, 6 * H], BF16)
        params = sb("params", [P, COLS["l2"].width], F32)
        params1 = params[:, 0:COLS["l1"].width]
        params0 = params[:, 0:COLS["l0"].width]
        params3 = params[:, 0:COLS["l3"].width]
        over_nodes = params[:, COLS["l3"].width:COLS["l3"].width + 4 * D].rearrange("p (n d) -> p n d", n=4)
        rows_flat = rows_buf[:, :, :, :].rearrange("p u g w -> p (u g w)")
        node_x = rows_flat[:, 0:2 * C * D].rearrange("p (s b d) -> p s b d", s=2, d=D)
        node_t = rows_flat[:, 2 * C * D:4 * C * D].rearrange("p (s j n) -> p s j n", s=2, n=P)

        dst_i = tmp[:, :, :].rearrange("p b d -> p (b d)")[:, 0:NT].bitcast(I32)
        dst_part = x_inner[:, :, :].rearrange("p b d -> p (b d)")[:, 0:NT].bitcast(I32)
        GR, GP = L.group_rows, NG // L.group_rows
        stage_flat = stage[:, :, :].rearrange("p b d -> p (b d)")
        acc_flat = acc[:, :, :].rearrange("p b d -> p (b d)")
        groups_i = stage_flat[0:GP, 0:GR * G * P].bitcast(I32).rearrange("p (r e) -> p r e", r=GR)
        groups_f = acc_flat[0:GP, 0:GR * G * P].rearrange("p (r e) -> p r e", r=GR)
        span = sb("span", [P, 4, max(GR, 2)], F32)
        span_i = sb("span_i", [P, 2, GR], I32)
        x_inner_flat = x_inner[:, :, :].rearrange("p b d -> p (b d)")
        base_i = x_inner_flat[:, NT:NT + 3 * NG].bitcast(I32).rearrange("p (n g) -> p n g", n=3)
        span_row = x_inner_flat[:, NT + 3 * NG:NT + 6 * NG].rearrange("p (n g) -> p n g", n=3)

        banks = ps("banks", [P, 8, 512], F32)
        bank = [banks[:, n, :] for n in range(8)]

        s_load = sem("s_load")
        s_load2 = sem("s_load2")
        s_store = sem("s_store")
        s_pool = sem("s_pool")
        s_dve = sem("s_dve")
        s_ready = sem("s_ready")
        s_var = sem("s_var")
        s_std = sem("s_std")
        s_pe = sem("s_pe")
        s_chunk_x = sem("s_chunk_x")
        s_chunk_t = sem("s_chunk_t")
        s_chunk_tc = sem("s_chunk_tc")
        s_chunk_m = sem("s_chunk_m")
        s_chunk_o = sem("s_chunk_o")
        s_chunk_h = sem("s_chunk_h")
        s_chunk_b = sem("s_chunk_b")
        s_chunk_l = sem("s_chunk_l")
        s_turn = sem("s_turn")
        s_idx = [sem(f"s_idx{u}") for u in range(U)]
        s_rows = [sem(f"s_rows{u}") for u in range(U)]
        s_attr = [sem(f"s_attr{u}") for u in range(U)]
        s_spill = [sem(f"s_spill{u}") for u in range(U)]
        s_hot = sem("s_hot")
        s_sum = sem("s_sum")
        s_acc = sem("s_acc")
        s_hid = sem("s_hid")
        s_act_hid = sem("s_act_hid")
        s_leaky = sem("s_leaky")
        s_edge = sem("s_edge")
        s_feat = sem("s_feat")
        s_split = sem("s_split")
        s_tr = sem("s_tr")
        s_tr_sb = sem("s_tr_sb")
        s_msg = sem("s_msg")
        s_bc = sem("s_bc")
        s_red = sem("s_red")
        s_group = sem("s_group")
        s_window = sem("s_window")
        s_hot_t = sem("s_hot_t")
        s_hot_t_sb = sem("s_hot_t_sb")
        s_dst = sem("s_dst")
        s_logit = sem("s_logit")
        s_exp = sem("s_exp")
        numbers = [s.num for s in semaphores]
        assert numbers == list(range(numbers[0], numbers[0] + len(numbers)))

        def stage_end():
            used = range(numbers[0], numbers[-1] + 1)
            nc.gpsimd.dma_reset(used)
            nc.gpsimd.sem_clear(used)
            nc.all_engine_barrier()

        def whole(t, width=D):
            return t[:, :, 0:width]

        def over_blocks(vector, width=D, blocks=B):
            return vector.unsqueeze(1).broadcast_to([P, blocks, width])

        def over_row(per_node, width=D, blocks=B):
            return per_node.unsqueeze(2).broadcast_to([P, blocks, width])

        def rows_of(t):
            return t.rearrange("(b p) d -> p b d", p=P)

        with nc.Block() as block:
            @block.sync
            def _(sp):
                sp.dma_start(dst_i, dst_tiles).then_inc(s_load, 16)
                sp.dma_start(groups_i, dst_groups.rearrange("(p r) e -> p r e", r=GR)).then_inc(s_idx[0], 16)
                sp.dma_start(params0, l0_params).then_inc(s_idx[1], 16)
                sp.dma_start(x_outer[:, :, :], x_in.rearrange("(b p) d -> p b d", p=P)).then_inc(s_idx[1], 16)
                sp.wait_ge(s_hot, 1)
                sp.dma_start(group_min.rearrange("(p r) o -> p (r o)", r=GR), span_i[0:GP, 0, :]).then_inc(s_store, 16)
                sp.dma_start(group_max.rearrange("(p r) o -> p (r o)", r=GR), span_i[0:GP, 1, :]).then_inc(s_store, 16)
                sp.wait_ge(s_store, 32)
                for n, t in enumerate((group_min, group_max)):
                    sp.dma_start(base_i[:, n, :], t.rearrange("g o -> o g").broadcast_to([P, NG])).then_inc(s_attr[0], 16)
                sp.wait_ge(s_idx[1], 32)

            @block.gpsimd
            def _(pool):
                pool.iota(iota1[:, :], pattern=[[1, P]], base=1, channel_multiplier=0,
                          allow_small_or_imprecise_dtypes=True).then_inc(s_pool, 1)
                pool.iota(iota_p[:, :], pattern=[[0, 1]], base=0, channel_multiplier=1,
                          allow_small_or_imprecise_dtypes=True).then_inc(s_pool, 1)
                pool.memset(ident[:, :], 0.0).then_inc(s_pool, 1)
                pool.memset(ones[:, :], 1.0).then_inc(s_pool, 1)
                pool.memset(far_ident[:, :, :], 0.0).then_inc(s_pool, 1)
                pool.memset(valid[:, :], 1.0).then_inc(s_pool, 1)
                pool.memset(pick[:, :], 0.0).then_inc(s_pool, 1)
                pool.wait_ge(s_pool, 7)
                for part in range(3):
                    pool.affine_select(out=pick[:, :], in_=pick[:, :], compare_op=ALU.not_equal, fill=1.0,
                                       base=-part * G * H, pattern=[[-1, G * H]],
                                       channel_multiplier=1).then_inc(s_pool, 1)
                    pool.wait_ge(s_pool, 8 + part)
                pool.affine_select(out=ident[:, :], in_=ident[:, :], compare_op=ALU.not_equal, fill=1.0,
                                   base=0, pattern=[[-1, P]], channel_multiplier=1).then_inc(s_pool, 1)
                pool.affine_select(out=far_ident[:, :, :], in_=far_ident[:, :, :], compare_op=ALU.not_equal,
                                   fill=-FAR, base=0, pattern=[[0, H], [-1, P]],
                                   channel_multiplier=1).then_inc(s_pool, 1)
                pool.affine_select(out=valid[:, :], in_=valid[:, :], compare_op=ALU.is_ge, fill=0.0,
                                   base=L.nodes - 1, pattern=[[-P, B]], channel_multiplier=-1).then_inc(s_pool, 1)
                pool.wait_ge(s_dve, 4)
                pool.affine_select(out=place_of[:, :], in_=place_of[:, :], compare_op=ALU.is_ge, fill=0.0,
                                   base=L.edges - 1, pattern=[[-P, NT]], channel_multiplier=-1).then_inc(s_pool, 1)

            @block.vector
            def _(dve):
                d = Steps(s_dve)

                def then(instruction):
                    d.add(instruction)
                    dve.wait_ge(s_dve, d.count)

                dve.wait_ge(s_load, 16)
                then(dve.tensor_scalar(dst_part, dst_i, 127, None, ALU.bitwise_and))
                then(dve.tensor_scalar(place_of[:, :], dst_part, 1.0, None, ALU.add))
                then(dve.tensor_scalar(dst_part, dst_i, 7, None, ALU.logical_shift_right))
                then(dve.tensor_copy(block_of[:, :], dst_part))
                dve.wait_ge(s_idx[0], 16)
                then(dve.tensor_copy(groups_f, groups_i))
                then(dve.tensor_reduce(out=span[0:GP, 0, 0:GR], in_=groups_f, op=ALU.min, axis=AX.X))
                then(dve.tensor_reduce(out=span[0:GP, 1, 0:GR], in_=groups_f, op=ALU.max, axis=AX.X))
                then(dve.tensor_copy(span_i[0:GP, :, :], span[0:GP, 0:2, 0:GR]))
                dve.wait_ge(s_dve, d.count)
                dve.sem_inc(s_hot, 1)
                dve.wait_ge(s_attr[0], 32)
                then(dve.tensor_scalar(base_i[:, 2, :], base_i[:, 0, :], 127, None, ALU.bitwise_and))
                then(dve.tensor_copy(base_place[:, :], base_i[:, 2, :]))
                then(dve.tensor_scalar(base_i[:, 2, :], base_i[:, 0, :], 7, None, ALU.logical_shift_right))
                then(dve.tensor_copy(near_block[:, :], base_i[0:1, 2, :]))
                then(dve.tensor_copy(span_row[:, 0:2, :], base_i[:, 0:2, :]))
                then(dve.tensor_tensor(span_row[:, 2, :], span_row[:, 1, :], span_row[:, 0, :], ALU.subtract))
                then(dve.tensor_reduce(out=span[:, 2, 0:1], in_=span_row[:, 2, :], op=ALU.max, axis=AX.X))
                then(dve.tensor_scalar(scattered[:, :], span[:, 2, 0:1], float(P), None, ALU.is_ge))
                then(dve.tensor_scalar(gathered_near[:, :], scattered[:, :], -1.0, 1.0, ALU.mult, ALU.add))
                then(dve.tensor_scalar(span[:, 3, 0:1], scattered[:, :], float(L.blocks_used - 1), 1.0, ALU.mult, ALU.add))
                then(dve.tensor_copy(windows[:, :], span[0:1, 3, 0:1]))
                then(dve.tensor_scalar(near_block[:, :], near_block[:, :], gathered_near[0:1, :], None, ALU.mult))
                dve.wait_ge(s_pool, 2)
                then(dve.tensor_scalar(low[:, :], base_place[:, :], iota_p[:, :], scattered[:, :], ALU.is_le, ALU.max))
                dve.wait_ge(s_pool, 11)
                then(dve.tensor_copy(ident_bf[:, :], ident[:, :]))
                then(dve.tensor_scalar(high[:, :], low[:, :], -1.0, 1.0, ALU.mult, ALU.add))
                then(dve.tensor_scalar(low_far[:, :], high[:, :], -FAR, None, ALU.mult))
                then(dve.tensor_scalar(high_far[:, :], low[:, :], -FAR, None, ALU.mult))
                dve.wait_ge(s_pool, 14)
        stage_end()
        pass_windows = nc.values_load(windows[0:1, 0:1], min_val=1, max_val=L.blocks_used,
                                      skip_runtime_bounds_check_because="it is 1 or the number of blocks")

        def each_group(engine, body):
            with engine.Fori(0, ITER - 1) as i:
                for u in range(U):
                    body(i * U + u, i, u, U)
            for u in range(U):
                body((ITER - 1) * U + u, ITER - 1, u, U - 1 - u)

        def of_group(t, g):
            return t[bass.ds(g, 1), :, :].rearrange("o p e -> (o p) e")

        def index_loads(sp, indices, after_rows=None, beside=None):
            for u in range(U):
                sp.dma_start(idx_buf[:, u, :], of_group(indices, u)).then_inc(s_idx[u], 16)

            def body(g, i, u, ahead):
                if beside:
                    beside(g, i, u)
                sp.wait_ge(s_rows[u], (i + 1) * (16 * G))
                if after_rows:
                    after_rows(g, i, u)
                if ahead >= U:
                    sp.dma_start(idx_buf[:, u, :], of_group(indices, g + U)).then_inc(s_idx[u], 16)

            each_group(sp, body)

        def gather(pool, source, slot_rows, wait_free):
            with pool.Fori(0, ITER) as i:
                for u in range(U):
                    pool.wait_ge(s_idx[u], (i + 1) * 16)
                    wait_free(pool, i * U + u, i, u)
                    pool.sem_inc(s_turn, 1)
                    for t in range(G):
                        pool.indirect_dma_start(
                            out=slot_rows(u, t), out_offset=None, in_=source,
                            in_offset=bass.IndirectOffsetOnAxis(ap=idx_buf[:, u, t:t + 1], axis=0),
                        ).then_inc(s_rows[u], 16)

        def open_windows(dve):
            d = Steps(s_dve)
            d.add(dve.tensor_scalar(key[:, :], block_of[:, :], window[:, :], gathered_near[:, :], ALU.is_equal, ALU.max))
            d.add(dve.tensor_tensor(span[0:1, 0, 0:1], window[0:1, :], scattered[0:1, :], ALU.mult))
            dve.wait_ge(s_dve, d.count)
            d.add(dve.tensor_tensor(key[:, :], key[:, :], place_of[:, :], ALU.mult))
            d.add(dve.tensor_scalar(pass_block[0:1, :], near_block[0:1, :], span[0:1, 0, 0:1], None, ALU.add))
            d.add(dve.tensor_scalar(window[:, :], window[:, :], 1.0, None, ALU.add))
            dve.wait_ge(s_dve, d.count)

        def make_onehot(dve, g, to, op=ALU.is_equal):
            dve.tensor_tensor(
                to, iota1[:, :].unsqueeze(1).broadcast_to([P, G, P]),
                key[:, bass.ds(g * G, G)].unsqueeze(2).broadcast_to([P, G, P]), op).then_inc(s_hot, 1)

        def block_of_group(dve, g):
            return dve.value_load(pass_block[0:1, bass.ds(g, 1)], min_val=0, max_val=L.blocks_used - 1)

        def add_side(dve, g, b, slot, width, n):
            if n == 0:
                dve.wait_ge(s_sum, g + (U + 1))
            dve.wait_ge(s_acc, g * 2 + (4 + n))
            to = acc[:, bass.ds(b + n, 1), 0:width].rearrange("p o w -> p (o w)")
            dve.scalar_tensor_tensor(
                out=to, in0=bank[6 + slot][:, 0:width], scalar=(low, high)[n][:, bass.ds(g, 1)], in1=to,
                op0=ALU.mult, op1=ALU.add).then_inc(s_acc, 1)

        def add_sums(dve, g, b, slot, width):
            for n in range(2):
                add_side(dve, g, b, slot, width, n)

        def sum_group(pe, g, slot, rows, width, hot=None):
            hot = onehot[:, slot, :, :] if hot is None else hot
            pe.wait_ge(s_hot, g + 1)
            pe.wait_ge(s_acc, g * 2 + 2)
            for t in range(G):
                ins = pe.matmul(bank[6 + slot][:, 0:width], hot[:, t, :], rows(t),
                                start=(t == 0), stop=(t == G - 1))
            ins.then_inc(s_sum, 1)

        def run_windows(emit):
            with nc.Fori(0, pass_windows):
                with nc.Block() as block:
                    emit(block)
                stage_end()

        def sum_pass(block):
            @block.sync
            def _(sp):
                index_loads(sp, src_idx)

            @block.gpsimd
            def _(pool):
                gather(pool, table, lambda u, t: rows_buf[:, u, t, 0:D],
                       lambda e, g, i, u: e.wait_ge(s_sum, g + 1))

            @block.vector
            def _(dve):
                dve.sem_inc(s_acc, 4)
                open_windows(dve)

                def body(g, i, u, ahead):
                    make_onehot(dve, g, onehot[:, u % 2, :, :])
                    add_sums(dve, g, block_of_group(dve, g), u % 2, D)

                each_group(dve, body)
                dve.wait_ge(s_acc, 4 + 2 * NG)

            @block.tensor
            def _(pe):
                pe.sem_inc(s_sum, U)

                def body(g, i, u, ahead):
                    pe.wait_ge(s_rows[u], (i + 1) * (16 * G))
                    sum_group(pe, g, u % 2, lambda t: rows_buf[:, u, t, 0:D], D)

                each_group(pe, body)

        def edge_mlp_pass(block):
            w1, b1 = COLS["l2"](params, "We1"), COLS["l2"](params, "be1")
            w2, b2 = COLS["l2"](params, "We2"), COLS["l2"](params, "be2")

            @block.sync
            def _(sp):
                def attributes(g, i, u):
                    sp.wait_ge(s_hid, g + 1)
                    sp.dma_start(attr_buf[:, u, :, :].rearrange("p a e -> p (a e)"), of_group(attr, g)).then_inc(s_attr[u], 16)

                index_loads(sp, src_idx, beside=attributes)

            @block.gpsimd
            def _(pool):
                gather(pool, table, lambda u, t: rows_buf[:, u, t, 0:D],
                       lambda e, g, i, u: e.wait_ge(s_msg, g + 1))

            @block.scalar
            def _(act):
                act.sem_inc(s_act_hid, 2)

                def body(g, i, u, ahead):
                    act.wait_ge(s_hid, g + (U + 1))
                    act.wait_ge(s_edge, g + 1)
                    act.activation(hidden[:, u % 2, :], bank[u % 2], ACT.Identity, bias=b1).then_inc(s_act_hid, 1)

                each_group(act, body)

            @block.vector
            def _(dve):
                dve.sem_inc(s_acc, 4)
                dve.sem_inc(s_msg, U)
                dve.sem_inc(s_feat, 2)
                open_windows(dve)

                def leaky(g, slot):
                    dve.wait_ge(s_act_hid, g + 3)
                    dve.scalar_tensor_tensor(out=hidden[:, slot, :], in0=hidden[:, slot, :], scalar=0.1,
                                             in1=hidden[:, slot, :], op0=ALU.mult, op1=ALU.max).then_inc(s_leaky, 1)

                leaky(0, 0)

                def body(g, i, u, ahead):
                    slot = u % 2
                    make_onehot(dve, g, onehot[:, slot, :, :])
                    b = block_of_group(dve, g)
                    if ahead >= 1:
                        leaky(g + 1, 1 - slot)
                    dve.wait_ge(s_edge, g + 3)
                    dve.wait_ge(s_msg, g + U)
                    dve.tensor_tensor(edge_feat[:, :, :], bank[4 + slot].rearrange("p (t d) -> p t d", d=D),
                                      b2.unsqueeze(1).broadcast_to([P, G, D]), ALU.add).then_inc(s_feat, 1)
                    dve.wait_ge(s_rows[u], (i + 1) * (16 * G))
                    dve.wait_ge(s_feat, g + 3)
                    dve.tensor_tensor(message[:, slot, :, 0:D], edge_feat[:, :, :], rows_buf[:, u, :, 0:D],
                                      ALU.mult).then_inc(s_msg, 1)
                    add_sums(dve, g, b, slot, D)

                each_group(dve, body)
                dve.wait_ge(s_acc, 4 + 2 * NG)

            @block.tensor
            def _(pe):
                pe.sem_inc(s_sum, U)
                pe.sem_inc(s_hid, U)
                pe.sem_inc(s_edge, 2)

                def hidden_layer(g, i, u):
                    pe.wait_ge(s_attr[u], (i + 1) * 16)
                    pe.wait_ge(s_act_hid, g + 1)
                    for pair in range(2):
                        ins = pe.matmul(bank[u % 2][:, pair * 2 * P:(pair + 1) * 2 * P], w1[:, pair * P:(pair + 1) * P],
                                        attr_buf[:, u, :, :].rearrange("p a e -> p (a e)"), start=True, stop=True)
                    ins.then_inc(s_hid, 1)

                def edge_features(g, slot):
                    pe.wait_ge(s_leaky, g + 1)
                    pe.wait_ge(s_feat, g + 1)
                    for half in range(2):
                        for pair in range(2):
                            t, at = 4 * half + 2 * pair, (2 * pair + half) * P
                            ins = pe.matmul(bank[4 + slot][:, t * D:(t + 2) * D], hidden[:, slot, at:at + P], w2,
                                            start=True, stop=True)
                    ins.then_inc(s_edge, 1)

                hidden_layer(0, 0, 0)
                hidden_layer(1, 0, 1)
                edge_features(0, 0)

                def body(g, i, u, ahead):
                    if ahead >= 2:
                        hidden_layer(g + 2, i + (u + 2) // U, (u + 2) % U)
                    if ahead >= 1:
                        edge_features(g + 1, (u + 1) % 2)
                    pe.wait_ge(s_msg, g + (U + 1))
                    sum_group(pe, g, u % 2, lambda t: message[:, u % 2, t, 0:D], D)

                each_group(pe, body)

        def transposed_bank(slot):
            return bank[4 + slot][0:3 * G * H, 0:P // 2].bitcast(BF16)

        def max_pass(block):
            @block.sync
            def _(sp):
                def keep(g, i, u):
                    sp.dma_start(of_group(spill, g), rows_buf[:, u, :, :].rearrange("p t w -> p (t w)")).then_inc(s_spill[u], 16)
                    sp.wait_ge(s_spill[u], (i + 1) * 16)

                index_loads(sp, src_idx, after_rows=keep)

            @block.gpsimd
            def _(pool):
                gather(pool, table0, lambda u, t: rows_buf[:, u, t, :],
                       lambda e, g, i, u: e.wait_ge(s_split, g * 5 + 5))

            @block.scalar
            def _(act):
                act.sem_inc(s_tr_sb, 2)

                def body(g, i, u, ahead):
                    act.wait_ge(s_tr, g + 3)
                    act.wait_ge(s_bc, g * 4 + (4 * U - 4))
                    act.activation(parts_t[:, u % 2, :], transposed_bank(u % 2), ACT.Copy).then_inc(s_tr_sb, 1)

                each_group(act, body)

            @block.vector
            def _(dve):
                dve.sem_inc(s_acc, 4)
                dve.sem_inc(s_red, 2)
                dve.sem_inc(s_split, 5 * U)
                open_windows(dve)

                def prepare(g, i, u):
                    slot = u % 2
                    make_onehot(dve, g, not_hot[:, slot, :, :], ALU.not_equal)
                    part = lambda n: parts[:, slot, n, :].rearrange("p (g h) -> p g h", h=H)
                    left = rest[:, slot, :, :]
                    a_src = rows_buf[:, u, :, D:D + H]
                    dve.wait_ge(s_rows[u], (i + 1) * (16 * G))
                    dve.wait_ge(s_tr, g + 1)
                    dve.tensor_copy(part(0), a_src).then_inc(s_split, 1)
                    dve.wait_ge(s_split, g * 5 + (5 * U + 1))
                    dve.tensor_tensor(left, a_src, part(0), ALU.subtract).then_inc(s_split, 1)
                    dve.wait_ge(s_split, g * 5 + (5 * U + 2))
                    dve.tensor_copy(part(1), left).then_inc(s_split, 1)
                    dve.wait_ge(s_split, g * 5 + (5 * U + 3))
                    dve.tensor_tensor(left, left, part(1), ALU.subtract).then_inc(s_split, 1)
                    dve.wait_ge(s_split, g * 5 + (5 * U + 4))
                    dve.tensor_copy(part(2), left).then_inc(s_split, 1)

                prepare(0, 0, 0)

                def body(g, i, u, ahead):
                    if ahead >= 1:
                        prepare(g + 1, i + (u + 1) // U, (u + 1) % U)
                    for k in range(4):
                        if k == 1:
                            b = block_of_group(dve, g)
                        dve.wait_ge(s_bc, g * 4 + (4 * U + k + 1))
                        dve.tensor_reduce(
                            out=red[:, 2 * k:2 * k + 2, :],
                            in_=banks[:, 2 * (k % 2):2 * (k % 2) + 2, :].rearrange("p b (h e) -> p b h e", h=H),
                            op=ALU.max, axis=AX.X).then_inc(s_red, 1)
                    dve.wait_ge(s_red, g * 4 + 6)
                    dve.wait_ge(s_acc, g * 2 + 4)
                    dve.tensor_reduce(out=red1[:, :], in_=red[:, :, :].rearrange("p g h -> p h g"),
                                      op=ALU.max, axis=AX.X).then_inc(s_group, 1)
                    dve.wait_ge(s_group, g + 1)
                    for n, side in enumerate((low_far, high_far)):
                        dve.wait_ge(s_acc, g * 2 + (4 + n))
                        to = head_max[:, bass.ds(b + n, 1), :].rearrange("p o w -> p (o w)")
                        dve.scalar_tensor_tensor(
                            out=to, in0=red1[:, :], scalar=side[:, bass.ds(g, 1)], in1=to,
                            op0=ALU.add, op1=ALU.max).then_inc(s_acc, 1)

                each_group(dve, body)
                dve.wait_ge(s_acc, 4 + 2 * NG)

            @block.tensor
            def _(pe):
                pe.sem_inc(s_bc, 4 * U)
                pe.sem_inc(s_tr, 2)

                def transpose_parts(g, slot):
                    pe.wait_ge(s_split, g * 5 + (5 * U + 5))
                    pe.wait_ge(s_tr_sb, g + 1)
                    pe.transpose(transposed_bank(slot), parts[:, slot, :, :].rearrange("p n a -> p (n a)"),
                                 ident_bf[:, :]).then_inc(s_tr, 1)

                transpose_parts(0, 0)

                def body(g, i, u, ahead):
                    slot = u % 2
                    pe.wait_ge(s_hot, g + 1)
                    pe.wait_ge(s_tr_sb, g + 3)
                    for k in range(4):
                        pe.wait_ge(s_red, g * 4 + (k + 1))
                        for t in (2 * k, 2 * k + 1):
                            to = bank[t % 4]
                            pe.matmul(to, not_hot[:, slot, t, :], far_ident[:, :, :].rearrange("p h e -> p (h e)"),
                                      start=True, stop=False)
                            for h in range(H):
                                ins = pe.matmul(to[:, h * P:(h + 1) * P],
                                                pick[:, t * H + h:t * H + h + 1].broadcast_to([3 * G * H, P]),
                                                parts_t[:, slot, :], start=False, stop=(h == H - 1))
                        ins.then_inc(s_bc, 1)
                    if ahead >= 1:
                        transpose_parts(g + 1, 1 - slot)

                each_group(pe, body)

        def attention_pass(block):
            @block.sync
            def _(sp):
                def body(g, i, u, ahead):
                    sp.wait_ge(s_msg, g + 1)
                    sp.dma_start(rows_buf[:, u, :, :].rearrange("p t w -> p (t w)"), of_group(spill, g)).then_inc(s_attr[u], 16)

                each_group(sp, body)

            @block.scalar
            def _(act):
                act.sem_inc(s_hot_t_sb, 2)

                def copy_hot(g, slot):
                    act.wait_ge(s_hot_t, g + 3)
                    act.wait_ge(s_dst, g + 1)
                    act.activation(onehots_t[:, slot, :, :].rearrange("p t e -> p (t e)"),
                                   bank[slot].bitcast(BF16), ACT.Copy).then_inc(s_hot_t_sb, 1)

                def weights(g, slot):
                    act.wait_ge(s_logit, g * 5 + 15)
                    act.wait_ge(s_sum, g + (U - 1))
                    act.activation(message[:, slot, :, D:D + H], logit[:, 3, :, :], ACT.Exp).then_inc(s_exp, 1)

                for g in range(3):
                    copy_hot(g, g % 2)
                    if g >= 1:
                        weights(g - 1, g - 1)

                def body(g, i, u, ahead):
                    if ahead >= 3:
                        copy_hot(g + 3, (u + 3) % 2)
                    if ahead >= 2:
                        weights(g + 2, u % 2)

                each_group(act, body)

            @block.vector
            def _(dve):
                dve.sem_inc(s_acc, 4)
                dve.sem_inc(s_msg, U)
                dve.sem_inc(s_logit, 10)
                open_windows(dve)

                def window_rows(g, slot, b, n):
                    to = window_dst[:, slot, :]
                    rows = dst_parts[:, bass.ds(b + n, 1), :, :].rearrange("p o h n -> p (o h n)")
                    if n == 0:
                        dve.tensor_scalar(to, rows, low[:, bass.ds(g, 1)], None, ALU.mult).then_inc(s_window, 1)
                    else:
                        dve.wait_ge(s_window, g * 2 + 1)
                        dve.scalar_tensor_tensor(out=to, in0=rows, scalar=high[:, bass.ds(g, 1)], in1=to,
                                                 op0=ALU.mult, op1=ALU.add).then_inc(s_window, 1)

                def logits(g, i, u, n):
                    if n == 0:
                        dve.wait_ge(s_dst, g + 3)
                        ins = dve.tensor_reduce(
                            out=dst_value[:, :, :], in_=bank[2 + u % 2][:, 0:G * 6 * H].rearrange("p (t h n) -> p t h n", h=2 * H, n=3),
                            op=ALU.add, axis=AX.X)
                    else:
                        dve.wait_ge(s_logit, g * 5 + (10 + n))
                    if n == 1:
                        dve.wait_ge(s_attr[u], (i + 1) * 16)
                        ins = dve.tensor_tensor(logit[:, 0, :, :], rows_buf[:, u, :, D:D + H], dst_value[:, :, 0:H], ALU.add)
                    elif n == 2:
                        ins = dve.scalar_tensor_tensor(out=logit[:, 1, :, :], in0=logit[:, 0, :, :], scalar=0.2,
                                                       in1=logit[:, 0, :, :], op0=ALU.mult, op1=ALU.max)
                    elif n == 3:
                        ins = dve.tensor_tensor(logit[:, 2, :, :], logit[:, 1, :, :], dst_value[:, :, H:2 * H], ALU.subtract)
                    elif n == 4:
                        ins = dve.tensor_scalar(logit[:, 3, :, :], logit[:, 2, :, :], 0.0, None, ALU.min)
                    ins.then_inc(s_logit, 1)

                def messages(g, u):
                    dve.wait_ge(s_exp, g + 1)
                    dve.tensor_tensor(
                        message[:, u % 2, :, 0:D].rearrange("p t (h c) -> p t h c", h=H),
                        rows_buf[:, u, :, 0:D].rearrange("p t (h c) -> p t h c", h=H),
                        message[:, u % 2, :, D:D + H].unsqueeze(3).broadcast_to([P, G, H, DH]),
                        ALU.mult).then_inc(s_msg, 1)

                for g in range(3):
                    make_onehot(dve, g, onehots[:, g, :, :])
                    b = block_of_group(dve, g)
                    for n in range(2):
                        window_rows(g, g % 2, b, n)
                    if g >= 1:
                        for n in range(5):
                            logits(g - 1, 0, g - 1, n)
                    if g == 1:
                        messages(0, 0)

                def body(g, i, u, ahead):
                    if ahead >= 3:
                        make_onehot(dve, g + 3, onehots[:, (u + 3) % U, :, :])
                        b_ahead = block_of_group(dve, g + 3)
                    b = block_of_group(dve, g)
                    if ahead >= 1:
                        messages(g + 1, (u + 1) % U)
                    next_i, next_u = i + (u + 2) // U, (u + 2) % U
                    for n in range(5):
                        if ahead >= 2:
                            logits(g + 2, next_i, next_u, n)
                        if n in (0, 2) and ahead >= 3:
                            window_rows(g + 3, (u + 3) % 2, b_ahead, n // 2)
                        if n in (1, 3):
                            add_side(dve, g, b, u % 2, ACCW, n // 2)

                each_group(dve, body)
                dve.wait_ge(s_acc, 4 + 2 * NG)

            @block.tensor
            def _(pe):
                pe.sem_inc(s_sum, U)
                pe.sem_inc(s_hot_t, 2)
                pe.sem_inc(s_dst, 2)

                def transpose_hot(g, slot, hot):
                    pe.wait_ge(s_hot, g + 1)
                    pe.wait_ge(s_hot_t_sb, g + 1)
                    upper = hot.rearrange("p t e -> p (t e)").bitcast(BF16).rearrange("p (t e two) -> p t e two", t=G, two=2)
                    for t in range(G):
                        ins = pe.transpose(bank[slot].bitcast(BF16)[:, t * P:(t + 1) * P], upper[:, t, :, 1], ident_bf[:, :])
                    ins.then_inc(s_hot_t, 1)

                def destinations(g, slot):
                    pe.wait_ge(s_hot_t_sb, g + 3)
                    pe.wait_ge(s_window, g * 2 + 2)
                    pe.wait_ge(s_logit, g * 5 + 1)
                    for t in range(G):
                        ins = pe.matmul(bank[2 + slot][:, t * 6 * H:(t + 1) * 6 * H], onehots_t[:, slot, t, :],
                                        window_dst[:, slot, :], start=True, stop=True)
                    ins.then_inc(s_dst, 1)

                def sums(g, u):
                    pe.wait_ge(s_msg, g + (U + 1))
                    sum_group(pe, g, u % 2, lambda t: message[:, u % 2, t, :], ACCW, onehots[:, u, :, :])

                for g in range(3):
                    transpose_hot(g, g % 2, onehots[:, g, :, :])
                    destinations(g, g % 2)
                sums(0, 0)

                def body(g, i, u, ahead):
                    if ahead >= 3:
                        transpose_hot(g + 3, (u + 3) % 2, onehots[:, (u + 3) % U, :, :])
                    if ahead >= 1:
                        sums(g + 1, (u + 1) % U)
                    if ahead >= 3:
                        destinations(g + 3, (u + 3) % 2)

                each_group(pe, body)

        def each_chunk_pair(engine, body):
            with engine.Fori(0, L.chunks // 2) as i:
                body(i)

        def bring_chunks(block, x):
            @block.gpsimd
            def _(pool):
                def body(i):
                    for slot in range(2):
                        c = i * 2 + slot
                        pool.wait_ge(s_chunk_t, c + 1)
                        pool.sem_inc(s_turn, 1)
                        pool.tensor_copy(node_x[:, slot, :, :], x[:, bass.ds(c * C, C), :]).then_inc(s_chunk_x, 1)

                each_chunk_pair(pool, body)

        def transpose_chunk(pe, c, slot):
            pe.wait_ge(s_chunk_x, c + 1)
            pe.wait_ge(s_chunk_tc, c + 1)
            for j in range(C // 2):
                ins = pe.transpose(bank[slot][:, j * P:(j + 1) * P],
                                   node_x[:, slot, 2 * j:2 * j + 2, :].rearrange("p b d -> p (b d)"), ident[:, :])
            ins.then_inc(s_chunk_t, 1)

        def copy_transposed(act, c, slot, s_used):
            act.wait_ge(s_chunk_t, c + 3)
            act.wait_ge(s_used, c + 1)
            act.activation(node_t[:, slot, :, :].rearrange("p j n -> p (j n)"), bank[slot][:, 0:C // 2 * P],
                           ACT.Copy).then_inc(s_chunk_tc, 1)

        def project(block, x, w):
            bring_chunks(block, x)

            @block.tensor
            def _(pe):
                pe.sem_inc(s_chunk_t, 2)
                pe.sem_inc(s_chunk_m, 2)
                pe.wait_ge(s_load, 16)

                def body(i):
                    for slot in range(2):
                        transpose_chunk(pe, i * 2 + slot, slot)
                    for slot in range(2):
                        c = i * 2 + slot
                        pe.wait_ge(s_chunk_tc, c + 3)
                        pe.wait_ge(s_chunk_o, c + 1)
                        for j in range(C // 2):
                            ins = pe.matmul(bank[4 + slot][:, j * 2 * D:(j + 1) * 2 * D], node_t[:, slot, j, :],
                                            w, start=True, stop=True)
                        ins.then_inc(s_chunk_m, 1)

                each_chunk_pair(pe, body)

        def project_copies(act):
            act.sem_inc(s_chunk_tc, 2)

            def body(i):
                for slot in range(2):
                    copy_transposed(act, i * 2 + slot, slot, s_chunk_m)

            each_chunk_pair(act, body)

        def take_products(dve, to, op):
            dve.sem_inc(s_chunk_o, 2)

            def body(i):
                for slot in range(2):
                    c = i * 2 + slot
                    dve.wait_ge(s_chunk_m, c + 3)
                    op(to[:, bass.ds(c * C, C), 0:D], bank[4 + slot][:, 0:C * D].rearrange("p (b d) -> p b d", d=D),
                       bass.ds(c * C, C)).then_inc(s_chunk_o, 1)

            each_chunk_pair(dve, body)
            dve.wait_ge(s_chunk_o, 2 + L.chunks)

        def layer_norm(dve, then, n, x, to, gamma=None, beta=None):
            then(dve.tensor_reduce(out=stat[:, 0, :], in_=x, op=ALU.add, axis=AX.X))
            then(dve.tensor_scalar(stat[:, 0, :], stat[:, 0, :], 1.0 / D, None, ALU.mult))
            then(dve.tensor_tensor(tmp[:, :, :], x, over_row(stat[:, 0, :]), ALU.subtract))
            then(dve.tensor_tensor(whole(stage), tmp[:, :, :], tmp[:, :, :], ALU.mult))
            then(dve.tensor_reduce(out=stat[:, 1, :], in_=whole(stage), op=ALU.add, axis=AX.X))
            dve.tensor_scalar(stat[:, 1, :], stat[:, 1, :], 1.0 / D, 1e-5, ALU.mult, ALU.add).then_inc(s_var, 1)
            dve.wait_ge(s_std, n + 1)
            then(dve.reciprocal(stat[:, 2, :], stat[:, 2, :]))
            then(dve.tensor_tensor(to, tmp[:, :, :], over_row(stat[:, 2, :]), ALU.mult))
            if gamma is not None:
                then(dve.tensor_tensor(to, to, over_blocks(gamma), ALU.mult))
                then(dve.tensor_tensor(to, to, over_blocks(beta), ALU.add))

        def layer_norm_root(act, n):
            act.wait_ge(s_var, n + 1)
            act.activation(stat[:, 2, :], stat[:, 1, :], ACT.Sqrt).then_inc(s_std, 1)

        def chain(dve):
            d = Steps(s_dve)

            def then(instruction):
                d.add(instruction)
                dve.wait_ge(s_dve, d.count)

            return then

        def store_table(sp, to, source):
            sp.wait_ge(s_ready, 1)
            sp.dma_start(rows_of(to), source).then_inc(s_store, 16)
            sp.wait_ge(s_store, 16)

        with nc.Block() as block:
            w0 = COLS["l0"](params0, "W")
            project(block, x_outer, w0)

            @block.sync
            def _(sp):
                sp.dma_start(params0, l0_params).then_inc(s_load, 16)
                store_table(sp, table0, stage[:, :, :])

            @block.scalar
            def _(act):
                project_copies(act)

            @block.vector
            def _(dve):
                then = chain(dve)
                take_products(dve, stage, lambda o, i, b: dve.tensor_copy(o, i))
                for name, to in (("att_dst", dst_rows[:, :, 0:H]), ("att_src", stage[:, :, D:D + H])):
                    then(dve.tensor_tensor(tmp[:, :, :], whole(stage), over_blocks(COLS["l0"](params0, name)), ALU.mult))
                    then(dve.tensor_reduce(out=to, in_=tmp[:, :, :].rearrange("p b (h c) -> p b h c", h=H),
                                           op=ALU.add, axis=AX.X))
                dve.sem_inc(s_ready, 1)
                then(dve.tensor_copy(head_max[:, :, :], stage[:, :, D:D + H]))
                then(dve.memset(window[:, :], 0.0))
        stage_end()

        run_windows(max_pass)

        with nc.Block() as block:
            @block.scalar
            def _(act):
                act.wait_ge(s_var, 1)
                act.activation(self_weight[:, :, :], self_weight[:, :, :], ACT.Exp).then_inc(s_std, 1)
                act.wait_ge(s_std, 1)

            @block.vector
            def _(dve):
                then = chain(dve)
                for source, to in ((head_max[:, :, :], dst_rows[:, :, H:2 * H]),
                                   (stage[:, :, D:D + H], self_weight[:, :, :])):
                    then(dve.tensor_tensor(to, source, dst_rows[:, :, 0:H], ALU.add))
                    then(dve.scalar_tensor_tensor(out=to, in0=to, scalar=0.2, in1=to, op0=ALU.mult, op1=ALU.max))
                dve.tensor_tensor(self_weight[:, :, :], self_weight[:, :, :], dst_rows[:, :, H:2 * H], ALU.subtract).then_inc(s_var, 1)
                left = tmp[:, :, 0:2 * H]
                then(dve.tensor_copy(dst_parts[:, :, :, 0], dst_rows[:, :, :]))
                then(dve.tensor_tensor(left, dst_rows[:, :, :], dst_parts[:, :, :, 0], ALU.subtract))
                then(dve.tensor_copy(dst_parts[:, :, :, 1], left))
                then(dve.tensor_tensor(left, left, dst_parts[:, :, :, 1], ALU.subtract))
                then(dve.tensor_copy(dst_parts[:, :, :, 2], left))
                then(dve.memset(acc[:, :, :], 0.0))
                then(dve.memset(message[:, :, :, D + H:ACCW], 1.0))
                then(dve.memset(window[:, :], 0.0))
        stage_end()

        run_windows(attention_pass)

        with nc.Block() as block:
            @block.scalar
            def _(act):
                act.wait_ge(s_var, 1)
                act.activation(dinv[:, :], dinv[:, :], ACT.Sqrt).then_inc(s_std, 1)
                layer_norm_root(act, 1)
                layer_norm_root(act, 2)

            @block.vector
            def _(dve):
                then = chain(dve)
                then(dve.tensor_copy(count[:, :], acc[:, :, D + H]))
                dve.tensor_scalar(dinv[:, :], count[:, :], 1.0, None, ALU.add).then_inc(s_var, 1)
                by_head = lambda t: t.rearrange("p b (h c) -> p (b h) c", h=H)
                weight = self_weight[:, :, :].rearrange("p b h -> p (b h)").unsqueeze(2).broadcast_to([P, B * H, DH])
                for h in range(H):
                    cols = slice(h * DH, (h + 1) * DH)
                    then(dve.tensor_tensor(tmp[:, :, cols], stage[:, :, cols], over_row(self_weight[:, :, h], DH), ALU.mult))
                then(dve.tensor_tensor(whole(acc), whole(acc), tmp[:, :, :], ALU.add))
                then(dve.tensor_tensor(self_weight[:, :, :], self_weight[:, :, :], acc[:, :, D:D + H], ALU.add))
                then(dve.tensor_scalar(self_weight[:, :, :], self_weight[:, :, :], 1e-16, None, ALU.add))
                then(dve.reciprocal(self_weight[:, :, :], self_weight[:, :, :]))
                for h in range(H):
                    cols = slice(h * DH, (h + 1) * DH)
                    then(dve.tensor_tensor(tmp[:, :, cols], acc[:, :, cols], over_row(self_weight[:, :, h], DH), ALU.mult))
                then(dve.tensor_tensor(x_inner[:, :, :], tmp[:, :, :], over_blocks(COLS["l0"](params0, "bias")), ALU.add))
                then(dve.tensor_tensor(x_inner[:, :, :], x_inner[:, :, :], x_outer[:, :, :], ALU.add))
                layer_norm(dve, then, 1, x_inner[:, :, :], x_inner[:, :, :],
                           COLS["l0"](params0, "gamma"), COLS["l0"](params0, "beta"))
                then(dve.tensor_tensor(x_inner[:, :, :], x_inner[:, :, :], x_outer[:, :, :], ALU.add))
                layer_norm(dve, then, 2, x_inner[:, :, :], x_outer[:, :, :])
                then(dve.reciprocal(dinv[:, :], dinv[:, :]))
                then(dve.tensor_copy(x_inner[:, :, :], x_outer[:, :, :]))
        stage_end()

        with nc.Fori(0, l1_layers) as layer:
            with nc.Block() as block:
                project(block, x_inner, COLS["l1"](params, "W"))

                @block.sync
                def _(sp):
                    sp.dma_start(params1, of_group(l1_params, layer)).then_inc(s_load, 16)
                    store_table(sp, table, whole(stage))

                @block.scalar
                def _(act):
                    project_copies(act)

                @block.vector
                def _(dve):
                    then = chain(dve)
                    take_products(dve, stage, lambda o, i, b: dve.tensor_tensor(
                        o, i, over_row(dinv[:, b], D, C), ALU.mult))
                    dve.sem_inc(s_ready, 1)
                    then(dve.memset(acc[:, :, :], 0.0))
                    then(dve.memset(window[:, :], 0.0))
            stage_end()

            run_windows(sum_pass)

            with nc.Block() as block:
                @block.vector
                def _(dve):
                    then = chain(dve)
                    then(dve.tensor_tensor(whole(acc), whole(acc), whole(stage), ALU.add))
                    then(dve.tensor_tensor(whole(acc), whole(acc), over_row(dinv[:, :]), ALU.mult))
                    then(dve.tensor_tensor(whole(acc), whole(acc), over_blocks(COLS["l1"](params, "b")), ALU.add))
                    then(dve.tensor_scalar(x_inner[:, :, :], whole(acc), 0.0, None, ALU.max))
            stage_end()

        with nc.Block() as block:
            project(block, x_inner, COLS["l1"](params, "W"))

            @block.sync
            def _(sp):
                sp.dma_start(params1, of_group(l1_params, l1_layers)).then_inc(s_load, 16)

            @block.scalar
            def _(act):
                project_copies(act)
                layer_norm_root(act, 0)

            @block.vector
            def _(dve):
                then = chain(dve)
                dve.wait_ge(s_load, 16)
                take_products(dve, acc, lambda o, i, b: dve.tensor_tensor(
                    o, i, over_blocks(COLS["l1"](params, "b"), D, C), ALU.add))
                then(dve.tensor_tensor(whole(acc), whole(acc), x_outer[:, :, :], ALU.add))
                layer_norm(dve, then, 0, whole(acc), x_outer[:, :, :])
                then(dve.tensor_copy(x_inner[:, :, :], x_outer[:, :, :]))
        stage_end()

        p2 = lambda name: COLS["l2"](params, name)
        with nc.Fori(0, l2_layers) as layer:
            with nc.Block() as block:
                @block.sync
                def _(sp):
                    sp.dma_start(params[:, :], of_group(l2_params, layer)).then_inc(s_load, 16)
                    store_table(sp, table, whole(stage))

                @block.scalar
                def _(act):
                    act.sem_inc(s_chunk_tc, 2)
                    act.sem_inc(s_chunk_b, 2)
                    act.wait_ge(s_load, 16)

                    def body(i):
                        for slot in range(2):
                            copy_transposed(act, i * 2 + slot, slot, s_chunk_h)
                        for slot in range(2):
                            c = i * 2 + slot
                            act.wait_ge(s_chunk_h, c + 3)
                            act.wait_ge(s_chunk_m, c + 1)
                            act.activation(hidden[:, slot, :], bank[2 + slot], ACT.Identity, bias=p2("b1")).then_inc(s_chunk_b, 1)

                    each_chunk_pair(act, body)

                bring_chunks(block, x_inner)

                @block.tensor
                def _(pe):
                    pe.sem_inc(s_chunk_t, 2)
                    pe.wait_ge(s_load, 16)
                    pe.sem_inc(s_chunk_h, 2)
                    pe.sem_inc(s_chunk_m, 2)

                    def body(i):
                        for slot in range(2):
                            transpose_chunk(pe, i * 2 + slot, slot)
                        for slot in range(2):
                            c = i * 2 + slot
                            pe.wait_ge(s_chunk_tc, c + 3)
                            pe.wait_ge(s_chunk_b, c + 1)
                            for n in range(C):
                                ins = pe.matmul(bank[2 + slot][:, n * P:(n + 1) * P], p2("W1")[:, n % 2 * P:(n % 2 + 1) * P],
                                                node_t[:, slot, n // 2, :], start=True, stop=True)
                            ins.then_inc(s_chunk_h, 1)
                        for slot in range(2):
                            c = i * 2 + slot
                            pe.wait_ge(s_chunk_l, c + 1)
                            pe.wait_ge(s_chunk_o, c + 1)
                            for n in range(C):
                                ins = pe.matmul(bank[6 + slot][:, n * D:(n + 1) * D],
                                                hidden[:, slot, n * P:(n + 1) * P], p2("W2"), start=True, stop=True)
                            ins.then_inc(s_chunk_m, 1)

                    each_chunk_pair(pe, body)

                @block.vector
                def _(dve):
                    then = chain(dve)
                    dve.sem_inc(s_chunk_o, 2)
                    dve.wait_ge(s_load, 16)

                    def body(i):
                        for slot in range(2):
                            c = i * 2 + slot
                            dve.wait_ge(s_chunk_b, c + 3)
                            dve.scalar_tensor_tensor(
                                out=hidden[:, slot, :], in0=hidden[:, slot, :], scalar=0.1,
                                in1=hidden[:, slot, :], op0=ALU.mult, op1=ALU.max).then_inc(s_chunk_l, 1)
                        for slot in range(2):
                            c = i * 2 + slot
                            dve.wait_ge(s_chunk_m, c + 3)
                            dve.tensor_tensor(
                                stage[:, bass.ds(c * C, C), 0:D], bank[6 + slot][:, 0:C * D].rearrange("p (b d) -> p b d", d=D),
                                over_blocks(p2("b2"), D, C), ALU.add).then_inc(s_chunk_o, 1)

                    each_chunk_pair(dve, body)
                    dve.wait_ge(s_chunk_o, 2 + L.chunks)
                    dve.sem_inc(s_ready, 1)
                    then(dve.memset(acc[:, :, :], 0.0))
                    then(dve.memset(window[:, :], 0.0))
            stage_end()

            run_windows(edge_mlp_pass)

            with nc.Block() as block:
                @block.scalar
                def _(act):
                    layer_norm_root(act, 0)

                @block.vector
                def _(dve):
                    then = chain(dve)
                    then(dve.tensor_scalar(whole(acc), whole(acc), p2("dot_scale"), p2("res_w"), ALU.mult, ALU.mult))
                    then(dve.tensor_tensor(x_inner[:, :, :], x_inner[:, :, :], whole(acc), ALU.add))
                    layer_norm(dve, then, 0, x_inner[:, :, :], x_inner[:, :, :], p2("ln_g"), p2("ln_b"))
            stage_end()

        with nc.Block() as block:
            @block.sync
            def _(sp):
                store_table(sp, table, x_outer[:, :, :])

            @block.scalar
            def _(act):
                layer_norm_root(act, 0)

            @block.vector
            def _(dve):
                then = chain(dve)
                then(dve.tensor_tensor(x_inner[:, :, :], x_inner[:, :, :], x_outer[:, :, :], ALU.add))
                layer_norm(dve, then, 0, x_inner[:, :, :], x_outer[:, :, :])
                dve.sem_inc(s_ready, 1)
                then(dve.memset(acc[:, :, :], 0.0))
                then(dve.memset(window[:, :], 0.0))
                then(dve.tensor_scalar(count[:, :], count[:, :], 1.0, None, ALU.max))
                then(dve.reciprocal(count[:, :], count[:, :]))
        stage_end()

        run_windows(sum_pass)

        with nc.Block() as block:
            @block.vector
            def _(dve):
                then = chain(dve)
                then(dve.tensor_tensor(x_inner[:, :, :], whole(acc), over_row(count[:, :]), ALU.mult))
        stage_end()

        with nc.Block() as block:
            p3 = lambda name: COLS["l3"](params3, name)
            w3 = p3("W")

            project(block, x_inner, w3)

            @block.sync
            def _(sp):
                sp.dma_start(params3, l3_params).then_inc(s_load, 16)

            @block.scalar
            def _(act):
                project_copies(act)
                act.wait_ge(s_var, 1)
                act.activation(tmp[:, :, :], tmp[:, :, :], ACT.Exp).then_inc(s_std, 1)

            @block.vector
            def _(dve):
                then = chain(dve)
                take_products(dve, acc, lambda o, i, b: dve.tensor_copy(o, i))
                dve.tensor_scalar(tmp[:, :, :], whole(acc), 0.0, None, ALU.min).then_inc(s_var, 1)
                then(dve.tensor_scalar(whole(acc), whole(acc), 0.0, -1.0, ALU.max, ALU.add))
                dve.wait_ge(s_std, 1)
                then(dve.tensor_tensor(whole(acc), whole(acc), tmp[:, :, :], ALU.add))
                then(dve.tensor_tensor(whole(acc), whole(acc), over_row(valid[:, :]), ALU.mult))
                then(dve.tensor_reduce(out=over_nodes[:, 0, :], in_=whole(acc).rearrange("p b d -> p d b"), op=ALU.add, axis=AX.X))
        stage_end()

        with nc.Block() as block:
            @block.tensor
            def _(pe):
                pe.matmul(bank[0][:, 0:D], ones[:, :], over_nodes[:, 0, :], start=True, stop=True).then_inc(s_pe, 1)
                pe.wait_ge(s_ready, 1)
                pe.matmul(bank[0][:, D:2 * D], ones[:, :], over_nodes[:, 2, :], start=True, stop=True).then_inc(s_pe, 1)

            @block.scalar
            def _(act):
                act.wait_ge(s_var, 1)
                act.activation(over_nodes[:, 3, :], over_nodes[:, 3, :], ACT.Sqrt).then_inc(s_std, 1)
                layer_norm_root(act, 1)

            @block.vector
            def _(dve):
                then = chain(dve)
                mean, squares, scale = (over_nodes[:, n, :] for n in (1, 2, 3))
                dve.wait_ge(s_pe, 1)
                then(dve.tensor_scalar(mean, bank[0][:, 0:D], 1.0 / L.nodes, None, ALU.mult))
                then(dve.tensor_tensor(whole(acc), whole(acc), over_blocks(mean), ALU.subtract))
                then(dve.tensor_tensor(tmp[:, :, :], whole(acc), whole(acc), ALU.mult))
                then(dve.tensor_tensor(tmp[:, :, :], tmp[:, :, :], over_row(valid[:, :]), ALU.mult))
                then(dve.tensor_reduce(out=squares, in_=tmp[:, :, :].rearrange("p b d -> p d b"), op=ALU.add, axis=AX.X))
                dve.sem_inc(s_ready, 1)
                dve.wait_ge(s_pe, 2)
                dve.tensor_scalar(scale, bank[0][:, D:2 * D], 1.0 / L.nodes, 1e-5, ALU.mult, ALU.add).then_inc(s_var, 1)
                dve.wait_ge(s_std, 1)
                then(dve.reciprocal(scale, scale))
                then(dve.tensor_tensor(scale, scale, p3("gamma"), ALU.mult))
                then(dve.tensor_tensor(whole(acc), whole(acc), over_blocks(scale), ALU.mult))
                then(dve.tensor_tensor(whole(acc), whole(acc), over_blocks(p3("beta")), ALU.add))
                then(dve.tensor_tensor(whole(acc), whole(acc), x_outer[:, :, :], ALU.add))
                layer_norm(dve, then, 1, whole(acc), x_outer[:, :, :])
                dve.sem_inc(s_turn, 1)

            @block.sync
            def _(sp):
                sp.wait_ge(s_turn, 1)
                full = L.nodes // P
                stores = 0
                if full:
                    sp.dma_start(rows_of(out[0:full * P, :]), x_outer[:, 0:full, :]).then_inc(s_store, 16)
                    stores += 1
                if L.nodes % P:
                    sp.dma_start(out[full * P:L.nodes, :], x_outer[0:L.nodes % P, full, :]).then_inc(s_store, 16)
                    stores += 1
                sp.wait_ge(s_store, 16 * stores)
    return nc


def kernel(x, src, dst, edge_attr_32, **w):
    import numpy as np
    import concourse.bacc as bacc
    from concourse.bass_utils import run_bass_kernel_spmd

    x, attr = np.asarray(x), np.asarray(edge_attr_32)
    nodes, dim = x.shape
    edges, edge_dim = attr.shape
    w = {k: np.asarray(v) for k, v in w.items()}
    heads = w["L0_gnn_att_src"].shape[0]
    L = Layout(nodes, edges, dim, heads, edge_dim)
    cols = param_columns(dim)

    def padded(a, n):
        return np.concatenate([a, np.broadcast_to(a[-1:], (n - a.shape[0],) + a.shape[1:])])

    def rows(v):
        return np.broadcast_to(np.reshape(v, (1, -1)), (P, np.size(v)))

    def stacked(m):
        return np.tile(m, (P // m.shape[0], 1))

    def diagonal(m, times):
        out = np.zeros((times, m.shape[0], times, m.shape[1]), m.dtype)
        for n in range(times):
            out[n, :, n, :] = m
        return out.reshape(times * m.shape[0], times * m.shape[1])

    def pair_columns(m):
        pair = diagonal(m, 2)
        none = np.zeros_like(pair)
        return np.block([[pair, none], [none, pair]])

    def packed(layer, **named):
        return np.ascontiguousarray(np.concatenate([named[n] for n in cols[layer].at], axis=1))

    src_p = padded(np.asarray(src).astype(np.int32), L.tiles * P)
    dst_p = padded(np.asarray(dst).astype(np.int32), L.tiles * P)

    def by_group(idx):
        return np.ascontiguousarray(idx.reshape(L.groups, G, P).transpose(0, 2, 1))

    attr_p = np.zeros((L.tiles * P, edge_dim), attr.dtype)
    attr_p[:edges] = attr
    attr_p = attr_p.reshape(L.groups, G // 4, 4, P, edge_dim).transpose(0, 2, 4, 1, 3)
    x_p = np.zeros((L.blocks * P, dim), x.dtype)
    x_p[:nodes] = x
    l1_w = list(w["L1_gnn_Ws"]) + [w["L1_gnn_W_out"]]
    l1_b = list(w["L1_gnn_bs"]) + [w["L1_gnn_b_out"]]
    l2 = {k[7:]: v for k, v in w.items() if k.startswith("L2_gnn_")}
    arrays = {
        "src_idx": by_group(src_p),
        "dst_tiles": np.ascontiguousarray(dst_p.reshape(L.tiles, P).T),
        "dst_groups": dst_p.reshape(L.groups, G * P),
        "x": x_p,
        "attr": np.ascontiguousarray(attr_p).reshape(L.groups, P, G // 4 * P),
        "l0_params": packed("l0", W=diagonal(w["L0_gnn_W"], 2), att_src=rows(w["L0_gnn_att_src"]),
                            att_dst=rows(w["L0_gnn_att_dst"]), bias=rows(w["L0_gnn_bias"]),
                            gamma=rows(w["L0_gnn_gamma"]), beta=rows(w["L0_gnn_beta"])),
        "l1_params": np.stack([packed("l1", W=diagonal(a, 2), b=rows(b)) for a, b in zip(l1_w, l1_b)]),
        "l2_params": np.stack([
            packed("l2", W1=diagonal(l2["W1"][n], 2), b1=l2["b1"][n][:, None], W2=l2["W2"][n], b2=rows(l2["b2"][n]),
                   We1=pair_columns(l2["We1"][n]), be1=stacked(l2["be1"][n][:, None]),
                   We2=diagonal(l2["We2"][n], 2), be2=rows(l2["be2"][n]), res_w=rows(l2["res_w"][n]),
                   dot_scale=rows(l2["dot_scale"][n]), ln_g=rows(l2["ln_g"][n]), ln_b=rows(l2["ln_b"][n]))
            for n in range(l2["W1"].shape[0])]),
        "l3_params": packed("l3", W=diagonal(w["L3_gnn_W"], 2), gamma=rows(w["L3_gnn_gamma"]), beta=rows(w["L3_gnn_beta"])),
    }
    nc = bacc.Bacc("TRN2", target_bir_lowering=False, num_devices=1)
    t = {k: nc.dram_tensor(k, a.shape, mybir.dt.from_np(a.dtype), kind="ExternalInput").ap() for k, a in arrays.items()}
    out = nc.dram_tensor("out", (nodes, dim), F32, kind="ExternalOutput").ap()
    build(nc, L, t["src_idx"], t["dst_tiles"], t["dst_groups"], t["x"], t["attr"], t["l0_params"],
          t["l1_params"], t["l2_params"], t["l3_params"], len(w["L1_gnn_Ws"]), len(l2["W1"]), out)
    r = run_bass_kernel_spmd(nc, [arrays], core_ids=[0])
    return r.results[0]["out"]
```

```python
import concourse.bass as bass
from concourse import mybir
from contextlib import ExitStack

F32 = mybir.dt.float32
BF16 = mybir.dt.bfloat16
I32 = mybir.dt.int32
ALU = mybir.AluOpType
ACT = mybir.ActivationFunctionType
AX = mybir.AxisListType

P = 128
G = 8
U = 4
C = 4
FAR = 2.0 ** 100


class Layout:

    def __init__(self, nodes, edges, dim, heads, edge_dim):
        self.nodes, self.edges, self.dim, self.heads, self.edge_dim = nodes, edges, dim, heads, edge_dim
        self.groups = -(-edges // (P * G * U)) * U
        self.tiles = self.groups * G
        self.blocks_used = -(-nodes // P)
        self.blocks = -(-(self.blocks_used + 1) // (2 * C)) * 2 * C
        self.chunks = self.blocks // C
        self.group_rows = -(-self.groups // P)
        while self.groups % self.group_rows:
            self.group_rows += 1


class Params:

    def __init__(self, *columns):
        self.at, self.width = {}, 0
        for name, width in columns:
            self.at[name] = (self.width, self.width + width)
            self.width += width

    def __call__(self, tensor, name):
        a, b = self.at[name]
        return tensor[:, a:b]


def param_columns(dim):
    return {
        "l0": Params(("W", 2 * dim), ("att_src", dim), ("att_dst", dim), ("bias", dim), ("gamma", dim),
                     ("beta", dim)),
        "l1": Params(("W", 2 * dim), ("b", dim)),
        "l2": Params(("W1", 4 * dim), ("b1", 1), ("W2", dim), ("b2", dim), ("We1", 4 * dim),
                     ("be1", 1), ("We2", 2 * dim), ("be2", dim), ("res_w", 1), ("dot_scale", 1),
                     ("ln_g", dim), ("ln_b", dim)),
        "l3": Params(("W", 2 * dim), ("gamma", dim), ("beta", dim)),
    }


class Steps:

    def __init__(self, semaphore):
        self.semaphore, self.count = semaphore, 0

    def add(self, instruction):
        instruction.then_inc(self.semaphore, 1)
        self.count += 1


def build(nc, L, src_idx, dst_tiles, dst_groups, x_in, attr, l0_params, l1_params, l2_params,
          l3_params, l1_layers, l2_layers, out):
    D, H, DH = L.dim, L.heads, L.dim // L.heads
    B, NG, NT = L.blocks, L.groups, L.tiles
    ITER = NG // U
    COLS = param_columns(D)
    ROW0 = D + H
    ACCW = D + H + 1
    ctx = ExitStack()
    with ctx:
        def sb(name, shape, dt):
            return ctx.enter_context(nc.sbuf_tensor(name, shape, dt))

        def ps(name, shape, dt):
            return ctx.enter_context(nc.psum_tensor(name, shape, dt))

        semaphores = []

        def sem(name):
            s = ctx.enter_context(nc.semaphore(name))
            semaphores.append(s)
            return s

        def scratch(name, shape, dt):
            return nc.dram_tensor(name, shape, dt, kind="Internal").ap()

        table0 = scratch("attention_table", (B * P, ROW0), F32)
        table = scratch("feature_table", (B * P, D), F32)
        spill = scratch("gathered_rows", (NG, P, G * ROW0), F32)
        group_min = scratch("group_min", (NG, 1), I32)
        group_max = scratch("group_max", (NG, 1), I32)

        ident = sb("ident", [P, P], F32)
        ident_bf = sb("ident_bf", [P, P], BF16)
        iota1 = sb("iota1", [P, P], F32)
        iota_p = sb("iota_p", [P, 1], F32)
        ones = sb("ones", [P, P], F32)
        far_ident = sb("far_ident", [P, H, P], BF16)
        assert B <= 256
        block_of = sb("block_of", [P, NT], BF16)
        place_of = sb("place_of", [P, NT], BF16)
        key = sb("key", [P, NT], F32)
        base_place = sb("base_place", [P, NG], F32)
        near_block = sb("near_block", [1, NG], F32)
        low = sb("low", [P, NG], F32)
        high = sb("high", [P, NG], F32)
        low_far = sb("low_far", [P, NG], F32)
        high_far = sb("high_far", [P, NG], F32)
        pass_block = sb("pass_block", [1, NG], I32)
        scattered = sb("scattered", [P, 1], F32)
        gathered_near = sb("gathered_near", [P, 1], F32)
        window = sb("window", [P, 1], F32)
        windows = sb("windows", [1, 1], I32)
        valid = sb("valid", [P, B], F32)
        count = sb("count", [P, B], F32)
        dinv = sb("dinv", [P, B], F32)
        stat = sb("stat", [P, 3, B], F32)
        x_outer = sb("x_outer", [P, B, D], F32)
        x_inner = sb("x_inner", [P, B, D], F32)
        acc = sb("acc", [P, B, ACCW], F32)
        stage = sb("stage", [P, B, ROW0], F32)
        tmp_flat = sb("tmp", [P, max(B * D, 5 * G * P)], F32)
        tmp = tmp_flat[:, 0:B * D].rearrange("p (b d) -> p b d", d=D)
        onehots = tmp_flat[:, 0:4 * G * P].rearrange("p (s t e) -> p s t e", s=4, t=G)
        onehots_t = tmp_flat[:, 4 * G * P:5 * G * P].bitcast(BF16).rearrange("p (s t e) -> p s t e", s=2, t=G)
        dst_parts = x_inner[:, :, 0:3 * H].bitcast(BF16).rearrange("p b (h n) -> p b h n", n=3)
        head_max = sb("head_max", [P, B, H], F32)
        dst_rows = sb("dst_rows", [P, B, 2 * H], F32)
        self_weight = sb("self_weight", [P, B, H], F32)

        idx_buf = sb("idx_buf", [P, U, G], I32)
        rows_buf = sb("rows_buf", [P, U, G, ROW0], F32)
        onehot = sb("onehot", [P, 2, G, P], F32)
        not_hot = onehot[:, 0, :, :].rearrange("p g e -> p (g e)").bitcast(BF16).rearrange("p (s g e) -> p s g e", s=2, g=G)
        attr_buf = sb("attr_buf", [P, U, G // 4, P], F32)
        hidden = sb("hidden", [P, 2, 4 * P], F32)
        message = sb("message", [P, 2, G, ACCW], F32)
        edge_feat = sb("edge_feat", [P, G, D], F32)
        parts = sb("parts", [P, 2, 3, G * H], BF16)
        rest = sb("rest", [P, 2, G, H], F32)
        parts_t = sb("parts_t", [3 * G * H, 2, P], BF16)
        pick = sb("pick", [3 * G * H, G * H], BF16)
        red = sb("red", [P, G, H], F32)
        red1 = sb("red1", [P, H], F32)
        logit = sb("logit", [P, 4, G, H], F32)
        dst_value = sb("dst_value", [P, G, 2 * H], F32)
        window_dst = sb("window_dst", [P, 2, 6 * H], BF16)
        params = sb("params", [P, COLS["l2"].width], F32)
        ln_g, ln_b = sb("ln_g", [P, D], F32), sb("ln_b", [P, D], F32)
        agg_scale = sb("agg_scale", [P, 1], F32)
        params1 = params[:, 0:COLS["l1"].width]
        params0 = params[:, 0:COLS["l0"].width]
        params3 = params[:, 0:COLS["l3"].width]
        over_nodes = params[:, COLS["l3"].width:COLS["l3"].width + 4 * D].rearrange("p (n d) -> p n d", n=4)
        rows_flat = rows_buf[:, :, :, :].rearrange("p u g w -> p (u g w)")
        node_x = rows_flat[:, 0:2 * C * D].rearrange("p (s b d) -> p s b d", s=2, d=D)
        node_t = rows_flat[:, 2 * C * D:4 * C * D].rearrange("p (s j n) -> p s j n", s=2, n=P)

        dst_i = tmp[:, :, :].rearrange("p b d -> p (b d)")[:, 0:NT].bitcast(I32)
        dst_part = x_inner[:, :, :].rearrange("p b d -> p (b d)")[:, 0:NT].bitcast(I32)
        GR, GP = L.group_rows, NG // L.group_rows
        stage_flat = stage[:, :, :].rearrange("p b d -> p (b d)")
        acc_flat = acc[:, :, :].rearrange("p b d -> p (b d)")
        groups_i = stage_flat[0:GP, 0:GR * G * P].bitcast(I32).rearrange("p (r e) -> p r e", r=GR)
        groups_f = acc_flat[0:GP, 0:GR * G * P].rearrange("p (r e) -> p r e", r=GR)
        span = sb("span", [P, 4, max(GR, 2)], F32)
        span_i = sb("span_i", [P, 2, GR], I32)
        x_inner_flat = x_inner[:, :, :].rearrange("p b d -> p (b d)")
        base_i = x_inner_flat[:, NT:NT + 3 * NG].bitcast(I32).rearrange("p (n g) -> p n g", n=3)
        span_row = x_inner_flat[:, NT + 3 * NG:NT + 6 * NG].rearrange("p (n g) -> p n g", n=3)

        banks = ps("banks", [P, 8, 512], F32)
        bank = [banks[:, n, :] for n in range(8)]

        s_load = sem("s_load")
        s_store = sem("s_store")
        s_pool = sem("s_pool")
        s_dve = sem("s_dve")
        s_ready = sem("s_ready")
        s_var = sem("s_var")
        s_std = sem("s_std")
        s_pe = sem("s_pe")
        s_chunk_x = sem("s_chunk_x")
        s_chunk_t = sem("s_chunk_t")
        s_chunk_tc = sem("s_chunk_tc")
        s_chunk_m = sem("s_chunk_m")
        s_chunk_o = sem("s_chunk_o")
        s_chunk_h = sem("s_chunk_h")
        s_chunk_b = sem("s_chunk_b")
        s_chunk_l = sem("s_chunk_l")
        s_ln_sum = sem("s_ln_sum")
        s_ln_var = sem("s_ln_var")
        s_ln_sq = sem("s_ln_sq")
        s_half = sem("s_half")
        s_half_sq = sem("s_half_sq")
        s_scaled = sem("s_scaled")
        s_kept = sem("s_kept")
        s_turn = sem("s_turn")
        s_idx = [sem(f"s_idx{u}") for u in range(U)]
        s_rows = [sem(f"s_rows{u}") for u in range(U)]
        s_attr = [sem(f"s_attr{u}") for u in range(U)]
        s_spill = [sem(f"s_spill{u}") for u in range(U)]
        s_hot = sem("s_hot")
        s_sum = sem("s_sum")
        s_acc = sem("s_acc")
        s_hid = sem("s_hid")
        s_act_hid = sem("s_act_hid")
        s_leaky = sem("s_leaky")
        s_edge = sem("s_edge")
        s_feat = sem("s_feat")
        s_split = sem("s_split")
        s_tr = sem("s_tr")
        s_tr_sb = sem("s_tr_sb")
        s_msg = sem("s_msg")
        s_bc = sem("s_bc")
        s_red = sem("s_red")
        s_group = sem("s_group")
        s_window = sem("s_window")
        s_hot_t = sem("s_hot_t")
        s_hot_t_sb = sem("s_hot_t_sb")
        s_dst = sem("s_dst")
        s_logit = sem("s_logit")
        s_exp = sem("s_exp")
        numbers = [s.num for s in semaphores]
        assert numbers == list(range(numbers[0], numbers[0] + len(numbers)))

        def stage_end():
            used = range(numbers[0], numbers[-1] + 1)
            nc.gpsimd.dma_reset(used)
            nc.gpsimd.sem_clear(used)
            nc.all_engine_barrier()

        def whole(t, width=D):
            return t[:, :, 0:width]

        def over_blocks(vector, width=D, blocks=B):
            return vector.unsqueeze(1).broadcast_to([P, blocks, width])

        def over_row(per_node, width=D, blocks=B):
            return per_node.unsqueeze(2).broadcast_to([P, blocks, width])

        def rows_of(t):
            return t.rearrange("(b p) d -> p b d", p=P)

        with nc.Block() as block:
            @block.sync
            def _(sp):
                sp.dma_start(dst_i, dst_tiles).then_inc(s_load, 16)
                sp.dma_start(groups_i, dst_groups.rearrange("(p r) e -> p r e", r=GR)).then_inc(s_idx[0], 16)
                sp.dma_start(params0, l0_params).then_inc(s_idx[1], 16)
                sp.dma_start(x_outer[:, :, :], x_in.rearrange("(b p) d -> p b d", p=P)).then_inc(s_idx[1], 16)
                sp.wait_ge(s_hot, 1)
                sp.dma_start(group_min.rearrange("(p r) o -> p (r o)", r=GR), span_i[0:GP, 0, :]).then_inc(s_store, 16)
                sp.dma_start(group_max.rearrange("(p r) o -> p (r o)", r=GR), span_i[0:GP, 1, :]).then_inc(s_store, 16)
                sp.wait_ge(s_store, 32)
                for n, t in enumerate((group_min, group_max)):
                    sp.dma_start(base_i[:, n, :], t.rearrange("g o -> o g").broadcast_to([P, NG])).then_inc(s_attr[0], 16)
                sp.wait_ge(s_idx[1], 32)

            @block.gpsimd
            def _(pool):
                pool.iota(iota1[:, :], pattern=[[1, P]], base=1, channel_multiplier=0,
                          allow_small_or_imprecise_dtypes=True).then_inc(s_pool, 1)
                pool.iota(iota_p[:, :], pattern=[[0, 1]], base=0, channel_multiplier=1,
                          allow_small_or_imprecise_dtypes=True).then_inc(s_pool, 1)
                pool.memset(ident[:, :], 0.0).then_inc(s_pool, 1)
                pool.memset(ones[:, :], 1.0).then_inc(s_pool, 1)
                pool.memset(far_ident[:, :, :], 0.0).then_inc(s_pool, 1)
                pool.memset(valid[:, :], 1.0).then_inc(s_pool, 1)
                pool.memset(pick[:, :], 0.0).then_inc(s_pool, 1)
                pool.wait_ge(s_pool, 7)
                for part in range(3):
                    pool.affine_select(out=pick[:, :], in_=pick[:, :], compare_op=ALU.not_equal, fill=1.0,
                                       base=-part * G * H, pattern=[[-1, G * H]],
                                       channel_multiplier=1).then_inc(s_pool, 1)
                    pool.wait_ge(s_pool, 8 + part)
                pool.affine_select(out=ident[:, :], in_=ident[:, :], compare_op=ALU.not_equal, fill=1.0,
                                   base=0, pattern=[[-1, P]], channel_multiplier=1).then_inc(s_pool, 1)
                pool.affine_select(out=far_ident[:, :, :], in_=far_ident[:, :, :], compare_op=ALU.not_equal,
                                   fill=-FAR, base=0, pattern=[[0, H], [-1, P]],
                                   channel_multiplier=1).then_inc(s_pool, 1)
                pool.affine_select(out=valid[:, :], in_=valid[:, :], compare_op=ALU.is_ge, fill=0.0,
                                   base=L.nodes - 1, pattern=[[-P, B]], channel_multiplier=-1).then_inc(s_pool, 1)
                pool.wait_ge(s_dve, 4)
                pool.affine_select(out=place_of[:, :], in_=place_of[:, :], compare_op=ALU.is_ge, fill=0.0,
                                   base=L.edges - 1, pattern=[[-P, NT]], channel_multiplier=-1).then_inc(s_pool, 1)

            @block.vector
            def _(dve):
                d = Steps(s_dve)

                def then(instruction):
                    d.add(instruction)
                    dve.wait_ge(s_dve, d.count)

                dve.wait_ge(s_load, 16)
                then(dve.tensor_scalar(dst_part, dst_i, 127, None, ALU.bitwise_and))
                then(dve.tensor_scalar(place_of[:, :], dst_part, 1.0, None, ALU.add))
                then(dve.tensor_scalar(dst_part, dst_i, 7, None, ALU.logical_shift_right))
                then(dve.tensor_copy(block_of[:, :], dst_part))
                dve.wait_ge(s_idx[0], 16)
                then(dve.tensor_copy(groups_f, groups_i))
                then(dve.tensor_reduce(out=span[0:GP, 0, 0:GR], in_=groups_f, op=ALU.min, axis=AX.X))
                then(dve.tensor_reduce(out=span[0:GP, 1, 0:GR], in_=groups_f, op=ALU.max, axis=AX.X))
                then(dve.tensor_copy(span_i[0:GP, :, :], span[0:GP, 0:2, 0:GR]))
                dve.wait_ge(s_dve, d.count)
                dve.sem_inc(s_hot, 1)
                dve.wait_ge(s_attr[0], 32)
                then(dve.tensor_scalar(base_i[:, 2, :], base_i[:, 0, :], 127, None, ALU.bitwise_and))
                then(dve.tensor_copy(base_place[:, :], base_i[:, 2, :]))
                then(dve.tensor_scalar(base_i[:, 2, :], base_i[:, 0, :], 7, None, ALU.logical_shift_right))
                then(dve.tensor_copy(near_block[:, :], base_i[0:1, 2, :]))
                then(dve.tensor_copy(span_row[:, 0:2, :], base_i[:, 0:2, :]))
                then(dve.tensor_tensor(span_row[:, 2, :], span_row[:, 1, :], span_row[:, 0, :], ALU.subtract))
                then(dve.tensor_reduce(out=span[:, 2, 0:1], in_=span_row[:, 2, :], op=ALU.max, axis=AX.X))
                then(dve.tensor_scalar(scattered[:, :], span[:, 2, 0:1], float(P), None, ALU.is_ge))
                then(dve.tensor_scalar(gathered_near[:, :], scattered[:, :], -1.0, 1.0, ALU.mult, ALU.add))
                then(dve.tensor_scalar(span[:, 3, 0:1], scattered[:, :], float(L.blocks_used - 1), 1.0, ALU.mult, ALU.add))
                then(dve.tensor_copy(windows[:, :], span[0:1, 3, 0:1]))
                then(dve.tensor_scalar(near_block[:, :], near_block[:, :], gathered_near[0:1, :], None, ALU.mult))
                dve.wait_ge(s_pool, 2)
                then(dve.tensor_scalar(low[:, :], base_place[:, :], iota_p[:, :], scattered[:, :], ALU.is_le, ALU.max))
                dve.wait_ge(s_pool, 11)
                then(dve.tensor_copy(ident_bf[:, :], ident[:, :]))
                then(dve.tensor_scalar(high[:, :], low[:, :], -1.0, 1.0, ALU.mult, ALU.add))
                then(dve.tensor_scalar(low_far[:, :], high[:, :], -FAR, None, ALU.mult))
                then(dve.tensor_scalar(high_far[:, :], low[:, :], -FAR, None, ALU.mult))
                dve.wait_ge(s_pool, 14)
        stage_end()
        pass_windows = nc.values_load(windows[0:1, 0:1], min_val=1, max_val=L.blocks_used,
                                      skip_runtime_bounds_check_because="it is 1 or the number of blocks")

        def each_group(engine, body):
            with engine.Fori(0, ITER - 1) as i:
                for u in range(U):
                    body(i * U + u, i, u, U)
            for u in range(U):
                body((ITER - 1) * U + u, ITER - 1, u, U - 1 - u)

        def of_group(t, g):
            return t[bass.ds(g, 1), :, :].rearrange("o p e -> (o p) e")

        def index_loads(sp, indices, after_rows=None, beside=None):
            for u in range(U):
                sp.dma_start(idx_buf[:, u, :], of_group(indices, u)).then_inc(s_idx[u], 16)

            def body(g, i, u, ahead):
                if beside:
                    beside(g, i, u)
                sp.wait_ge(s_rows[u], (i + 1) * (16 * G))
                if after_rows:
                    after_rows(g, i, u)
                if ahead >= U:
                    sp.dma_start(idx_buf[:, u, :], of_group(indices, g + U)).then_inc(s_idx[u], 16)

            each_group(sp, body)

        def gather(pool, source, slot_rows, wait_free):
            with pool.Fori(0, ITER) as i:
                for u in range(U):
                    pool.wait_ge(s_idx[u], (i + 1) * 16)
                    wait_free(pool, i * U + u, i, u)
                    pool.sem_inc(s_turn, 1)
                    for t in range(G):
                        pool.indirect_dma_start(
                            out=slot_rows(u, t), out_offset=None, in_=source,
                            in_offset=bass.IndirectOffsetOnAxis(ap=idx_buf[:, u, t:t + 1], axis=0),
                        ).then_inc(s_rows[u], 16)

        def open_windows(dve):
            d = Steps(s_dve)
            d.add(dve.tensor_scalar(key[:, :], block_of[:, :], window[:, :], gathered_near[:, :], ALU.is_equal, ALU.max))
            d.add(dve.tensor_tensor(span[0:1, 0, 0:1], window[0:1, :], scattered[0:1, :], ALU.mult))
            dve.wait_ge(s_dve, d.count)
            d.add(dve.tensor_tensor(key[:, :], key[:, :], place_of[:, :], ALU.mult))
            d.add(dve.tensor_scalar(pass_block[0:1, :], near_block[0:1, :], span[0:1, 0, 0:1], None, ALU.add))
            d.add(dve.tensor_scalar(window[:, :], window[:, :], 1.0, None, ALU.add))
            dve.wait_ge(s_dve, d.count)

        def make_onehot(dve, g, to, op=ALU.is_equal):
            dve.tensor_tensor(
                to, iota1[:, :].unsqueeze(1).broadcast_to([P, G, P]),
                key[:, bass.ds(g * G, G)].unsqueeze(2).broadcast_to([P, G, P]), op).then_inc(s_hot, 1)

        def block_of_group(dve, g):
            return dve.value_load(pass_block[0:1, bass.ds(g, 1)], min_val=0, max_val=L.blocks_used - 1)

        def add_side(dve, g, b, slot, width, n):
            if n == 0:
                dve.wait_ge(s_sum, g + (U + 1))
            dve.wait_ge(s_acc, g * 2 + (4 + n))
            to = acc[:, bass.ds(b + n, 1), 0:width].rearrange("p o w -> p (o w)")
            dve.scalar_tensor_tensor(
                out=to, in0=bank[6 + slot][:, 0:width], scalar=(low, high)[n][:, bass.ds(g, 1)], in1=to,
                op0=ALU.mult, op1=ALU.add).then_inc(s_acc, 1)

        def add_sums(dve, g, b, slot, width):
            for n in range(2):
                add_side(dve, g, b, slot, width, n)

        def sum_group(pe, g, slot, rows, width, hot=None):
            hot = onehot[:, slot, :, :] if hot is None else hot
            pe.wait_ge(s_hot, g + 1)
            pe.wait_ge(s_acc, g * 2 + 2)
            for t in range(G):
                ins = pe.matmul(bank[6 + slot][:, 0:width], hot[:, t, :], rows(t),
                                start=(t == 0), stop=(t == G - 1))
            ins.then_inc(s_sum, 1)

        def run_windows(emit):
            with nc.Fori(0, pass_windows):
                with nc.Block() as block:
                    emit(block)
                stage_end()

        def sum_pass(block):
            @block.sync
            def _(sp):
                index_loads(sp, src_idx)

            @block.gpsimd
            def _(pool):
                gather(pool, table, lambda u, t: rows_buf[:, u, t, 0:D],
                       lambda e, g, i, u: e.wait_ge(s_sum, g + 1))

            @block.vector
            def _(dve):
                dve.sem_inc(s_acc, 4)
                open_windows(dve)

                def body(g, i, u, ahead):
                    make_onehot(dve, g, onehot[:, u % 2, :, :])
                    add_sums(dve, g, block_of_group(dve, g), u % 2, D)

                each_group(dve, body)
                dve.wait_ge(s_acc, 4 + 2 * NG)

            @block.tensor
            def _(pe):
                pe.sem_inc(s_sum, U)

                def body(g, i, u, ahead):
                    pe.wait_ge(s_rows[u], (i + 1) * (16 * G))
                    sum_group(pe, g, u % 2, lambda t: rows_buf[:, u, t, 0:D], D)

                each_group(pe, body)

        def edge_mlp_pass(block):
            w1, b1 = COLS["l2"](params, "We1"), COLS["l2"](params, "be1")
            w2, b2 = COLS["l2"](params, "We2"), COLS["l2"](params, "be2")

            @block.sync
            def _(sp):
                def attributes(g, i, u):
                    sp.wait_ge(s_hid, g + 1)
                    sp.dma_start(attr_buf[:, u, :, :].rearrange("p a e -> p (a e)"), of_group(attr, g)).then_inc(s_attr[u], 16)

                index_loads(sp, src_idx, beside=attributes)

            @block.gpsimd
            def _(pool):
                gather(pool, table, lambda u, t: rows_buf[:, u, t, 0:D],
                       lambda e, g, i, u: e.wait_ge(s_msg, g + 1))

            @block.scalar
            def _(act):
                act.sem_inc(s_act_hid, 2)

                def body(g, i, u, ahead):
                    act.wait_ge(s_hid, g + (U + 1))
                    act.wait_ge(s_edge, g + 1)
                    act.activation(hidden[:, u % 2, :], bank[u % 2], ACT.Identity, bias=b1).then_inc(s_act_hid, 1)

                each_group(act, body)

            @block.vector
            def _(dve):
                dve.sem_inc(s_acc, 4)
                dve.sem_inc(s_msg, U)
                dve.sem_inc(s_feat, 2)
                open_windows(dve)

                def leaky(g, slot):
                    dve.wait_ge(s_act_hid, g + 3)
                    dve.scalar_tensor_tensor(out=hidden[:, slot, :], in0=hidden[:, slot, :], scalar=0.1,
                                             in1=hidden[:, slot, :], op0=ALU.mult, op1=ALU.max).then_inc(s_leaky, 1)

                make_onehot(dve, 0, onehot[:, 0, :, :])
                leaky(0, 0)

                def body(g, i, u, ahead):
                    slot = u % 2
                    if ahead >= 1:
                        leaky(g + 1, 1 - slot)
                    dve.wait_ge(s_edge, g + 3)
                    dve.wait_ge(s_msg, g + U)
                    dve.tensor_tensor(edge_feat[:, :, :], bank[4 + slot].rearrange("p (t d) -> p t d", d=D),
                                      b2.unsqueeze(1).broadcast_to([P, G, D]), ALU.add).then_inc(s_feat, 1)
                    dve.wait_ge(s_rows[u], (i + 1) * (16 * G))
                    dve.wait_ge(s_feat, g + 3)
                    dve.tensor_tensor(message[:, slot, :, 0:D], edge_feat[:, :, :], rows_buf[:, u, :, 0:D],
                                      ALU.mult).then_inc(s_msg, 1)
                    if ahead >= 1:
                        make_onehot(dve, g + 1, onehot[:, 1 - slot, :, :])
                    b = block_of_group(dve, g)
                    add_sums(dve, g, b, slot, D)

                each_group(dve, body)
                dve.wait_ge(s_acc, 4 + 2 * NG)

            @block.tensor
            def _(pe):
                pe.sem_inc(s_sum, U)
                pe.sem_inc(s_hid, U)
                pe.sem_inc(s_edge, 2)

                def hidden_layer(g, i, u):
                    pe.wait_ge(s_attr[u], (i + 1) * 16)
                    pe.wait_ge(s_act_hid, g + 1)
                    for pair in range(2):
                        ins = pe.matmul(bank[u % 2][:, pair * 2 * P:(pair + 1) * 2 * P], w1[:, pair * P:(pair + 1) * P],
                                        attr_buf[:, u, :, :].rearrange("p a e -> p (a e)"), start=True, stop=True)
                    ins.then_inc(s_hid, 1)

                def edge_features(g, slot):
                    pe.wait_ge(s_leaky, g + 1)
                    pe.wait_ge(s_feat, g + 1)
                    for half in range(2):
                        for pair in range(2):
                            t, at = 4 * half + 2 * pair, (2 * pair + half) * P
                            ins = pe.matmul(bank[4 + slot][:, t * D:(t + 2) * D], hidden[:, slot, at:at + P], w2,
                                            start=True, stop=True)
                    ins.then_inc(s_edge, 1)

                hidden_layer(0, 0, 0)
                hidden_layer(1, 0, 1)
                edge_features(0, 0)

                def body(g, i, u, ahead):
                    if ahead >= 2:
                        hidden_layer(g + 2, i + (u + 2) // U, (u + 2) % U)
                    if ahead >= 1:
                        edge_features(g + 1, (u + 1) % 2)
                    pe.wait_ge(s_msg, g + (U + 1))
                    sum_group(pe, g, u % 2, lambda t: message[:, u % 2, t, 0:D], D)

                each_group(pe, body)

        def transposed_bank(slot):
            return bank[4 + slot][0:3 * G * H, 0:P // 2].bitcast(BF16)

        def max_pass(block):
            @block.sync
            def _(sp):
                def keep(g, i, u):
                    sp.dma_start(of_group(spill, g), rows_buf[:, u, :, :].rearrange("p t w -> p (t w)")).then_inc(s_spill[u], 16)
                    sp.wait_ge(s_spill[u], (i + 1) * 16)

                index_loads(sp, src_idx, after_rows=keep)

            @block.gpsimd
            def _(pool):
                gather(pool, table0, lambda u, t: rows_buf[:, u, t, :],
                       lambda e, g, i, u: e.wait_ge(s_split, g * 5 + 5))

            @block.scalar
            def _(act):
                act.sem_inc(s_tr_sb, 2)

                def body(g, i, u, ahead):
                    act.wait_ge(s_tr, g + 3)
                    act.wait_ge(s_bc, g * 4 + (4 * U - 4))
                    act.activation(parts_t[:, u % 2, :], transposed_bank(u % 2), ACT.Copy).then_inc(s_tr_sb, 1)

                each_group(act, body)

            @block.vector
            def _(dve):
                dve.sem_inc(s_acc, 4)
                dve.sem_inc(s_red, 2)
                dve.sem_inc(s_split, 5 * U)
                open_windows(dve)

                def split(g, i, u, n):
                    part = lambda n: parts[:, u % 2, n, :].rearrange("p (g h) -> p g h", h=H)
                    left = rest[:, u % 2, :, :]
                    a_src = rows_buf[:, u, :, D:D + H]
                    if n == 0:
                        dve.wait_ge(s_rows[u], (i + 1) * (16 * G))
                        dve.wait_ge(s_tr, g + 1)
                        ins = dve.tensor_copy(part(0), a_src)
                    else:
                        dve.wait_ge(s_split, g * 5 + (5 * U + n))
                    if n == 1:
                        ins = dve.tensor_tensor(left, a_src, part(0), ALU.subtract)
                    elif n == 2:
                        ins = dve.tensor_copy(part(1), left)
                    elif n == 3:
                        ins = dve.tensor_tensor(left, left, part(1), ALU.subtract)
                    elif n == 4:
                        ins = dve.tensor_copy(part(2), left)
                    ins.then_inc(s_split, 1)

                def masks(g, slot):
                    make_onehot(dve, g, not_hot[:, slot, :, :], ALU.not_equal)

                def pair_maxima(g):
                    for k in range(4):
                        dve.wait_ge(s_bc, g * 4 + (4 * U + k + 1))
                        dve.tensor_reduce(
                            out=red[:, 2 * k:2 * k + 2, :],
                            in_=banks[:, 2 * (k % 2):2 * (k % 2) + 2, :].rearrange("p b (h e) -> p b h e", h=H),
                            op=ALU.max, axis=AX.X).then_inc(s_red, 1)

                def take_maximum(g, b, n):
                    if n == 0:
                        dve.wait_ge(s_red, g * 4 + 6)
                        dve.wait_ge(s_acc, g * 2 + 4)
                        dve.tensor_reduce(out=red1[:, :], in_=red[:, :, :].rearrange("p g h -> p h g"),
                                          op=ALU.max, axis=AX.X).then_inc(s_group, 1)
                        return
                    if n == 1:
                        dve.wait_ge(s_group, g + 1)
                    dve.wait_ge(s_acc, g * 2 + (3 + n))
                    to = head_max[:, bass.ds(b + (n - 1), 1), :].rearrange("p o w -> p (o w)")
                    dve.scalar_tensor_tensor(
                        out=to, in0=red1[:, :], scalar=(low_far, high_far)[n - 1][:, bass.ds(g, 1)], in1=to,
                        op0=ALU.add, op1=ALU.max).then_inc(s_acc, 1)

                for g in range(2):
                    masks(g, g)
                    for n in range(5):
                        split(g, 0, g, n)
                pair_maxima(0)

                def body(g, i, u, ahead):
                    if ahead >= 2:
                        masks(g + 2, u % 2)
                    b = block_of_group(dve, g)
                    for n in range(5):
                        if n < 3:
                            take_maximum(g, b, n)
                        if ahead >= 2:
                            split(g + 2, i + (u + 2) // U, (u + 2) % U, n)
                    if ahead >= 1:
                        pair_maxima(g + 1)

                each_group(dve, body)
                dve.wait_ge(s_acc, 4 + 2 * NG)

            @block.tensor
            def _(pe):
                pe.sem_inc(s_bc, 4 * U)
                pe.sem_inc(s_tr, 2)

                def transpose_parts(g, slot):
                    pe.wait_ge(s_split, g * 5 + (5 * U + 5))
                    pe.wait_ge(s_tr_sb, g + 1)
                    pe.transpose(transposed_bank(slot), parts[:, slot, :, :].rearrange("p n a -> p (n a)"),
                                 ident_bf[:, :]).then_inc(s_tr, 1)

                def spread(g, slot, between):
                    pe.wait_ge(s_hot, g + 1)
                    pe.wait_ge(s_tr_sb, g + 3)
                    for k in range(4):
                        if k == 2:
                            between()
                        pe.wait_ge(s_red, g * 4 + (k + 1))
                        for t in (2 * k, 2 * k + 1):
                            to = bank[t % 4]
                            pe.matmul(to, not_hot[:, slot, t, :], far_ident[:, :, :].rearrange("p h e -> p (h e)"),
                                      start=True, stop=False)
                            for h in range(H):
                                ins = pe.matmul(to[:, h * P:(h + 1) * P],
                                                pick[:, t * H + h:t * H + h + 1].broadcast_to([3 * G * H, P]),
                                                parts_t[:, slot, :], start=False, stop=(h == H - 1))
                        ins.then_inc(s_bc, 1)

                transpose_parts(0, 0)
                spread(0, 0, lambda: transpose_parts(1, 1))

                def body(g, i, u, ahead):
                    if ahead >= 1:
                        spread(g + 1, (u + 1) % 2, lambda: transpose_parts(g + 2, u % 2) if ahead >= 2 else None)

                each_group(pe, body)

        def attention_pass(block):
            @block.sync
            def _(sp):
                def body(g, i, u, ahead):
                    sp.wait_ge(s_msg, g + 1)
                    sp.dma_start(rows_buf[:, u, :, :].rearrange("p t w -> p (t w)"), of_group(spill, g)).then_inc(s_attr[u], 16)

                each_group(sp, body)

            @block.scalar
            def _(act):
                act.sem_inc(s_hot_t_sb, 2)

                def copy_hot(g, slot):
                    act.wait_ge(s_hot_t, g + 3)
                    act.wait_ge(s_dst, g + 1)
                    act.activation(onehots_t[:, slot, :, :].rearrange("p t e -> p (t e)"),
                                   bank[slot].bitcast(BF16), ACT.Copy).then_inc(s_hot_t_sb, 1)

                def weights(g, slot):
                    act.wait_ge(s_logit, g * 5 + 15)
                    act.wait_ge(s_sum, g + (U - 1))
                    act.activation(message[:, slot, :, D:D + H], logit[:, 3, :, :], ACT.Exp).then_inc(s_exp, 1)

                for g in range(3):
                    copy_hot(g, g % 2)
                    if g >= 1:
                        weights(g - 1, g - 1)

                def body(g, i, u, ahead):
                    if ahead >= 3:
                        copy_hot(g + 3, (u + 3) % 2)
                    if ahead >= 2:
                        weights(g + 2, u % 2)

                each_group(act, body)

            @block.vector
            def _(dve):
                dve.sem_inc(s_acc, 4)
                dve.sem_inc(s_msg, U)
                dve.sem_inc(s_logit, 10)
                open_windows(dve)

                def window_rows(g, slot, b, n):
                    to = window_dst[:, slot, :]
                    rows = dst_parts[:, bass.ds(b + n, 1), :, :].rearrange("p o h n -> p (o h n)")
                    if n == 0:
                        dve.tensor_scalar(to, rows, low[:, bass.ds(g, 1)], None, ALU.mult).then_inc(s_window, 1)
                    else:
                        dve.wait_ge(s_window, g * 2 + 1)
                        dve.scalar_tensor_tensor(out=to, in0=rows, scalar=high[:, bass.ds(g, 1)], in1=to,
                                                 op0=ALU.mult, op1=ALU.add).then_inc(s_window, 1)

                def logits(g, i, u, n):
                    if n == 0:
                        dve.wait_ge(s_dst, g + 3)
                        ins = dve.tensor_reduce(
                            out=dst_value[:, :, :], in_=bank[2 + u % 2][:, 0:G * 6 * H].rearrange("p (t h n) -> p t h n", h=2 * H, n=3),
                            op=ALU.add, axis=AX.X)
                    else:
                        dve.wait_ge(s_logit, g * 5 + (10 + n))
                    if n == 1:
                        dve.wait_ge(s_attr[u], (i + 1) * 16)
                        ins = dve.tensor_tensor(logit[:, 0, :, :], rows_buf[:, u, :, D:D + H], dst_value[:, :, 0:H], ALU.add)
                    elif n == 2:
                        ins = dve.scalar_tensor_tensor(out=logit[:, 1, :, :], in0=logit[:, 0, :, :], scalar=0.2,
                                                       in1=logit[:, 0, :, :], op0=ALU.mult, op1=ALU.max)
                    elif n == 3:
                        ins = dve.tensor_tensor(logit[:, 2, :, :], logit[:, 1, :, :], dst_value[:, :, H:2 * H], ALU.subtract)
                    elif n == 4:
                        ins = dve.tensor_scalar(logit[:, 3, :, :], logit[:, 2, :, :], 0.0, None, ALU.min)
                    ins.then_inc(s_logit, 1)

                def messages(g, u):
                    dve.wait_ge(s_exp, g + 1)
                    dve.tensor_tensor(
                        message[:, u % 2, :, 0:D].rearrange("p t (h c) -> p t h c", h=H),
                        rows_buf[:, u, :, 0:D].rearrange("p t (h c) -> p t h c", h=H),
                        message[:, u % 2, :, D:D + H].unsqueeze(3).broadcast_to([P, G, H, DH]),
                        ALU.mult).then_inc(s_msg, 1)

                for g in range(3):
                    make_onehot(dve, g, onehots[:, g, :, :])
                    b = block_of_group(dve, g)
                    for n in range(2):
                        window_rows(g, g % 2, b, n)
                    if g >= 1:
                        for n in range(5):
                            logits(g - 1, 0, g - 1, n)
                    if g == 1:
                        messages(0, 0)

                def body(g, i, u, ahead):
                    if ahead >= 3:
                        make_onehot(dve, g + 3, onehots[:, (u + 3) % U, :, :])
                        b_ahead = block_of_group(dve, g + 3)
                    b = block_of_group(dve, g)
                    if ahead >= 1:
                        messages(g + 1, (u + 1) % U)
                    next_i, next_u = i + (u + 2) // U, (u + 2) % U
                    for n in range(5):
                        if ahead >= 2:
                            logits(g + 2, next_i, next_u, n)
                        if n in (0, 2) and ahead >= 3:
                            window_rows(g + 3, (u + 3) % 2, b_ahead, n // 2)
                        if n in (1, 3):
                            add_side(dve, g, b, u % 2, ACCW, n // 2)

                each_group(dve, body)
                dve.wait_ge(s_acc, 4 + 2 * NG)

            @block.tensor
            def _(pe):
                pe.sem_inc(s_sum, U)
                pe.sem_inc(s_hot_t, 2)
                pe.sem_inc(s_dst, 2)

                def transpose_hot(g, slot, hot):
                    pe.wait_ge(s_hot, g + 1)
                    pe.wait_ge(s_hot_t_sb, g + 1)
                    upper = hot.rearrange("p t e -> p (t e)").bitcast(BF16).rearrange("p (t e two) -> p t e two", t=G, two=2)
                    for t in range(G):
                        ins = pe.transpose(bank[slot].bitcast(BF16)[:, t * P:(t + 1) * P], upper[:, t, :, 1], ident_bf[:, :])
                    ins.then_inc(s_hot_t, 1)

                def destinations(g, slot):
                    pe.wait_ge(s_hot_t_sb, g + 3)
                    pe.wait_ge(s_window, g * 2 + 2)
                    pe.wait_ge(s_logit, g * 5 + 1)
                    for t in range(G):
                        ins = pe.matmul(bank[2 + slot][:, t * 6 * H:(t + 1) * 6 * H], onehots_t[:, slot, t, :],
                                        window_dst[:, slot, :], start=True, stop=True)
                    ins.then_inc(s_dst, 1)

                def sums(g, u):
                    pe.wait_ge(s_msg, g + (U + 1))
                    sum_group(pe, g, u % 2, lambda t: message[:, u % 2, t, :], ACCW, onehots[:, u, :, :])

                for g in range(3):
                    transpose_hot(g, g % 2, onehots[:, g, :, :])
                    destinations(g, g % 2)
                sums(0, 0)

                def body(g, i, u, ahead):
                    if ahead >= 3:
                        transpose_hot(g + 3, (u + 3) % 2, onehots[:, (u + 3) % U, :, :])
                    if ahead >= 1:
                        sums(g + 1, (u + 1) % U)
                    if ahead >= 3:
                        destinations(g + 3, (u + 3) % 2)

                each_group(pe, body)

        def each_chunk_pair(engine, body):
            with engine.Fori(0, L.chunks // 2) as i:
                body(i)

        def bring_chunks(block, x, summed=False, clear=False):
            @block.gpsimd
            def _(pool):
                def body(i):
                    if summed:
                        pool.wait_ge(s_ln_sum, i * 3 + 3)
                    for slot in range(2):
                        c = i * 2 + slot
                        pool.wait_ge(s_chunk_t, c + 1)
                        pool.sem_inc(s_turn, 1)
                        pool.tensor_copy(node_x[:, slot, :, :], x[:, bass.ds(c * C, C), :]).then_inc(s_chunk_x, 1)

                each_chunk_pair(pool, body)
                if clear:
                    pool.memset(acc[:, :, :], 0.0).then_inc(s_pool, 1)
                    pool.wait_ge(s_pool, 1)

        def transpose_chunk(pe, c, slot):
            pe.wait_ge(s_chunk_x, c + 1)
            pe.wait_ge(s_chunk_tc, c + 1)
            for j in range(C // 2):
                ins = pe.transpose(bank[slot][:, j * P:(j + 1) * P],
                                   node_x[:, slot, 2 * j:2 * j + 2, :].rearrange("p b d -> p (b d)"), ident[:, :])
            ins.then_inc(s_chunk_t, 1)

        def copy_transposed(act, c, slot, s_used, function=ACT.Copy):
            act.wait_ge(s_chunk_t, c + 3)
            act.wait_ge(s_used, c + 1)
            act.activation(node_t[:, slot, :, :].rearrange("p j n -> p (j n)"), bank[slot][:, 0:C // 2 * P],
                           function).then_inc(s_chunk_tc, 1)

        def project(block, x, w, summed=False, clear=False):
            bring_chunks(block, x, summed, clear)

            @block.tensor
            def _(pe):
                pe.sem_inc(s_chunk_t, 2)
                pe.sem_inc(s_chunk_m, 2)
                pe.wait_ge(s_load, 16)

                def body(i):
                    for slot in range(2):
                        transpose_chunk(pe, i * 2 + slot, slot)
                    for slot in range(2):
                        c = i * 2 + slot
                        pe.wait_ge(s_chunk_tc, c + 3)
                        pe.wait_ge(s_chunk_o, c + 1)
                        for j in range(C // 2):
                            ins = pe.matmul(bank[4 + slot][:, j * 2 * D:(j + 1) * 2 * D], node_t[:, slot, j, :],
                                            w, start=True, stop=True)
                        ins.then_inc(s_chunk_m, 1)

                each_chunk_pair(pe, body)

        def project_copies(act, function=ACT.Copy):
            act.sem_inc(s_chunk_tc, 2)

            def body(i):
                for slot in range(2):
                    copy_transposed(act, i * 2 + slot, slot, s_chunk_m, function)

            each_chunk_pair(act, body)

        def take_products(dve, to, op):
            dve.sem_inc(s_chunk_o, 2)

            def body(i):
                for slot in range(2):
                    c = i * 2 + slot
                    dve.wait_ge(s_chunk_m, c + 3)
                    op(to[:, bass.ds(c * C, C), 0:D], bank[4 + slot][:, 0:C * D].rearrange("p (b d) -> p b d", d=D),
                       bass.ds(c * C, C)).then_inc(s_chunk_o, 1)

            each_chunk_pair(dve, body)
            dve.wait_ge(s_chunk_o, 2 + L.chunks)

        HALVES = [slice(h * B // 2, (h + 1) * B // 2) for h in range(2)]
        PIECES = [slice(q * B // 4, (q + 1) * B // 4) for q in range(4)]

        def layer_norm(dve, then, n, x, to, gamma=None, beta=None, signal=None, before=0):
            for h in HALVES:
                then(dve.tensor_reduce(out=stat[:, 0, h], in_=x[:, h, :], op=ALU.add, axis=AX.X))
                then(dve.tensor_scalar(stat[:, 0, h], stat[:, 0, h], 1.0 / D, None, ALU.mult))
                dve.tensor_tensor(tmp[:, h, :], x[:, h, :], over_row(stat[:, 0, h], D, B // 2), ALU.subtract).then_inc(s_half, 1)
            for k, h in enumerate(HALVES):
                dve.wait_ge(s_half_sq, 2 * (n - before) + k + 1)
                then(dve.tensor_reduce(out=stat[:, 1, h], in_=stage[:, h, 0:D], op=ALU.add, axis=AX.X))
            dve.tensor_scalar(stat[:, 1, :], stat[:, 1, :], 1.0 / D, 1e-5, ALU.mult, ALU.add).then_inc(s_var, 1)
            dve.wait_ge(s_std, n + 1)
            then(dve.reciprocal(stat[:, 2, :], stat[:, 2, :]))
            if signal is not None:
                for q in PIECES:
                    dve.tensor_tensor(to[:, q, :], tmp[:, q, :], over_row(stat[:, 2, q], D, B // 4), ALU.mult).then_inc(signal, 1)
                dve.wait_ge(signal, len(PIECES))
                return
            then(dve.tensor_tensor(to, tmp[:, :, :], over_row(stat[:, 2, :]), ALU.mult))
            if gamma is not None:
                then(dve.tensor_tensor(to, to, over_blocks(gamma), ALU.mult))
                then(dve.tensor_tensor(to, to, over_blocks(beta), ALU.add))

        def layer_norm_root(act, n, before=0):
            for k, h in enumerate(HALVES):
                act.wait_ge(s_half, 2 * (n - before) + k + 1)
                act.activation(stage[:, h, 0:D], tmp[:, h, :], ACT.Square).then_inc(s_half_sq, 1)
            act.wait_ge(s_var, n + 1)
            act.activation(stat[:, 2, :], stat[:, 1, :], ACT.Sqrt).then_inc(s_std, 1)

        def chain(dve):
            d = Steps(s_dve)

            def then(instruction):
                d.add(instruction)
                dve.wait_ge(s_dve, d.count)

            return then

        S = 2 * C
        SPANS = B // S

        def span_of(t, j, width=D):
            return t[:, bass.ds(j * S, S), 0:width]

        def pipelined(engine, *steps):
            last = max(lag for lag, step in steps)

            def turn(i):
                for lag, step in steps:
                    if 0 <= i - lag < SPANS:
                        step(i - lag)

            for i in range(min(last, SPANS)):
                turn(i)
            if SPANS > last:
                with engine.Fori(last, SPANS) as i:
                    for lag, step in steps:
                        step(i - lag)
            for i in range(max(last, SPANS) if SPANS > last else SPANS, SPANS + last):
                turn(i)

        def store_spans(sp, to, source, takes=1):
            def store(j):
                sp.wait_ge(s_chunk_o, j * takes + 2 * takes)
                sp.dma_start(to[bass.ds(j * (S * P), S * P), :].rearrange("(b p) d -> p b d", p=P),
                             span_of(source, j)).then_inc(s_store, 16)

            pipelined(sp, (0, store))
            sp.wait_ge(s_store, 16 * SPANS)

        def store_table(sp, to, source):
            sp.wait_ge(s_ready, 1)
            sp.dma_start(rows_of(to), source).then_inc(s_store, 16)
            sp.wait_ge(s_store, 16)

        with nc.Block() as block:
            w0 = COLS["l0"](params0, "W")
            project(block, x_outer, w0)

            @block.sync
            def _(sp):
                sp.dma_start(params0, l0_params).then_inc(s_load, 16)
                store_table(sp, table0, stage[:, :, :])

            @block.scalar
            def _(act):
                project_copies(act)

            @block.vector
            def _(dve):
                then = chain(dve)
                take_products(dve, stage, lambda o, i, b: dve.tensor_copy(o, i))
                for name, to in (("att_src", stage[:, :, D:D + H]), ("att_dst", dst_rows[:, :, 0:H])):
                    then(dve.tensor_tensor(tmp[:, :, :], whole(stage), over_blocks(COLS["l0"](params0, name)), ALU.mult))
                    then(dve.tensor_reduce(out=to, in_=tmp[:, :, :].rearrange("p b (h c) -> p b h c", h=H),
                                           op=ALU.add, axis=AX.X))
                    dve.sem_inc(s_ready, 1)
                then(dve.tensor_copy(head_max[:, :, :], stage[:, :, D:D + H]))
                then(dve.memset(window[:, :], 0.0))
        stage_end()

        run_windows(max_pass)

        with nc.Block() as block:
            @block.scalar
            def _(act):
                act.wait_ge(s_var, 1)
                act.activation(self_weight[:, :, :], self_weight[:, :, :], ACT.Exp).then_inc(s_std, 1)
                act.wait_ge(s_std, 1)

            @block.vector
            def _(dve):
                then = chain(dve)
                for source, to in ((head_max[:, :, :], dst_rows[:, :, H:2 * H]),
                                   (stage[:, :, D:D + H], self_weight[:, :, :])):
                    then(dve.tensor_tensor(to, source, dst_rows[:, :, 0:H], ALU.add))
                    then(dve.scalar_tensor_tensor(out=to, in0=to, scalar=0.2, in1=to, op0=ALU.mult, op1=ALU.max))
                dve.tensor_tensor(self_weight[:, :, :], self_weight[:, :, :], dst_rows[:, :, H:2 * H], ALU.subtract).then_inc(s_var, 1)
                left = tmp[:, :, 0:2 * H]
                then(dve.tensor_copy(dst_parts[:, :, :, 0], dst_rows[:, :, :]))
                then(dve.tensor_tensor(left, dst_rows[:, :, :], dst_parts[:, :, :, 0], ALU.subtract))
                then(dve.tensor_copy(dst_parts[:, :, :, 1], left))
                then(dve.tensor_tensor(left, left, dst_parts[:, :, :, 1], ALU.subtract))
                then(dve.tensor_copy(dst_parts[:, :, :, 2], left))
                then(dve.memset(acc[:, :, :], 0.0))
                then(dve.memset(message[:, :, :, D + H:ACCW], 1.0))
                then(dve.memset(window[:, :], 0.0))
        stage_end()

        run_windows(attention_pass)

        with nc.Block() as block:
            @block.scalar
            def _(act):
                act.wait_ge(s_var, 1)
                act.activation(dinv[:, :], dinv[:, :], ACT.Sqrt).then_inc(s_std, 1)
                layer_norm_root(act, 1, 1)
                layer_norm_root(act, 2, 1)

            @block.vector
            def _(dve):
                then = chain(dve)
                then(dve.tensor_copy(count[:, :], acc[:, :, D + H]))
                dve.tensor_scalar(dinv[:, :], count[:, :], 1.0, None, ALU.add).then_inc(s_var, 1)
                for h in range(H):
                    cols = slice(h * DH, (h + 1) * DH)
                    then(dve.tensor_tensor(tmp[:, :, cols], stage[:, :, cols], over_row(self_weight[:, :, h], DH), ALU.mult))
                then(dve.tensor_tensor(whole(acc), whole(acc), tmp[:, :, :], ALU.add))
                then(dve.tensor_tensor(self_weight[:, :, :], self_weight[:, :, :], acc[:, :, D:D + H], ALU.add))
                then(dve.tensor_scalar(self_weight[:, :, :], self_weight[:, :, :], 1e-16, None, ALU.add))
                then(dve.reciprocal(self_weight[:, :, :], self_weight[:, :, :]))
                for h in range(H):
                    cols = slice(h * DH, (h + 1) * DH)
                    then(dve.tensor_tensor(tmp[:, :, cols], acc[:, :, cols], over_row(self_weight[:, :, h], DH), ALU.mult))
                then(dve.tensor_tensor(x_inner[:, :, :], tmp[:, :, :], over_blocks(COLS["l0"](params0, "bias")), ALU.add))
                then(dve.tensor_tensor(x_inner[:, :, :], x_inner[:, :, :], x_outer[:, :, :], ALU.add))
                layer_norm(dve, then, 1, x_inner[:, :, :], x_inner[:, :, :],
                           COLS["l0"](params0, "gamma"), COLS["l0"](params0, "beta"), before=1)
                then(dve.tensor_tensor(x_inner[:, :, :], x_inner[:, :, :], x_outer[:, :, :], ALU.add))
                layer_norm(dve, then, 2, x_inner[:, :, :], x_outer[:, :, :], before=1)
                then(dve.reciprocal(dinv[:, :], dinv[:, :]))
        stage_end()

        def convolution_rows(o, i, b):
            return nc.vector.tensor_tensor(o, i, over_row(dinv[:, b], D, C), ALU.mult)

        with nc.Block() as block:
            project(block, x_outer, COLS["l1"](params, "W"))

            @block.sync
            def _(sp):
                sp.dma_start(params1, of_group(l1_params, 0)).then_inc(s_load, 16)
                store_spans(sp, table, stage, 2)

            @block.scalar
            def _(act):
                project_copies(act)

            @block.vector
            def _(dve):
                then = chain(dve)
                take_products(dve, stage, convolution_rows)
                then(dve.memset(acc[:, :, :], 0.0))
                then(dve.memset(window[:, :], 0.0))
        stage_end()

        def end_convolution(dve, to, op):
            def with_own(j):
                dve.tensor_tensor(span_of(x_inner, j), span_of(acc, j), span_of(stage, j), ALU.add).then_inc(s_ln_sum, 1)

            def normalized(j):
                dve.wait_ge(s_ln_sum, j * 3 + 1)
                dve.tensor_tensor(span_of(x_inner, j), span_of(x_inner, j),
                                  over_row(dinv[:, bass.ds(j * S, S)], D, S), ALU.mult).then_inc(s_ln_sum, 1)

            def with_bias(j):
                dve.wait_ge(s_ln_sum, j * 3 + 2)
                dve.tensor_tensor(span_of(x_inner, j), span_of(x_inner, j), over_blocks(ln_b[:, :], D, S), ALU.add).then_inc(s_ln_sum, 1)

            def take(slot):
                def step(j):
                    c = j * 2 + slot
                    dve.wait_ge(s_chunk_m, c + 3)
                    op(to[:, bass.ds(c * C, C), 0:D], bank[4 + slot][:, 0:C * D].rearrange("p (b d) -> p b d", d=D),
                       bass.ds(c * C, C)).then_inc(s_chunk_o, 1)
                return step

            dve.sem_inc(s_chunk_o, 2)
            pipelined(dve, (0, with_own), (2, take(0)), (0, normalized), (2, take(1)), (0, with_bias))
            dve.wait_ge(s_chunk_o, 2 + L.chunks)

        with nc.Fori(1, l1_layers) as layer:
            run_windows(sum_pass)

            with nc.Block() as block:
                project(block, x_inner, COLS["l1"](params, "W"), summed=True, clear=True)

                @block.sync
                def _(sp):
                    sp.wait_ge(s_dve, 1)
                    sp.dma_start(params1, of_group(l1_params, layer)).then_inc(s_load, 16)
                    store_spans(sp, table, stage, 2)

                @block.scalar
                def _(act):
                    project_copies(act, ACT.Relu)

                @block.vector
                def _(dve):
                    then = chain(dve)
                    then(dve.tensor_copy(ln_b[:, :], COLS["l1"](params, "b")))
                    end_convolution(dve, stage, convolution_rows)
                    then(dve.memset(window[:, :], 0.0))
            stage_end()

        run_windows(sum_pass)

        with nc.Block() as block:
            project(block, x_inner, COLS["l1"](params, "W"), summed=True)

            @block.sync
            def _(sp):
                sp.wait_ge(s_dve, 1)
                sp.dma_start(params1, of_group(l1_params, l1_layers)).then_inc(s_load, 16)

            @block.scalar
            def _(act):
                project_copies(act, ACT.Relu)
                layer_norm_root(act, 0)

            @block.vector
            def _(dve):
                then = chain(dve)
                then(dve.tensor_copy(ln_b[:, :], COLS["l1"](params, "b")))
                dve.wait_ge(s_load, 16)
                end_convolution(dve, acc, lambda o, i, b: dve.tensor_tensor(
                    o, i, over_blocks(COLS["l1"](params, "b"), D, C), ALU.add))
                then(dve.tensor_tensor(whole(acc), whole(acc), x_outer[:, :, :], ALU.add))
                layer_norm(dve, then, 0, whole(acc), x_outer[:, :, :])
                then(dve.tensor_copy(x_inner[:, :, :], x_outer[:, :, :]))
        stage_end()

        p2 = lambda name: COLS["l2"](params, name)
        with nc.Block() as block:
            @block.sync
            def _(sp):
                sp.dma_start(params[:, :], of_group(l2_params, 0)).then_inc(s_load, 16)
                store_spans(sp, table, stage, 2)

            @block.scalar
            def _(act):
                act.sem_inc(s_chunk_tc, 2)
                act.sem_inc(s_chunk_b, 2)
                act.wait_ge(s_load, 16)

                def body(i):
                    for slot in range(2):
                        copy_transposed(act, i * 2 + slot, slot, s_chunk_h)
                    for slot in range(2):
                        c = i * 2 + slot
                        act.wait_ge(s_chunk_h, c + 3)
                        act.wait_ge(s_chunk_m, c + 1)
                        act.activation(hidden[:, slot, :], bank[2 + slot], ACT.Identity, bias=p2("b1")).then_inc(s_chunk_b, 1)

                each_chunk_pair(act, body)

            bring_chunks(block, x_inner)

            @block.tensor
            def _(pe):
                pe.sem_inc(s_chunk_t, 2)
                pe.wait_ge(s_load, 16)
                pe.sem_inc(s_chunk_h, 2)
                pe.sem_inc(s_chunk_m, 2)

                def body(i):
                    for slot in range(2):
                        transpose_chunk(pe, i * 2 + slot, slot)
                    for slot in range(2):
                        c = i * 2 + slot
                        pe.wait_ge(s_chunk_tc, c + 3)
                        pe.wait_ge(s_chunk_b, c + 1)
                        for n in range(C):
                            ins = pe.matmul(bank[2 + slot][:, n * P:(n + 1) * P], p2("W1")[:, n % 2 * P:(n % 2 + 1) * P],
                                            node_t[:, slot, n // 2, :], start=True, stop=True)
                        ins.then_inc(s_chunk_h, 1)
                    for slot in range(2):
                        c = i * 2 + slot
                        pe.wait_ge(s_chunk_l, c + 1)
                        pe.wait_ge(s_chunk_o, c + 1)
                        for n in range(C):
                            ins = pe.matmul(bank[6 + slot][:, n * D:(n + 1) * D],
                                            hidden[:, slot, n * P:(n + 1) * P], p2("W2"), start=True, stop=True)
                        ins.then_inc(s_chunk_m, 1)

                each_chunk_pair(pe, body)

            @block.vector
            def _(dve):
                then = chain(dve)
                dve.sem_inc(s_chunk_o, 2)
                dve.wait_ge(s_load, 16)

                def body(i):
                    for slot in range(2):
                        c = i * 2 + slot
                        dve.wait_ge(s_chunk_b, c + 3)
                        dve.scalar_tensor_tensor(
                            out=hidden[:, slot, :], in0=hidden[:, slot, :], scalar=0.1,
                            in1=hidden[:, slot, :], op0=ALU.mult, op1=ALU.max).then_inc(s_chunk_l, 1)
                    for slot in range(2):
                        c = i * 2 + slot
                        dve.wait_ge(s_chunk_m, c + 3)
                        dve.tensor_tensor(
                            stage[:, bass.ds(c * C, C), 0:D], bank[6 + slot][:, 0:C * D].rearrange("p (b d) -> p b d", d=D),
                            over_blocks(p2("b2"), D, C), ALU.add).then_inc(s_chunk_o, 1)

                each_chunk_pair(dve, body)
                dve.wait_ge(s_chunk_o, 2 + L.chunks)
                dve.sem_inc(s_ready, 1)
                then(dve.memset(acc[:, :, :], 0.0))
                then(dve.memset(window[:, :], 0.0))
        stage_end()

        def between_layers(block, layer):
            span_x = rows_flat[:, 0:S * D].rearrange("p (b d) -> p b d", d=D)
            span_t = rows_flat[:, S * D:2 * S * D].rearrange("p (j n) -> p j n", n=P)

            @block.sync
            def _(sp):
                sp.wait_ge(s_dve, 3)
                sp.dma_start(params[:, :], of_group(l2_params, layer)).then_inc(s_load, 16)
                store_spans(sp, table, stage)

            @block.vector
            def _(dve):
                d = Steps(s_dve)
                d.add(dve.tensor_copy(ln_g[:, :], p2("ln_g")))
                d.add(dve.tensor_copy(ln_b[:, :], p2("ln_b")))
                d.add(dve.tensor_tensor(agg_scale[:, :], p2("dot_scale"), p2("res_w"), ALU.mult))
                dve.wait_ge(s_dve, d.count)
                dve.sem_inc(s_chunk_o, 1)

                def at(j, n):
                    return stat[:, n, bass.ds(j * S, S)]

                def add_aggregate(j):
                    dve.scalar_tensor_tensor(out=span_of(tmp, j), in0=span_of(acc, j), scalar=agg_scale[:, :],
                                             in1=span_of(x_inner, j), op0=ALU.mult, op1=ALU.add).then_inc(s_ln_sum, 1)

                def total(j):
                    dve.wait_ge(s_ln_sum, j * 4 + 1)
                    dve.tensor_reduce(out=at(j, 0), in_=span_of(tmp, j), op=ALU.add, axis=AX.X).then_inc(s_ln_sum, 1)

                def mean(j):
                    dve.wait_ge(s_ln_sum, j * 4 + 2)
                    dve.tensor_scalar(at(j, 0), at(j, 0), 1.0 / D, None, ALU.mult).then_inc(s_ln_sum, 1)

                def less_mean(j):
                    dve.wait_ge(s_ln_sum, j * 4 + 3)
                    dve.tensor_tensor(span_of(tmp, j), span_of(tmp, j), over_row(at(j, 0), D, S), ALU.subtract).then_inc(s_ln_sum, 1)

                def squares_total(j):
                    dve.wait_ge(s_ln_sq, j + 1)
                    dve.tensor_reduce(out=at(j, 1), in_=span_of(stage, j), op=ALU.add, axis=AX.X).then_inc(s_ln_var, 1)

                def variance(j):
                    dve.wait_ge(s_ln_var, j * 4 + 1)
                    dve.tensor_scalar(at(j, 1), at(j, 1), 1.0 / D, 1e-5, ALU.mult, ALU.add).then_inc(s_ln_var, 1)

                def scale(j):
                    dve.wait_ge(s_std, j + 1)
                    dve.reciprocal(at(j, 2), at(j, 2)).then_inc(s_ln_var, 1)

                def scaled(j):
                    dve.wait_ge(s_ln_var, j * 4 + 3)
                    dve.tensor_tensor(span_of(tmp, j), span_of(tmp, j), over_row(at(j, 2), D, S), ALU.mult).then_inc(s_ln_var, 1)

                def leaky(half):
                    def step(j):
                        dve.wait_ge(s_chunk_b, j * 2 + (3 + half))
                        dve.scalar_tensor_tensor(
                            out=hidden[:, half, :], in0=hidden[:, half, :], scalar=0.1,
                            in1=hidden[:, half, :], op0=ALU.mult, op1=ALU.max).then_inc(s_chunk_l, 1)
                    return step

                def take(j):
                    dve.wait_ge(s_chunk_m, j * 2 + 4)
                    dve.tensor_tensor(span_of(stage, j), bank[6].rearrange("p (b d) -> p b d", d=D),
                                      over_blocks(p2("b2"), D, S), ALU.add).then_inc(s_chunk_o, 1)

                pipelined(dve, (0, add_aggregate), (1, squares_total), (0, total), (5, take), (1, variance), (0, mean), (4, leaky(0)), (0, less_mean), (1, scale), (4, leaky(1)), (1, scaled))
                dve.memset(window[:, :], 0.0).then_inc(s_dve, 1)
                dve.wait_ge(s_chunk_o, 1 + SPANS)
                dve.wait_ge(s_dve, d.count + 1)

            @block.gpsimd
            def _(pool):
                def gamma(j):
                    pool.wait_ge(s_ln_var, j * 4 + 4)
                    pool.sem_inc(s_turn, 1)
                    pool.tensor_tensor(span_of(tmp, j), span_of(tmp, j), over_blocks(ln_g[:, :], D, S), ALU.mult).then_inc(s_scaled, 1)

                def beta(j):
                    pool.wait_ge(s_scaled, j + 1)
                    pool.wait_ge(s_chunk_t, j + 1)
                    pool.wait_ge(s_kept, j + 1)
                    pool.sem_inc(s_turn, 1)
                    pool.tensor_tensor(span_x, span_of(tmp, j), over_blocks(ln_b[:, :], D, S), ALU.add).then_inc(s_chunk_x, 1)

                pipelined(pool, (0, gamma), (0, beta))
                pool.memset(acc[:, :, :], 0.0).then_inc(s_pool, 1)
                pool.wait_ge(s_pool, 1)

            @block.scalar
            def _(act):
                act.sem_inc(s_kept, 1)
                act.sem_inc(s_chunk_tc, 1)
                act.sem_inc(s_chunk_b, 2)

                def square(j):
                    act.wait_ge(s_ln_sum, j * 4 + 4)
                    act.activation(span_of(stage, j), span_of(tmp, j), ACT.Square).then_inc(s_ln_sq, 1)

                def root(j):
                    act.wait_ge(s_ln_var, j * 4 + 2)
                    act.activation(stat[:, 2, bass.ds(j * S, S)], stat[:, 1, bass.ds(j * S, S)], ACT.Sqrt).then_inc(s_std, 1)

                def keep(j):
                    act.wait_ge(s_chunk_x, j + 1)
                    act.activation(span_of(x_inner, j), span_x, ACT.Copy).then_inc(s_kept, 1)

                def copy_transpose(j):
                    act.wait_ge(s_chunk_t, j + 2)
                    act.wait_ge(s_chunk_h, j * 2 + 2)
                    act.activation(span_t.rearrange("p j n -> p (j n)"), bank[0], ACT.Copy).then_inc(s_chunk_tc, 1)

                def bias(half):
                    def step(j):
                        if isinstance(j, int) and j == 0:
                            act.wait_ge(s_load, 16)
                        act.wait_ge(s_chunk_h, j * 2 + (3 + half))
                        act.wait_ge(s_chunk_m, j * 2 + (1 + half))
                        act.activation(hidden[:, half, :], bank[2 + half], ACT.Identity, bias=p2("b1")).then_inc(s_chunk_b, 1)
                    return step

                pipelined(act, (1, root), (0, square), (2, keep), (2, copy_transpose), (3, bias(0)), (3, bias(1)))
                act.wait_ge(s_kept, 1 + SPANS)

            @block.tensor
            def _(pe):
                pe.sem_inc(s_chunk_t, 1)
                pe.sem_inc(s_chunk_h, 2)
                pe.sem_inc(s_chunk_m, 2)
                pe.wait_ge(s_load, 16)

                def transpose(j):
                    pe.wait_ge(s_chunk_x, j + 1)
                    pe.wait_ge(s_chunk_tc, j + 1)
                    for n in range(S // 2):
                        ins = pe.transpose(bank[0][:, n * P:(n + 1) * P],
                                           span_x[:, 2 * n:2 * n + 2, :].rearrange("p b d -> p (b d)"), ident[:, :])
                    ins.then_inc(s_chunk_t, 1)

                def first_product(half):
                    def step(j):
                        pe.wait_ge(s_chunk_tc, j + 2)
                        pe.wait_ge(s_chunk_b, j * 2 + (1 + half))
                        for n in range(C):
                            ins = pe.matmul(bank[2 + half][:, n * P:(n + 1) * P], p2("W1")[:, n % 2 * P:(n % 2 + 1) * P],
                                            span_t[:, (half * C + n) // 2, :], start=True, stop=True)
                        ins.then_inc(s_chunk_h, 1)
                    return step

                def second_product(half):
                    def step(j):
                        pe.wait_ge(s_chunk_l, j * 2 + (1 + half))
                        pe.wait_ge(s_chunk_o, j + 1)
                        for n in range(C):
                            at = (half * C + n) * D
                            ins = pe.matmul(bank[6][:, at:at + D], hidden[:, half, n * P:(n + 1) * P],
                                            p2("W2"), start=True, stop=True)
                        ins.then_inc(s_chunk_m, 1)
                    return step

                pipelined(pe, (1, first_product(0)), (0, transpose), (2, second_product(0)), (1, first_product(1)), (2, second_product(1)))

        with nc.Fori(1, l2_layers) as layer:
            run_windows(edge_mlp_pass)
            with nc.Block() as block:
                between_layers(block, layer)
            stage_end()

        run_windows(edge_mlp_pass)

        with nc.Block() as block:
            @block.scalar
            def _(act):
                layer_norm_root(act, 0)

            @block.vector
            def _(dve):
                then = chain(dve)
                then(dve.tensor_tensor(agg_scale[:, :], p2("dot_scale"), p2("res_w"), ALU.mult))
                then(dve.scalar_tensor_tensor(out=x_inner[:, :, :], in0=whole(acc), scalar=agg_scale[:, :],
                                              in1=x_inner[:, :, :], op0=ALU.mult, op1=ALU.add))
                layer_norm(dve, then, 0, x_inner[:, :, :], x_inner[:, :, :], p2("ln_g"), p2("ln_b"))
        stage_end()

        with nc.Block() as block:
            @block.sync
            def _(sp):
                for k, q in enumerate(PIECES):
                    sp.wait_ge(s_ready, k + 1)
                    sp.dma_start(rows_of(table)[:, q, :], x_outer[:, q, :]).then_inc(s_store, 16)
                sp.wait_ge(s_store, 16 * len(PIECES))

            @block.scalar
            def _(act):
                layer_norm_root(act, 0)

            @block.vector
            def _(dve):
                then = chain(dve)
                then(dve.tensor_tensor(x_inner[:, :, :], x_inner[:, :, :], x_outer[:, :, :], ALU.add))
                layer_norm(dve, then, 0, x_inner[:, :, :], x_outer[:, :, :], signal=s_ready)
                then(dve.memset(acc[:, :, :], 0.0))
                then(dve.memset(window[:, :], 0.0))
                then(dve.tensor_scalar(count[:, :], count[:, :], 1.0, None, ALU.max))
                then(dve.reciprocal(count[:, :], count[:, :]))
        stage_end()

        run_windows(sum_pass)

        with nc.Block() as block:
            p3 = lambda name: COLS["l3"](params3, name)
            LAST = L.nodes // P
            w3 = p3("W")

            project(block, whole(acc), w3)

            @block.sync
            def _(sp):
                sp.dma_start(params3, l3_params).then_inc(s_load, 16)

            @block.scalar
            def _(act):
                project_copies(act)
                act.wait_ge(s_var, 1)
                act.activation(tmp[:, :, :], tmp[:, :, :], ACT.Exp).then_inc(s_std, 1)

            @block.vector
            def _(dve):
                then = chain(dve)
                take_products(dve, acc, lambda o, i, b: dve.tensor_tensor(o, i, over_row(count[:, b], D, C), ALU.mult))
                dve.tensor_scalar(tmp[:, :, :], whole(acc), 0.0, None, ALU.min).then_inc(s_var, 1)
                then(dve.tensor_scalar(whole(acc), whole(acc), 0.0, -1.0, ALU.max, ALU.add))
                dve.wait_ge(s_std, 1)
                then(dve.tensor_tensor(whole(acc), whole(acc), tmp[:, :, :], ALU.add))
                then(dve.tensor_tensor(acc[:, LAST:, 0:D], acc[:, LAST:, 0:D], over_row(valid[:, LAST:], D, B - LAST), ALU.mult))
                then(dve.tensor_reduce(out=over_nodes[:, 0, :], in_=whole(acc).rearrange("p b d -> p d b"), op=ALU.add, axis=AX.X))
        stage_end()

        with nc.Block() as block:
            @block.tensor
            def _(pe):
                pe.matmul(bank[0][:, 0:D], ones[:, :], over_nodes[:, 0, :], start=True, stop=True).then_inc(s_pe, 1)
                pe.wait_ge(s_ready, 1)
                pe.matmul(bank[0][:, D:2 * D], ones[:, :], over_nodes[:, 2, :], start=True, stop=True).then_inc(s_pe, 1)

            @block.scalar
            def _(act):
                act.wait_ge(s_var, 1)
                act.activation(over_nodes[:, 3, :], over_nodes[:, 3, :], ACT.Sqrt).then_inc(s_std, 1)
                layer_norm_root(act, 1, 1)

            @block.vector
            def _(dve):
                then = chain(dve)
                mean, squares, scale = (over_nodes[:, n, :] for n in (1, 2, 3))
                dve.wait_ge(s_pe, 1)
                then(dve.tensor_scalar(mean, bank[0][:, 0:D], 1.0 / L.nodes, None, ALU.mult))
                then(dve.tensor_tensor(whole(acc), whole(acc), over_blocks(mean), ALU.subtract))
                then(dve.tensor_tensor(tmp[:, :, :], whole(acc), whole(acc), ALU.mult))
                then(dve.tensor_tensor(tmp[:, LAST:, :], tmp[:, LAST:, :], over_row(valid[:, LAST:], D, B - LAST), ALU.mult))
                then(dve.tensor_reduce(out=squares, in_=tmp[:, :, :].rearrange("p b d -> p d b"), op=ALU.add, axis=AX.X))
                dve.sem_inc(s_ready, 1)
                dve.wait_ge(s_pe, 2)
                dve.tensor_scalar(scale, bank[0][:, D:2 * D], 1.0 / L.nodes, 1e-5, ALU.mult, ALU.add).then_inc(s_var, 1)
                dve.wait_ge(s_std, 1)
                then(dve.reciprocal(scale, scale))
                then(dve.tensor_tensor(scale, scale, p3("gamma"), ALU.mult))
                then(dve.tensor_tensor(whole(acc), whole(acc), over_blocks(scale), ALU.mult))
                then(dve.tensor_tensor(whole(acc), whole(acc), over_blocks(p3("beta")), ALU.add))
                then(dve.tensor_tensor(whole(acc), whole(acc), x_outer[:, :, :], ALU.add))
                layer_norm(dve, then, 1, whole(acc), x_outer[:, :, :], signal=s_turn, before=1)

            @block.sync
            def _(sp):
                stores = 0
                for k, q in enumerate(PIECES):
                    sp.wait_ge(s_turn, k + 1)
                    end = min(q.stop, LAST)
                    if q.start < end:
                        sp.dma_start(rows_of(out[q.start * P:end * P, :]), x_outer[:, q.start:end, :]).then_inc(s_store, 16)
                        stores += 1
                if L.nodes % P:
                    sp.dma_start(out[LAST * P:L.nodes, :], x_outer[0:L.nodes % P, LAST, :]).then_inc(s_store, 16)
                    stores += 1
                sp.wait_ge(s_store, 16 * stores)
    return nc


def kernel(x, src, dst, edge_attr_32, **w):
    import numpy as np
    import concourse.bacc as bacc
    from concourse.bass_utils import run_bass_kernel_spmd

    x, attr = np.asarray(x), np.asarray(edge_attr_32)
    nodes, dim = x.shape
    edges, edge_dim = attr.shape
    w = {k: np.asarray(v) for k, v in w.items()}
    heads = w["L0_gnn_att_src"].shape[0]
    L = Layout(nodes, edges, dim, heads, edge_dim)
    cols = param_columns(dim)

    def padded(a, n):
        return np.concatenate([a, np.broadcast_to(a[-1:], (n - a.shape[0],) + a.shape[1:])])

    def rows(v):
        return np.broadcast_to(np.reshape(v, (1, -1)), (P, np.size(v)))

    def stacked(m):
        return np.tile(m, (P // m.shape[0], 1))

    def diagonal(m, times):
        out = np.zeros((times, m.shape[0], times, m.shape[1]), m.dtype)
        for n in range(times):
            out[n, :, n, :] = m
        return out.reshape(times * m.shape[0], times * m.shape[1])

    def pair_columns(m):
        pair = diagonal(m, 2)
        none = np.zeros_like(pair)
        return np.block([[pair, none], [none, pair]])

    def packed(layer, **named):
        return np.ascontiguousarray(np.concatenate([named[n] for n in cols[layer].at], axis=1))

    src_p = padded(np.asarray(src).astype(np.int32), L.tiles * P)
    dst_p = padded(np.asarray(dst).astype(np.int32), L.tiles * P)

    def by_group(idx):
        return np.ascontiguousarray(idx.reshape(L.groups, G, P).transpose(0, 2, 1))

    attr_p = np.zeros((L.tiles * P, edge_dim), attr.dtype)
    attr_p[:edges] = attr
    attr_p = attr_p.reshape(L.groups, G // 4, 4, P, edge_dim).transpose(0, 2, 4, 1, 3)
    x_p = np.zeros((L.blocks * P, dim), x.dtype)
    x_p[:nodes] = x
    l1_w = list(w["L1_gnn_Ws"]) + [w["L1_gnn_W_out"]]
    l1_b = list(w["L1_gnn_bs"]) + [w["L1_gnn_b_out"]]
    l2 = {k[7:]: v for k, v in w.items() if k.startswith("L2_gnn_")}
    arrays = {
        "src_idx": by_group(src_p),
        "dst_tiles": np.ascontiguousarray(dst_p.reshape(L.tiles, P).T),
        "dst_groups": dst_p.reshape(L.groups, G * P),
        "x": x_p,
        "attr": np.ascontiguousarray(attr_p).reshape(L.groups, P, G // 4 * P),
        "l0_params": packed("l0", W=diagonal(w["L0_gnn_W"], 2), att_src=rows(w["L0_gnn_att_src"]),
                            att_dst=rows(w["L0_gnn_att_dst"]), bias=rows(w["L0_gnn_bias"]),
                            gamma=rows(w["L0_gnn_gamma"]), beta=rows(w["L0_gnn_beta"])),
        "l1_params": np.stack([packed("l1", W=diagonal(a, 2), b=rows(b)) for a, b in zip(l1_w, l1_b)]),
        "l2_params": np.stack([
            packed("l2", W1=diagonal(l2["W1"][n], 2), b1=l2["b1"][n][:, None], W2=l2["W2"][n], b2=rows(l2["b2"][n]),
                   We1=pair_columns(l2["We1"][n]), be1=stacked(l2["be1"][n][:, None]),
                   We2=diagonal(l2["We2"][n], 2), be2=rows(l2["be2"][n]), res_w=rows(l2["res_w"][n]),
                   dot_scale=rows(l2["dot_scale"][n]), ln_g=rows(l2["ln_g"][n]), ln_b=rows(l2["ln_b"][n]))
            for n in range(l2["W1"].shape[0])]),
        "l3_params": packed("l3", W=diagonal(w["L3_gnn_W"], 2), gamma=rows(w["L3_gnn_gamma"]), beta=rows(w["L3_gnn_beta"])),
    }
    nc = bacc.Bacc("TRN2", target_bir_lowering=False, num_devices=1)
    t = {k: nc.dram_tensor(k, a.shape, mybir.dt.from_np(a.dtype), kind="ExternalInput").ap() for k, a in arrays.items()}
    out = nc.dram_tensor("out", (nodes, dim), F32, kind="ExternalOutput").ap()
    build(nc, L, t["src_idx"], t["dst_tiles"], t["dst_groups"], t["x"], t["attr"], t["l0_params"],
          t["l1_params"], t["l2_params"], t["l3_params"], len(w["L1_gnn_Ws"]), len(l2["W1"]), out)
    r = run_bass_kernel_spmd(nc, [arrays], core_ids=[0])
    return r.results[0]["out"]
```
